# Optimizing a Trainium2 kernel written in Bass

```python
import numpy as np
import jax
import jax.numpy as jnp

def _softmax(x, axis=-1):
    return jax.nn.softmax(x, axis=axis)

def _gelu(x):
    return jax.nn.gelu(x, approximate=True)

def _silu(x):
    return jax.nn.silu(x)

def _sigmoid(x):
    return jax.nn.sigmoid(x)

def _layernorm(x, axis=-1, eps=1e-05):
    m = jnp.mean(x, axis=axis, keepdims=True)
    v = jnp.var(x, axis=axis, keepdims=True)
    return (x - m) / jnp.sqrt(v + eps)

def _scatter_add(tgt, idx, src, axis=0):
    return tgt.at[idx].add(src)

def _segment_sum(src, seg, n):
    return jax.ops.segment_sum(src, seg, n)
kernel_name = 'mk_early_fusion_embed_d1_tok_img1024_r4_a88a71'

def setup_inputs(seed: int=0):
    np.random.seed(seed)
    _w = jnp.asarray

    def _rec_inputs():
        import jax
        import jax.numpy as jnp
        _rk = jax.random.key(seed)
        x = 7.22013e-05 + 1.00017 * jax.random.normal(jax.random.fold_in(_rk, 1), (8, 64, 256, 4), jnp.float32)
        x_txt = jax.random.randint(jax.random.fold_in(_rk, 51), (8, 128), 0, 12564, jnp.int32)
        return (x, x_txt)
    x, x_txt = _rec_inputs()

    def _L0_tok_setup():
        import jax, jax.numpy as jnp
        import numpy as np
        B, F, L, H, D = (8, 64, 256, 4, 64)
        MODEL = H * F
        WIN = 128

        def _local_mask():
            m = np.ones((L, L), dtype=bool)
            m = np.tril(m, WIN - 1)
            m = np.triu(m, -(WIN - 1))
            return jnp.asarray(m)

        def _flatten(y):
            n = y.shape[0]
            return y.transpose(0, 2, 3, 1).reshape(n, L, -1)
        key = jax.random.key(seed)
        ks = jax.random.split(key, 12)
        s = lambda n: 1.0 / np.sqrt(n)
        xav = np.sqrt(6.0 / (L + L))
        return {'x': jax.random.normal(ks[0], (B, F, L, H), jnp.float32), 'Wq_w': jax.random.normal(ks[1], (D, F), jnp.float32) * s(F), 'Wq_b': jnp.zeros((D,), jnp.float32), 'Wk_w': jax.random.normal(ks[2], (D, F), jnp.float32) * s(F), 'Wk_b': jnp.zeros((D,), jnp.float32), 'Wv_w': jax.random.normal(ks[3], (D, F), jnp.float32) * s(F), 'Wv_b': jnp.zeros((D,), jnp.float32), 'w_bias': jax.random.uniform(ks[4], (L, L), jnp.float32, -xav, xav), 'out_w': jax.random.normal(ks[5], (H * D, MODEL), jnp.float32) * s(H * D), 'out_b': jnp.zeros((MODEL,), jnp.float32), 'ln_g': jnp.ones((MODEL,), jnp.float32), 'ln_b': jnp.zeros((MODEL,), jnp.float32), 'local_mask': _local_mask()}
    _L0_tok_all = _L0_tok_setup()
    _L0_tok_in = {k: v for k, v in _L0_tok_all.items() if k in ('Wq_w', 'Wq_b', 'Wk_w', 'Wk_b', 'Wv_w', 'Wv_b', 'w_bias', 'out_w', 'out_b', 'ln_g', 'ln_b', 'local_mask')}
    del _L0_tok_all

    def _L0_txt_setup():
        import math
        import jax, jax.numpy as jnp
        import numpy as np
        D_VOCAB = 50257
        D_MODEL = 256
        key = jax.random.key(seed)
        k_tok, k_w = jax.random.split(key)
        tokens = jax.random.randint(k_tok, (8, 512), 0, D_VOCAB)
        W_E = jax.random.normal(k_w, (D_VOCAB, D_MODEL), dtype=jnp.float32)
        return {'tokens': tokens, 'W_E': W_E}
    _L0_txt_all = _L0_txt_setup()
    _L0_txt_in = {k: v for k, v in _L0_txt_all.items() if k in ('W_E',)}
    del _L0_txt_all

    def _L0_attn_setup():
        import jax, jax.numpy as jnp
        import numpy as np
        B, L, E, H, WINDOW = (4, 256, 256, 16, 4)
        D = E // H
        SCALING = D ** (-0.5)

        def _get_relative_embeddings(emb, length):
            pad_length = max(length - (WINDOW + 1), 0)
            if pad_length > 0:
                emb = jnp.pad(emb, ((0, 0), (pad_length, pad_length), (0, 0)))
            start = max(WINDOW + 1 - length, 0)
            return emb[:, start:start + 2 * length - 1]

        def _rel_to_abs(x):
            bh, length, _ = x.shape
            x = jnp.pad(x, ((0, 0), (0, 0), (0, 1)))
            xf = x.reshape(bh, length * 2 * length)
            xf = jnp.pad(xf, ((0, 0), (0, length - 1)))
            xfin = xf.reshape(bh, length + 1, 2 * length - 1)
            return xfin[:, :length, length - 1:]

        def _abs_to_rel(x):
            bh, length, _ = x.shape
            x = jnp.pad(x, ((0, 0), (0, 0), (0, length - 1)))
            xf = x.reshape(bh, length * (2 * length - 1))
            xf = jnp.pad(xf, ((0, 0), (length, 0)))
            xfin = xf.reshape(bh, length, 2 * length)
            return xfin[:, :, 1:]
        key = jax.random.key(seed)
        ks = jax.random.split(key, 12)
        s = E ** (-0.5)
        return {'hidden_states': jax.random.normal(ks[0], (B, L, E), dtype=jnp.float32), 'Wq': jax.random.normal(ks[1], (E, E), dtype=jnp.float32) * s, 'bq': jnp.zeros((E,), dtype=jnp.float32), 'Wk': jax.random.normal(ks[2], (E, E), dtype=jnp.float32) * s, 'bk': jnp.zeros((E,), dtype=jnp.float32), 'Wv': jax.random.normal(ks[3], (E, E), dtype=jnp.float32) * s, 'bv': jnp.zeros((E,), dtype=jnp.float32), 'Wo': jax.random.normal(ks[4], (E, E), dtype=jnp.float32) * s, 'bo': jnp.zeros((E,), dtype=jnp.float32), 'emb_rel_k': jax.random.normal(ks[5], (1, 2 * WINDOW + 1, D), dtype=jnp.float32) * SCALING, 'emb_rel_v': jax.random.normal(ks[6], (1, 2 * WINDOW + 1, D), dtype=jnp.float32) * SCALING}
    _L0_attn_all = _L0_attn_setup()
    _L0_attn_in = {k: v for k, v in _L0_attn_all.items() if k in ('Wq', 'bq', 'Wk', 'bk', 'Wv', 'bv', 'Wo', 'bo', 'emb_rel_k', 'emb_rel_v')}
    del _L0_attn_all

    def _L0_ffn_setup():
        import jax, jax.numpy as jnp
        import numpy as np
        import math
        GOLDEN_CENTER = 1.0 / math.e
        GOLDEN_LOWER = 0.5 - math.log(4.0 / 3.0)
        GOLDEN_UPPER = 0.5
        B, T, D = (4, 512, 256)
        E = 8
        I = 1024 // (E // 2)

        def _routing_weights(x, Wr, temperature):
            inh = jax.nn.sigmoid(x @ Wr / temperature)
            in_zone = (inh >= GOLDEN_LOWER) & (inh <= GOLDEN_UPPER)
            dist = jnp.abs(inh - GOLDEN_CENTER)
            w = jnp.exp(-dist / 0.1) * in_zone.astype(x.dtype)
            wsum = w.sum(axis=-1, keepdims=True)
            no_expert = wsum < 1e-08
            fb = jnp.exp(-dist / 0.3)
            _, top2 = jax.lax.top_k(fb, 2)
            fb_mask = jax.nn.one_hot(top2, E, dtype=x.dtype).sum(axis=-2)
            fb_w = fb * fb_mask
            fb_w = fb_w / jnp.clip(fb_w.sum(axis=-1, keepdims=True), 1e-08)
            w = jnp.where(no_expert, fb_w, w)
            wsum = w.sum(axis=-1, keepdims=True)
            return w / jnp.clip(wsum, 1e-08)
        key = jax.random.key(seed)
        k = jax.random.split(key, 6)
        s_d = 1.0 / math.sqrt(D)
        s_i = 1.0 / math.sqrt(I)
        return {'x': jax.random.normal(k[0], (B, T, D), jnp.float32), 'Wg': jax.random.normal(k[1], (E, D, I), jnp.float32) * s_d, 'Wu': jax.random.normal(k[2], (E, D, I), jnp.float32) * s_d, 'Wd': jax.random.normal(k[3], (E, I, D), jnp.float32) * s_i, 'Wr': jax.random.normal(k[4], (D, E), jnp.float32) * s_d, 'temperature': jnp.ones((1,), jnp.float32)}
    _L0_ffn_all = _L0_ffn_setup()
    _L0_ffn_in = {k: v for k, v in _L0_ffn_all.items() if k in ('Wg', 'Wu', 'Wd', 'Wr', 'temperature')}
    del _L0_ffn_all
    return {'x': x, 'x_txt': x_txt, 'L0_tok_Wq_w': _L0_tok_in['Wq_w'], 'L0_tok_Wq_b': _L0_tok_in['Wq_b'], 'L0_tok_Wk_w': _L0_tok_in['Wk_w'], 'L0_tok_Wk_b': _L0_tok_in['Wk_b'], 'L0_tok_Wv_w': _L0_tok_in['Wv_w'], 'L0_tok_Wv_b': _L0_tok_in['Wv_b'], 'L0_tok_w_bias': _L0_tok_in['w_bias'], 'L0_tok_out_w': _L0_tok_in['out_w'], 'L0_tok_out_b': _L0_tok_in['out_b'], 'L0_tok_ln_g': _L0_tok_in['ln_g'], 'L0_tok_ln_b': _L0_tok_in['ln_b'], 'L0_tok_local_mask': _L0_tok_in['local_mask'], 'L0_txt_W_E': _L0_txt_in['W_E'], 'L0_attn_Wq': _L0_attn_in['Wq'], 'L0_attn_bq': _L0_attn_in['bq'], 'L0_attn_Wk': _L0_attn_in['Wk'], 'L0_attn_bk': _L0_attn_in['bk'], 'L0_attn_Wv': _L0_attn_in['Wv'], 'L0_attn_bv': _L0_attn_in['bv'], 'L0_attn_Wo': _L0_attn_in['Wo'], 'L0_attn_bo': _L0_attn_in['bo'], 'L0_attn_emb_rel_k': _L0_attn_in['emb_rel_k'], 'L0_attn_emb_rel_v': _L0_attn_in['emb_rel_v'], 'L0_ffn_Wg': _L0_ffn_in['Wg'], 'L0_ffn_Wu': _L0_ffn_in['Wu'], 'L0_ffn_Wd': _L0_ffn_in['Wd'], 'L0_ffn_Wr': _L0_ffn_in['Wr'], 'L0_ffn_temperature': _L0_ffn_in['temperature']}

def reference(x, x_txt, L0_tok_Wq_w, L0_tok_Wq_b, L0_tok_Wk_w, L0_tok_Wk_b, L0_tok_Wv_w, L0_tok_Wv_b, L0_tok_w_bias, L0_tok_out_w, L0_tok_out_b, L0_tok_ln_g, L0_tok_ln_b, L0_tok_local_mask, L0_txt_W_E, L0_attn_Wq, L0_attn_bq, L0_attn_Wk, L0_attn_bk, L0_attn_Wv, L0_attn_bv, L0_attn_Wo, L0_attn_bo, L0_attn_emb_rel_k, L0_attn_emb_rel_v, L0_ffn_Wg, L0_ffn_Wu, L0_ffn_Wd, L0_ffn_Wr, L0_ffn_temperature):
    import jax
    import jax.numpy as jnp

    def _L0_tok_ref(x, Wq_w, Wq_b, Wk_w, Wk_b, Wv_w, Wv_b, w_bias, out_w, out_b, ln_g, ln_b, local_mask):
        import jax, jax.numpy as jnp
        import numpy as np
        B, F, L, H, D = (8, 64, 256, 4, 64)
        MODEL = H * F
        WIN = 128

        def _local_mask():
            m = np.ones((L, L), dtype=bool)
            m = np.tril(m, WIN - 1)
            m = np.triu(m, -(WIN - 1))
            return jnp.asarray(m)

        def _flatten(y):
            n = y.shape[0]
            return y.transpose(0, 2, 3, 1).reshape(n, L, -1)

        def proj(w, b):
            y = jnp.einsum('nclh,dc->ndlh', x, w) + b[None, :, None, None]
            return _flatten(y)
        q = proj(Wq_w, Wq_b)
        k = proj(Wk_w, Wk_b)
        v = proj(Wv_w, Wv_b)
        wb = w_bias * local_mask.astype(w_bias.dtype)
        ew = jnp.exp(wb)
        ek = jnp.exp(k)
        num = jnp.einsum('ts,nsd->ntd', ew, ek * v)
        den = jnp.einsum('ts,nsd->ntd', ew, ek)
        y = jax.nn.sigmoid(q) * num / den
        h = y @ out_w + out_b + _flatten(x)
        mu = jnp.mean(h, axis=-1, keepdims=True)
        var = jnp.mean(jnp.square(h - mu), axis=-1, keepdims=True)
        return (h - mu) * jax.lax.rsqrt(var + 1e-05) * ln_g + ln_b

    def _L0_txt_ref(tokens, W_E):
        import math
        import jax, jax.numpy as jnp
        import numpy as np
        D_VOCAB = 50257
        D_MODEL = 256
        scale = jnp.asarray(math.sqrt(W_E.shape[1]), dtype=W_E.dtype)
        return jnp.take(W_E, tokens, axis=0) * scale

    def _L0_attn_ref(hidden_states, Wq, bq, Wk, bk, Wv, bv, Wo, bo, emb_rel_k, emb_rel_v):
        import jax, jax.numpy as jnp
        import numpy as np
        B, L, E, H, WINDOW = (4, 256, 256, 16, 4)
        D = E // H
        SCALING = D ** (-0.5)

        def _get_relative_embeddings(emb, length):
            pad_length = max(length - (WINDOW + 1), 0)
            if pad_length > 0:
                emb = jnp.pad(emb, ((0, 0), (pad_length, pad_length), (0, 0)))
            start = max(WINDOW + 1 - length, 0)
            return emb[:, start:start + 2 * length - 1]

        def _rel_to_abs(x):
            bh, length, _ = x.shape
            x = jnp.pad(x, ((0, 0), (0, 0), (0, 1)))
            xf = x.reshape(bh, length * 2 * length)
            xf = jnp.pad(xf, ((0, 0), (0, length - 1)))
            xfin = xf.reshape(bh, length + 1, 2 * length - 1)
            return xfin[:, :length, length - 1:]

        def _abs_to_rel(x):
            bh, length, _ = x.shape
            x = jnp.pad(x, ((0, 0), (0, 0), (0, length - 1)))
            xf = x.reshape(bh, length * (2 * length - 1))
            xf = jnp.pad(xf, ((0, 0), (length, 0)))
            xfin = xf.reshape(bh, length, 2 * length)
            return xfin[:, :, 1:]
        bsz, tgt_len, _ = hidden_states.shape

        def shape(t):
            return t.reshape(bsz, tgt_len, H, D).transpose(0, 2, 1, 3).reshape(bsz * H, tgt_len, D)
        q = shape((hidden_states @ Wq + bq) * SCALING)
        k = shape(hidden_states @ Wk + bk)
        v = shape(hidden_states @ Wv + bv)
        src_len = k.shape[1]
        attn_weights = jnp.einsum('btd,bsd->bts', q, k)
        rel_k = _get_relative_embeddings(emb_rel_k, src_len)
        rel_logits = jnp.einsum('btd,md->btm', q, rel_k[0])
        attn_weights = attn_weights + _rel_to_abs(rel_logits)
        attn_probs = jax.nn.softmax(attn_weights, axis=-1)
        attn_output = jnp.einsum('bts,bsd->btd', attn_probs, v)
        rel_v = _get_relative_embeddings(emb_rel_v, src_len)
        rel_weights = _abs_to_rel(attn_probs)
        attn_output = attn_output + jnp.einsum('btm,md->btd', rel_weights, rel_v[0])
        out = attn_output.reshape(bsz, H, tgt_len, D).transpose(0, 2, 1, 3).reshape(bsz, tgt_len, E)
        return out @ Wo + bo

    def _L0_ffn_ref(x, Wg, Wu, Wd, Wr, temperature):
        import jax, jax.numpy as jnp
        import numpy as np
        import math
        GOLDEN_CENTER = 1.0 / math.e
        GOLDEN_LOWER = 0.5 - math.log(4.0 / 3.0)
        GOLDEN_UPPER = 0.5
        B, T, D = (4, 512, 256)
        E = 8
        I = 1024 // (E // 2)

        def _routing_weights(x, Wr, temperature):
            inh = jax.nn.sigmoid(x @ Wr / temperature)
            in_zone = (inh >= GOLDEN_LOWER) & (inh <= GOLDEN_UPPER)
            dist = jnp.abs(inh - GOLDEN_CENTER)
            w = jnp.exp(-dist / 0.1) * in_zone.astype(x.dtype)
            wsum = w.sum(axis=-1, keepdims=True)
            no_expert = wsum < 1e-08
            fb = jnp.exp(-dist / 0.3)
            _, top2 = jax.lax.top_k(fb, 2)
            fb_mask = jax.nn.one_hot(top2, E, dtype=x.dtype).sum(axis=-2)
            fb_w = fb * fb_mask
            fb_w = fb_w / jnp.clip(fb_w.sum(axis=-1, keepdims=True), 1e-08)
            w = jnp.where(no_expert, fb_w, w)
            wsum = w.sum(axis=-1, keepdims=True)
            return w / jnp.clip(wsum, 1e-08)
        weights = _routing_weights(x, Wr, temperature)
        gate = jnp.einsum('btd,edi->beti', x, Wg)
        up = jnp.einsum('btd,edi->beti', x, Wu)
        h = jax.nn.silu(gate) * up
        e_out = jnp.einsum('beti,eid->betd', h, Wd)
        out = jnp.einsum('bte,betd->btd', weights, e_out)
        return out
    h = _L0_tok_ref(x, L0_tok_Wq_w, L0_tok_Wq_b, L0_tok_Wk_w, L0_tok_Wk_b, L0_tok_Wv_w, L0_tok_Wv_b, L0_tok_w_bias, L0_tok_out_w, L0_tok_out_b, L0_tok_ln_g, L0_tok_ln_b, L0_tok_local_mask)
    h = jnp.concatenate([h, _L0_txt_ref(x_txt, L0_txt_W_E)], axis=1)
    h = h + _L0_attn_ref(_layernorm(h, axis=-1), L0_attn_Wq, L0_attn_bq, L0_attn_Wk, L0_attn_bk, L0_attn_Wv, L0_attn_bv, L0_attn_Wo, L0_attn_bo, L0_attn_emb_rel_k, L0_attn_emb_rel_v)
    h = h + _L0_ffn_ref(_layernorm(h, axis=-1), L0_ffn_Wg, L0_ffn_Wu, L0_ffn_Wd, L0_ffn_Wr, L0_ffn_temperature)
    return h

_drawn_inputs = setup_inputs


def setup_inputs(seed=0):
    import zlib

    import numpy as np

    out = dict(_drawn_inputs(seed))
    spreads = {'L0_tok_Wq_b': (0.0, 0.8),
     'L0_tok_Wk_b': (0.0, 0.8),
     'L0_tok_Wv_b': (0.0, 0.641),
     'L0_tok_out_b': (0.0, 0.427),
     'L0_tok_ln_g': (1.0, 0.6),
     'L0_tok_ln_b': (0.0, 0.473),
     'L0_attn_bq': (0.0, 0.8),
     'L0_attn_bk': (0.0, 0.8),
     'L0_attn_bv': (0.0, 0.565),
     'L0_attn_bo': (0.0, 0.54)}
    factors = {'L0_tok_Wq_w': 7.622,
     'L0_tok_Wk_w': 3.967,
     'L0_tok_Wv_w': 3.339,
     'L0_tok_w_bias': 8.0,
     'L0_tok_out_w': 2.969,
     'L0_attn_Wq': 4.184,
     'L0_attn_Wk': 4.053,
     'L0_attn_emb_rel_k': 8.0,
     'L0_attn_emb_rel_v': 8.0}
    for name, (base, spread) in spreads.items():
        noise = np.random.default_rng([zlib.crc32(name.encode()), seed]).standard_normal(out[name].shape)
        drawn = base * np.exp(spread * noise) if base else spread * noise
        out[name] = jnp.asarray(drawn.astype(out[name].dtype))
    for name, factor in factors.items():
        out[name] = (out[name] * factor).astype(out[name].dtype)
    return out
```

```python
from contextlib import ExitStack

import numpy as np

import concourse.bass as bass
from concourse import mybir

F32 = mybir.dt.float32
F32R = mybir.dt.float32r
BF16 = mybir.dt.bfloat16
I32 = mybir.dt.int32
U8 = mybir.dt.uint8
ALU = mybir.AluOpType
ACT = mybir.ActivationFunctionType
AX = mybir.AxisListType.X

P = 128
NB = 8
F, L, H = 64, 256, 4
E = H * F
KT = E // P
TXT = 128
T = L + TXT
TT = T // P
IT = L // P
AH, AD = 16, 16
WIN = 4
NJ = 2 * WIN + 1
NE = 8
FI = 256
FT = FI // P
SLOTS = 6
KST = SLOTS * AD
Q_PART = [0, 0, 1, 0, 2, 1]
K_PART = [0, 1, 0, 2, 0, 1]
BL = 32
WD_ = BL + 2 * WIN
ROW = WD_ * AH
RJ = NJ * AH
BPITCH = BL * ROW + BL * AH
LEAD = 4096
BAND = LEAD + (T // BL) * BPITCH + 8192
PAD = WIN
GRP = 4
PTS = 7
VC = AD + 1
EPS = 1e-5
WINS = P // BL + 2
N_LOADS = 27 + P // AD + NJ
N_ZERO = 7
SET_DVE_WB, SET_DVE_STAGED, SET_DVE_ALL = 11, 19, 24
SET_ACT_EW, SET_ACT_STAGED, SET_ACT_ALL = 2, 3, 6
R_DIST = 4
ZONE_LO = float(np.float32(0.5 - np.log(4.0 / 3.0)))
ZONE_HI = 0.5
CENTER = float(np.float32(1.0 / np.e))


class Signal:

    def __init__(self, sem, n, unit=1):
        self.sem, self.n, self.unit = sem, n, unit

    def at(self, b, k):
        return b * (self.n * self.unit) + k * self.unit


def fusion_block(nc, a, out):
    ctx = ExitStack()

    def sb(name, shape, dt=F32):
        return ctx.enter_context(nc.sbuf_tensor(name, shape, dt))

    def ps(name, shape, dt=F32):
        return ctx.enter_context(nc.psum_tensor(name, shape, dt))

    def sem(name):
        return ctx.enter_context(nc.semaphore(name))

    def sig(name, n, unit=1):
        return Signal(sem(name), n, unit)

    with ctx:
        ident = sb("ident", [P, P])
        head_of_row = sb("head_of_row", [P, KT, AH])
        head_of_rel = sb("head_of_rel", [P, AH])
        earlier = sb("earlier", [P, NE, NE])
        wkv = sb("wkv", [F + 1, 2 * F])
        wq_t = sb("wq_t", [F + 1, F])
        resid = sb("resid", [F + 1, H, F])
        ew_t = sb("ew_t", [P, IT, L])
        out_w = sb("out_w", [P, KT, E])
        ln_g = sb("ln_g", [P, E])
        ln_b = sb("ln_b", [P, E])
        bv_all = sb("bv_all", [P, E])
        bo_all = sb("bo_all", [P, E])
        bq4 = sb("bq4", [P, KT])
        bk1 = sb("bk1", [P, KT])
        w_q = sb("w_q", [P, KT, E])
        w_k = sb("w_k", [P, KT, E])
        w_v = sb("w_v", [P, KT, E])
        w_o = sb("w_o", [P, KT, E])
        rel_k = sb("rel_k", [P, KT, NJ, AH])
        rel_v0 = sb("rel_v0", [P, AH, AD])
        rel_v1 = sb("rel_v1", [RJ - P, AH, AD])
        wg_hi = sb("wg_hi", [P, NE, KT, FI], F32R)
        wg_lo = sb("wg_lo", [P, NE, KT, FI], F32R)
        wu_hi = sb("wu_hi", [P, NE, KT, FI], F32R)
        wu_lo = sb("wu_lo", [P, NE, KT, FI], F32R)
        w_d = sb("w_d", [P, NE, FT, E])
        w_r = sb("w_r", [P, KT, NE])
        wr_hi = sb("wr_hi", [P, KT, NE], F32R)
        wr_lo = sb("wr_lo", [P, KT, NE], F32R)
        neg_temp = sb("neg_temp", [P, 1])

        x_in = sb("x_in", [F + 1, L, H])
        txt_idx = sb("txt_idx", [P, 1], I32)
        txt_row = sb("txt_row", [P, E])
        hid = sb("hid", [P, TT, E])
        q_st = sb("q_st", [KST + 2, AH, T], BF16)
        k_st = sb("k_st", [KST + 2, AH, T], BF16)
        v_one = sb("v_one", [P, TT, AH, VC])
        band_t = sb("band_t", [P, TT, WD_, AH])
        band_s = sb("band_s", [P, TT, WD_, AH])
        maxima = sb("maxima", [P, TT, AH])
        neg_max = sb("neg_max", [AH, 2, T], BF16)
        o_sb = sb("o_sb", [P, AH // GRP, T])
        res = sb("res", [P, TT, E])
        x2_hi = sb("x2_hi", [P, KT, T], F32R)
        x2_lo = sb("x2_lo", [P, KT, T], F32R)
        wgt = sb("wgt", [P, TT, NE])
        silu = sb("silu", [P, T])
        hT = sb("hT", [P, 3, T])
        stat = sb("stat", [P, TT, 6])
        mv = sb("mv", [P, TT, 2])
        rstd = sb("rstd", [P, TT])
        eps = sb("eps", [P, 1])
        root_e = sb("root_e", [P, 1])
        one = sb("one", [P, 1])
        spare = sb("spare", [P, 2])

        Z = sb("scratch", [P, max(PTS * TT * T, 2 * NE * KT * FI)])

        def zone(start, *dims, rows=P):
            n = int(np.prod(dims))
            v = Z[0:rows, start:start + n]
            names = "abcd"[:len(dims)]
            if len(dims) > 1:
                v = v.rearrange(f"p ({' '.join(names)}) -> p {' '.join(names)}",
                                **{c: d for c, d in zip(names[1:], dims[1:])})
            return v

        p_t = zone(0, PTS, TT, T)
        ek, ekv = zone(0, IT, E), zone(512, IT, E)
        eq, dd, y_t = zone(1024, KT, L), zone(1536, KT, L), zone(2048, KT, L)
        xn = zone(2560, TT, E)
        xn_t = zone(3328, KT, T)
        qf, kf = zone(4096, KT, T), zone(4864, KT, T)
        qr, kr = zone(0, KT, T), zone(768, KT, T)
        rel_log = zone(5632, TT, RJ)
        parts = [Z[:, at:at + KT * T // 2].bitcast(BF16).rearrange("p (m t) -> p m t", m=KT)
                 for at in (1536, 1920, 6064, 6448, 6832, 7216)]
        rel_w = zone(0, TT, RJ)
        rwt0, rwt1 = zone(512, T), zone(896, T, rows=RJ - P)
        attn, attn_t = zone(1280, TT, E), zone(2048, KT, T)
        xn2 = zone(2816, TT, E)
        rden = zone(3584, TT, AH)
        rt = [zone(3700 + 32 * i, TT, NE) for i in range(14)]
        rsum = zone(4200, TT)
        rpair = zone(4300, TT, NE, NE)
        rpair2 = zone(4500, TT, NE, NE)

        S = ps("S", [P, 3, 512])
        O = ps("O", [P, 512])
        G = ps("G", [P, 512])
        U = ps("U", [P, 512])
        D = ps("D", [P, 2, 512])

        d_parts = nc.dram_tensor("d_parts", [6, E, T], BF16, kind="Internal").ap()
        d_neg = nc.dram_tensor("d_neg", [2, AH, T], BF16, kind="Internal").ap()
        d_band_t = nc.dram_tensor("d_band_t", [T * ROW], F32, kind="Internal").ap()
        d_band_s = nc.dram_tensor("d_band_s", [BAND], F32, kind="Internal").ap()
        d_band_w = nc.dram_tensor("d_band_w", [BAND], F32, kind="Internal").ap()

        def dram(t, offset, *dims):
            return bass.AP(tensor=t.tensor, offset=offset, ap=[list(d) for d in dims])

        loaded = sem("loaded")
        gu_loaded = sem("gu_loaded")
        zeroed = sem("zeroed")
        set_dve, set_act, set_pe = sem("set_dve"), sem("set_act"), sem("set_pe")
        x_loaded = sig("x_loaded", 1, 16)
        idx_loaded = sig("idx_loaded", 1, 16)
        txt_loaded = sig("txt_loaded", 1, 16)
        mix_pe = sig("mix_pe", 7)
        mix_act = sig("mix_act", 3)
        mix_dve = sig("mix_dve", 12)
        hid_ready = sig("hid_ready", 5)
        mix_root, ln2_root, ln3_root = sig("mix_root", 1), sig("ln2_root", 1), sig("ln3_root", 1)
        ln2 = sig("ln2", 3 * TT + 1)
        xt_pe, xt_act = sig("xt_pe", 2), sig("xt_act", 2)
        proj_pe = sig("proj_pe", 10)
        proj_act = sig("proj_act", 7)
        v_done = sig("v_done", TT)
        split = sig("split", 8)
        parts_out = sig("parts_out", 6, 16)
        stacked = sig("stacked", 12, 16)
        rel_out = sig("rel_out", 7, 16)
        band_in = sig("band_in", 5, 16)
        max_pe = sig("max_pe", AH)
        max_add = sig("max_add", 4 * AH)
        max_done = sig("max_done", AH)
        neg_pe, neg_act, neg_dve = sig("neg_pe", 1), sig("neg_act", 1), sig("neg_dve", 1)
        neg_out, neg_in = sig("neg_out", 1, 16), sig("neg_in", 1, 16)
        sc_pe = sig("sc_pe", AH)
        sc_add = sig("sc_add", 4 * AH)
        exp_done = sig("exp_done", AH)
        win_done = sig("win_done", WINS * AH)
        pv_done = sig("pv_done", AH // GRP)
        o_copied = sig("o_copied", AH // GRP)
        win_out = sig("win_out", 4, 16)
        relw_in = sig("relw_in", 3, 16)
        rw_pe, rw_act = sig("rw_pe", 2), sig("rw_act", 2)
        ot_pe = sig("ot_pe", TT)
        or_pe = sig("or_pe", TT)
        att_dve = sig("att_dve", 3 * TT)
        att_mid = sig("att_mid", TT)
        at_pe, at_act = sig("at_pe", 2), sig("at_act", 2)
        wo_pe = sig("wo_pe", TT)
        hid_bo = sig("hid_bo", 1)
        res_ready = sig("res_ready", TT)
        ln3 = sig("ln3", 3 * TT + 1)
        x2_pe, x2_hi_done, x2_lo_done = sig("x2_pe", 2), sig("x2_hi_done", 2), sig("x2_lo_done", 2)
        r_pe = sig("r_pe", 1)
        r_act = sig("r_act", 3)
        R_STEPS = 24
        r_dve = sig("r_dve", R_STEPS)
        gate_pe, up_pe = sig("gate_pe", NE * FT), sig("up_pe", NE * FT)
        silu_done = sig("silu_done", NE * FT)
        h_done = sig("h_done", NE * FT)
        down_pe = sig("down_pe", NE)
        acc_done = sig("acc_done", NE * TT)
        stored = sig("stored", 1, 16)

        units = [("u", 0), ("u", 1)]
        for e in range(NE):
            if e + 1 < NE:
                units += [("u", 2 * e + 2), ("d", e), ("u", 2 * e + 3)]
            else:
                units += [("d", e)]

        def schedule(attention, ffn):
            left = list(units) if ffn else []
            steps = []

            def fill(n):
                for _ in range(min(n, len(left))):
                    steps.append(("ffn",) + left.pop(0))

            if attention:
                steps.append(("mix",))
                fill(2)
                steps.append(("project",))
                fill(4)
                for h in range(AH):
                    steps.append(("maxima", h))
                    if h % 2 == 0:
                        fill(1)
                steps.append(("negate",))
                fill(1)
                for h in range(AH):
                    steps.append(("attend", h))
                    fill(1 if h % 2 == 0 or h > 12 else 0)
                    if h % GRP == GRP - 1:
                        steps.append(("values", h // GRP))
                fill(len(left))
                if ffn:
                    steps.append(("store",))
                steps.append(("output",))
            else:
                fill(len(left))
                steps.append(("store",))
            return steps

        def rounds(engine, do):
            for s in schedule(True, False):
                do(s, 0, None)
            with engine.Fori(1, NB) as b:
                for s in schedule(True, True):
                    do(s, b, b - 1)
            for s in schedule(False, True):
                do(s, None, NB - 1)

        block = ctx.enter_context(nc.Block())

        @block.sync
        def _(sp):
            loads = [
                (ident[:], a["ident"]), (head_of_row[:], a["head_of_row"]),
                (head_of_rel[:], a["head_of_rel"]), (earlier[:], a["earlier"]),
                (Z[:, 0:512].rearrange("p (i s) -> p i s", i=IT),
                 a["L0_tok_w_bias"].rearrange("(i p) s -> p i s", p=P)),
                (Z[:, 512:640].bitcast(U8).rearrange("p (i s) -> p i s", i=IT),
                 a["mask"].rearrange("(i p) s -> p i s", p=P)),
                (wkv[0:F, 0:F], a["tok_wk_t"]), (wkv[0:F, F:2 * F], a["tok_wv_t"]),
                (wkv[F:F + 1, 0:F], a["L0_tok_Wk_b"].unsqueeze(0)),
                (wkv[F:F + 1, F:2 * F], a["L0_tok_Wv_b"].unsqueeze(0)),
                (wq_t[0:F, :], a["tok_wq_t"]), (wq_t[F:F + 1, :], a["L0_tok_Wq_b"].unsqueeze(0)),
                (resid[F:F + 1, :, :], a["L0_tok_out_b"].rearrange("(o h c) -> o h c", o=1, h=H)),
                (out_w[:], a["L0_tok_out_w"].rearrange("(k p) n -> p k n", p=P)),
                (ln_g[:], a["L0_tok_ln_g"].partition_broadcast(P)),
                (ln_b[:], a["L0_tok_ln_b"].partition_broadcast(P)),
                (bv_all[:], a["L0_attn_bv"].partition_broadcast(P)),
                (bo_all[:], a["L0_attn_bo"].partition_broadcast(P)),
                (bq4[:], a["L0_attn_bq"].rearrange("(k p) -> p k", p=P)),
                (bk1[:], a["L0_attn_bk"].rearrange("(k p) -> p k", p=P)),
                (w_q[:], a["L0_attn_Wq"].rearrange("(k p) n -> p k n", p=P)),
                (w_k[:], a["L0_attn_Wk"].rearrange("(k p) n -> p k n", p=P)),
                (w_v[:], a["L0_attn_Wv"].rearrange("(k p) n -> p k n", p=P)),
                (w_o[:], a["L0_attn_Wo"].rearrange("(k p) n -> p k n", p=P)),
                (w_r[:], a["L0_ffn_Wr"].rearrange("(k p) n -> p k n", p=P)),
                (neg_temp[:], a["L0_ffn_temperature"].partition_broadcast(P)),
                (w_d[:], a["L0_ffn_Wd"].rearrange("e (k p) n -> p e k n", p=P)),
            ]
            emb_k = a["L0_attn_emb_rel_k"]
            emb_v = a["L0_attn_emb_rel_v"]
            for r in range(P // AD):
                loads.append((Z[AD * r:AD * (r + 1), 640:640 + NJ],
                              emb_k.rearrange("o j d -> d (o j)")))
            for j in range(NJ):
                rows = slice(AH * j, AH * (j + 1)) if j < 8 else slice(0, AH)
                at = 656 if j < 8 else 672
                loads.append((Z[rows, at:at + AD], dram(emb_v, j * AD, (0, AH), (1, AD))))
            for dst, src in loads:
                with nc.allow_non_contiguous_dma(reason="small bias and embedding columns, once"):
                    sp.dma_start(dst, src).then_inc(loaded, 16)
            assert len(loads) == N_LOADS
            sp.wait_ge(set_dve, 1)
            zero = band_t[:].rearrange("p i w h -> p (i w h)")
            sp.dma_start(dram(d_band_t, 0, (TT * ROW, P), (1, TT * ROW)), zero).then_inc(zeroed, 16)
            for d in (d_band_s, d_band_w):
                n = TT * ROW
                for i in range(-(-BAND // (P * n))):
                    rows = min(P, (BAND - i * P * n) // n)
                    if rows:
                        sp.dma_start(dram(d, i * P * n, (n, rows), (1, n)), zero[0:rows]).then_inc(zeroed, 16)
                    rest = BAND - (i * P + rows) * n
                    if rows < P and rest:
                        sp.dma_start(dram(d, (i * P + rows) * n, (rest, 1), (1, rest)),
                                     zero[0:1, 0:rest]).then_inc(zeroed, 16)
            sp.wait_ge(set_dve, SET_DVE_STAGED)
            sp.wait_ge(set_act, SET_ACT_STAGED)
            sp.dma_start(zone(0, NE, KT, FI), a["L0_ffn_Wg"].rearrange("e (k p) n -> p e k n", p=P)
                         ).then_inc(gu_loaded, 16)
            sp.dma_start(zone(4096, NE, KT, FI), a["L0_ffn_Wu"].rearrange("e (k p) n -> p e k n", p=P)
                         ).then_inc(gu_loaded, 16)
            sp.wait_ge(zeroed, N_ZERO * 16)

            def do(step, b, f):
                kind = step[0]
                if kind == "mix":
                    if not isinstance(b, int):
                        sp.wait_ge(mix_pe.sem, mix_pe.at(b - 1, 7))
                        sp.wait_ge(txt_loaded.sem, txt_loaded.at(b - 1, 1))
                    sp.dma_start(x_in[0:F, :, :], a["x"][b]).then_inc(x_loaded.sem, 16)
                    sp.dma_start(txt_idx[:], a["txt_t"][b]).then_inc(idx_loaded.sem, 16)
                elif kind == "project":
                    sp.wait_ge(proj_act.sem, proj_act.at(b, 7))
                    for c in range(P // BL):
                        sp.dma_start(
                            dram(d_band_t, c * BL * ROW, (ROW + AH, BL), (P * ROW, TT), (1, RJ)),
                            rel_log[c * BL:(c + 1) * BL]).then_inc(rel_out.sem, 16)
                    for i in range(TT):
                        sp.dma_start(
                            dram(d_band_s, LEAD + (i * P) * (ROW + AH) - WIN * ROW + WIN * AH,
                                 (ROW + AH, P), (ROW, NJ), (1, AH)),
                            rel_log[:, i].rearrange("p (j h) -> p j h", j=NJ)).then_inc(rel_out.sem, 16)
                    for n in range(6):
                        sp.wait_ge(split.sem, split.at(b, 4 * (n // 3) + (1, 3, 4)[n % 3]))
                        sp.dma_start(d_parts[n].rearrange("(m p) t -> p m t", p=P),
                                     parts[n]).then_inc(parts_out.sem, 16)
                    sp.wait_ge(parts_out.sem, parts_out.at(b, 6))
                    if not isinstance(b, int):
                        sp.wait_ge(sc_pe.sem, sc_pe.at(b - 1, AH))
                    for n, (st, base, order) in enumerate([(q_st, 0, Q_PART), (k_st, 3, K_PART)]):
                        for s in range(SLOTS):
                            sp.dma_start(
                                st[AD * s:AD * (s + 1)],
                                d_parts[base + order[s]].rearrange("(h d) t -> d h t", d=AD)
                            ).then_inc(stacked.sem, 16)
                    sp.wait_ge(rel_out.sem, rel_out.at(b, 7))
                    if not isinstance(b, int):
                        sp.wait_ge(win_out.sem, win_out.at(b - 1, 4))
                        sp.wait_ge(sc_add.sem, sc_add.at(b - 1, 4 * AH))
                    sp.dma_start(band_t[:].rearrange("p i w h -> p i (w h)"),
                                 dram(d_band_t, 0, (ROW, P), (P * ROW, TT), (1, ROW))
                                 ).then_inc(band_in.sem, 16)
                    for c in range(P // BL):
                        sp.dma_start(
                            band_s[c * BL:(c + 1) * BL].rearrange("p i w h -> p i (w h)"),
                            dram(d_band_s, LEAD + c * BPITCH, (ROW, BL), (P // BL * BPITCH, TT), (1, ROW))
                        ).then_inc(band_in.sem, 16)
                elif kind == "negate":
                    sp.wait_ge(neg_act.sem, neg_act.at(b, 1))
                    sp.wait_ge(neg_dve.sem, neg_dve.at(b, 1))
                    sp.dma_start(d_neg.rearrange("i h t -> h i t"), neg_max[:]).then_inc(neg_out.sem, 16)
                    sp.wait_ge(neg_out.sem, neg_out.at(b, 1))
                    sp.dma_start(q_st[KST:KST + 2], d_neg).then_inc(neg_in.sem, 16)
                elif kind == "output":
                    sp.wait_ge(win_done.sem, win_done.at(b, WINS * AH))
                    for c in range(P // BL):
                        sp.dma_start(
                            dram(d_band_w, LEAD + c * BPITCH, (ROW, BL), (P // BL * BPITCH, TT), (1, ROW)),
                            band_t[c * BL:(c + 1) * BL].rearrange("p i w h -> p i (w h)")
                        ).then_inc(win_out.sem, 16)
                    sp.wait_ge(win_out.sem, win_out.at(b, 4))
                    sp.wait_ge(pv_done.sem, pv_done.at(b, AH // GRP))
                    for i in range(TT):
                        sp.dma_start(
                            rel_w[:, i].rearrange("p (j h) -> p j h", j=NJ),
                            dram(d_band_w, LEAD + (i * P) * (ROW + AH) - WIN * ROW + WIN * AH,
                                 (ROW + AH, P), (ROW, NJ), (1, AH))).then_inc(relw_in.sem, 16)
                elif kind == "store":
                    sp.wait_ge(acc_done.sem, acc_done.at(f, NE * TT))
                    sp.dma_start(out[f].rearrange("(i p) e -> p i e", p=P), res[:]).then_inc(stored.sem, 16)

            rounds(sp, do)
            sp.wait_ge(stored.sem, stored.at(NB - 1, 1))

        @block.tensor
        def _(pe):
            def turn(dst, src, rows=P):
                return pe.transpose(dst, src, ident[0:rows, 0:rows])

            pe.wait_ge(set_act, SET_ACT_EW)
            for si in range(IT):
                for ti in range(IT):
                    last = turn(S[:, si, ti * P:(ti + 1) * P], Z[:, 1024 + ti * L + si * P:1024 + ti * L + (si + 1) * P])
                last.then_inc(set_pe, 1)
            pe.wait_ge(set_dve, SET_DVE_ALL)
            pe.wait_ge(set_act, SET_ACT_ALL)

            def mix(b):
                if not isinstance(b, int):
                    pe.wait_ge(r_act.sem, r_act.at(b - 1, 1))
                pe.wait_ge(x_loaded.sem, x_loaded.at(b, 1))
                for i in range(IT):
                    for h in range(H):
                        mm = pe.matmul(S[:, i, h * P:(h + 1) * P], x_in[:, i * P:(i + 1) * P, h],
                                       wkv[:], start=True, stop=True)
                    mm.then_inc(mix_pe.sem, 1)
                for h in range(H):
                    mm = pe.matmul(S[F * (h % 2):F * (h % 2) + F, 2, (h // 2) * L:(h // 2 + 1) * L],
                                   wq_t[:], x_in[:, :, h], start=True, stop=True)
                mm.then_inc(mix_pe.sem, 1)
                pe.wait_ge(mix_act.sem, mix_act.at(b, 2))
                for m in range(KT):
                    for i in range(IT):
                        mm = pe.matmul(O[:, m * L:(m + 1) * L], ek[:, i, m * P:(m + 1) * P],
                                       ew_t[:, i, :], start=(i == 0), stop=(i == IT - 1))
                mm.then_inc(mix_pe.sem, 1)
                pe.wait_ge(mix_dve.sem, mix_dve.at(b, 2))
                for m in range(KT):
                    for i in range(IT):
                        mm = pe.matmul(S[:, 0, m * L:(m + 1) * L], ekv[:, i, m * P:(m + 1) * P],
                                       ew_t[:, i, :], start=(i == 0), stop=(i == IT - 1))
                mm.then_inc(mix_pe.sem, 1)
                pe.wait_ge(mix_dve.sem, mix_dve.at(b, 5))
                for i in range(IT):
                    for k in range(KT):
                        pe.matmul(S[:, 1, i * E:(i + 1) * E], y_t[:, k, i * P:(i + 1) * P], out_w[:, k, :],
                                  start=(k == 0), stop=False, skip_group_check=True)
                    for h in range(H):
                        mm = pe.matmul(S[:, 1, i * E + h * F:i * E + (h + 1) * F],
                                       x_in[:, i * P:(i + 1) * P, h], resid[:, h, :],
                                       start=False, stop=(h == H - 1), skip_group_check=True)
                    mm.then_inc(mix_pe.sem, 1)

            def turned(src, ready, steps, done, b):
                pe.wait_ge(ready.sem, ready.at(b, steps))
                for k in range(KT):
                    for i in range(TT):
                        last = turn(S[:, k, i * P:(i + 1) * P], src[:, i, k * P:(k + 1) * P])
                    last.then_inc(done.sem, 1)

            banks = [S[:, 2], S[:, 0], S[:, 1], O[:]]

            def project(b):
                turned(xn, ln2, 3 * TT + 1, xt_pe, b)
                pe.wait_ge(xt_act.sem, xt_act.at(b, 2))
                for n, (w, m) in enumerate([(w_q, 0), (w_q, 1), (w_k, 0), (w_k, 1)]):
                    for k in range(KT):
                        mm = pe.matmul(banks[n][:, 0:T], w[:, k, m * P:(m + 1) * P], xn_t[:, k, :],
                                       start=(k == 0), stop=(k == KT - 1))
                    mm.then_inc(proj_pe.sem, 1)
                for i in range(TT):
                    pe.wait_ge(proj_act.sem, proj_act.at(b, i + 1))
                    for k in range(KT):
                        mm = pe.matmul(banks[i][:, 0:E], xn_t[:, k, i * P:(i + 1) * P], w_v[:, k, :],
                                       start=(k == 0), stop=(k == KT - 1))
                    mm.then_inc(proj_pe.sem, 1)
                pe.wait_ge(proj_act.sem, proj_act.at(b, 4))
                for i in range(TT):
                    if i:
                        pe.wait_ge(v_done.sem, v_done.at(b, i))
                    for m in range(KT):
                        mm = pe.matmul(banks[(3 + i) % 4][:, 0:RJ], qf[:, m, i * P:(i + 1) * P],
                                       rel_k[:, m].rearrange("p j h -> p (j h)"),
                                       start=(m == 0), stop=(m == KT - 1))
                    mm.then_inc(proj_pe.sem, 1)

            def maxima_head(b, h):
                if h == 0:
                    pe.wait_ge(stacked.sem, stacked.at(b, 12))
                    pe.wait_ge(v_done.sem, v_done.at(b, TT))
                    pe.wait_ge(proj_act.sem, proj_act.at(b, 7))
                else:
                    pe.wait_ge(max_done.sem, max_done.at(b, h))
                for i in range(TT):
                    mm = pe.matmul(S[:, i, PAD:PAD + T], q_st[0:KST, h, i * P:(i + 1) * P],
                                   k_st[0:KST, h, :], start=True, stop=True)
                mm.then_inc(max_pe.sem, 1)

            def negate(b):
                pe.wait_ge(max_done.sem, max_done.at(b, AH))
                for i in range(TT):
                    last = turn(O[0:AH, i * P:(i + 1) * P], maxima[:, i, :])
                last.then_inc(neg_pe.sem, 1)

            def attend(b, h):
                if h == 0:
                    pe.wait_ge(neg_in.sem, neg_in.at(b, 1))
                else:
                    pe.wait_ge(exp_done.sem, exp_done.at(b, h))
                for i in range(TT):
                    mm = pe.matmul(S[:, i, PAD:PAD + T], k_st[:, h, i * P:(i + 1) * P],
                                   q_st[:, h, :], start=True, stop=True)
                mm.then_inc(sc_pe.sem, 1)

            def values(b, g):
                pe.wait_ge(exp_done.sem, exp_done.at(b, GRP * (g + 1)))
                if g:
                    pe.wait_ge(o_copied.sem, o_copied.at(b, g))
                else:
                    pe.wait_ge(neg_dve.sem, neg_dve.at(b, 1))
                    pe.wait_ge(neg_act.sem, neg_act.at(b, 1))
                for i in range(TT):
                    for l in range(GRP):
                        h = GRP * g + l
                        mm = pe.matmul(O[32 * l:32 * l + VC, 0:T], v_one[:, i, h, :], p_t[:, h % PTS, i, :],
                                       start=(i == 0), stop=(i == TT - 1), skip_group_check=True)
                mm.then_inc(pv_done.sem, 1)

            def output(b):
                pe.wait_ge(relw_in.sem, relw_in.at(b, TT))
                pe.wait_ge(o_copied.sem, o_copied.at(b, AH // GRP))
                for i in range(TT):
                    last = turn(O[:, i * P:(i + 1) * P], rel_w[:, i, 0:P])
                last.then_inc(rw_pe.sem, 1)
                for i in range(TT):
                    last = turn(S[0:RJ - P, 0, i * P:(i + 1) * P], rel_w[:, i, P:RJ])
                last.then_inc(rw_pe.sem, 1)
                for n, i in enumerate((1, 2, 0)):
                    if n == 2:
                        pe.wait_ge(rw_act.sem, rw_act.at(b, 2))
                    for g in range(AH // GRP):
                        last = turn(S[:, i, g * P:(g + 1) * P], o_sb[:, g, i * P:(i + 1) * P])
                    last.then_inc(ot_pe.sem, 1)
                for n, i in enumerate((1, 2, 0)):
                    if n:
                        pe.wait_ge(att_dve.sem, att_dve.at(b, 3 * (n - 1) + 1))
                    pe.matmul(O[:, 0:E], rwt0[:, i * P:(i + 1) * P],
                              rel_v0[:].rearrange("p h d -> p (h d)"), start=True, stop=False)
                    pe.matmul(O[:, 0:E], rwt1[:, i * P:(i + 1) * P],
                              rel_v1[:].rearrange("p h d -> p (h d)"), start=False, stop=True
                              ).then_inc(or_pe.sem, 1)
                turned(attn, att_dve, 3 * TT, at_pe, b)
                pe.wait_ge(at_act.sem, at_act.at(b, 2))
                for i in range(TT):
                    dst = S[:, 2, i * E:(i + 1) * E] if i < 2 else O[:, 0:E]
                    for k in range(KT):
                        mm = pe.matmul(dst, attn_t[:, k, i * P:(i + 1) * P], w_o[:, k, :],
                                       start=(k == 0), stop=(k == KT - 1))
                    mm.then_inc(wo_pe.sem, 1)
                turned(xn2, ln3, 3 * TT + 1, x2_pe, b)
                pe.wait_ge(x2_hi_done.sem, x2_hi_done.at(b, 2))
                pe.wait_ge(x2_lo_done.sem, x2_lo_done.at(b, 2))
                for i in range(TT):
                    n = 0
                    for xs, ws in ((x2_hi, wr_hi), (x2_hi, wr_lo), (x2_lo, wr_hi)):
                        for k in range(KT):
                            mm = pe.matmul(S[:, 2, i * NE:(i + 1) * NE], xs[:, k, i * P:(i + 1) * P],
                                           ws[:, k, :], start=(n == 0), stop=(n == 3 * KT - 1))
                            n += 1
                mm.then_inc(r_pe.sem, 1)

            def gate_up(f, n):
                e, m = n // FT, n % FT
                for dst, hi, lo, done, free in ((G, wg_hi, wg_lo, gate_pe, silu_done),
                                                (U, wu_hi, wu_lo, up_pe, h_done)):
                    if n:
                        pe.wait_ge(free.sem, free.at(f, n))
                    j = 0
                    for ws, xs in ((hi, x2_hi), (hi, x2_lo), (lo, x2_hi)):
                        for k in range(KT):
                            mm = pe.matmul(dst[:, 0:T], ws[:, e, k, m * P:(m + 1) * P], xs[:, k, :],
                                           start=(j == 0), stop=(j == 3 * KT - 1))
                            j += 1
                    mm.then_inc(done.sem, 1)

            def down(f, e):
                pe.wait_ge(h_done.sem, h_done.at(f, FT * (e + 1)))
                if e:
                    pe.wait_ge(acc_done.sem, acc_done.at(f, TT * e))
                for i in range(TT):
                    for m in range(FT):
                        mm = pe.matmul(D[:, i // 2, (i % 2) * E:(i % 2 + 1) * E],
                                       hT[:, (FT * e + m) % 3, i * P:(i + 1) * P], w_d[:, e, m, :],
                                       start=(m == 0), stop=(m == FT - 1))
                mm.then_inc(down_pe.sem, 1)

            def do(step, b, f):
                kind = step[0]
                if kind == "mix":
                    mix(b)
                elif kind == "project":
                    project(b)
                elif kind == "maxima":
                    maxima_head(b, step[1])
                elif kind == "negate":
                    negate(b)
                elif kind == "attend":
                    attend(b, step[1])
                elif kind == "values":
                    values(b, step[1])
                elif kind == "output":
                    output(b)
                elif kind == "ffn":
                    if step[1] == "u":
                        gate_up(f, step[2])
                    else:
                        down(f, step[2])

            rounds(pe, do)

        @block.scalar
        def _(act):
            act.wait_ge(loaded, 16 * N_LOADS)
            nc.scalar.activation(bq4[:], bq4[:], ACT.Copy, scale=AD ** -0.5).then_inc(set_act, 1)
            act.wait_ge(set_dve, SET_DVE_WB)
            nc.scalar.activation(zone(1024, IT, L), zone(0, IT, L), ACT.Exp).then_inc(set_act, 1)
            act.wait_ge(set_pe, IT)
            nc.scalar.activation(ew_t[:], S[:, 0:IT, 0:L], ACT.Copy).then_inc(set_act, 1)
            nc.scalar.activation(wr_hi[:], w_r[:], ACT.Copy).then_inc(set_act, 1)
            act.wait_ge(gu_loaded, 32)
            nc.scalar.activation(wg_hi[:], zone(0, NE, KT, FI), ACT.Copy).then_inc(set_act, 1)
            nc.scalar.activation(wu_hi[:], zone(4096, NE, KT, FI), ACT.Copy).then_inc(set_act, 1)
            act.wait_ge(set_dve, SET_DVE_ALL)

            def root(b, stats, steps, done, tiles):
                act.wait_ge(stats.sem, stats.at(b, steps))
                nc.scalar.activation(rstd[:, 0:tiles], mv[:, 0:tiles, 1], ACT.Sqrt, bias=eps[:]
                                     ).then_inc(done.sem, 1)

            def mix(b):
                for i in range(IT):
                    act.wait_ge(mix_pe.sem, mix_pe.at(b, i + 1))
                    nc.scalar.activation(ek[:, i].rearrange("p (h d) -> p h d", h=H),
                                         S[:, i].rearrange("p (h c) -> p h c", h=H)[:, :, 0:F],
                                         ACT.Exp).then_inc(mix_act.sem, 1)
                act.wait_ge(mix_pe.sem, mix_pe.at(b, 3))
                nc.scalar.activation(eq, S[:, 2].rearrange("p (m t) -> p m t", m=KT), ACT.Exp,
                                     scale=-1.0).then_inc(mix_act.sem, 1)
                root(b, mix_dve, 5 + 2 * IT, mix_root, IT)
                root(b, ln2, 2 * TT, ln2_root, TT)

            def project(b):
                for k in range(KT):
                    act.wait_ge(xt_pe.sem, xt_pe.at(b, k + 1))
                    nc.scalar.activation(xn_t[:, k], S[:, k, 0:T], ACT.Copy).then_inc(xt_act.sem, 1)
                banks = [S[:, 2], S[:, 0], S[:, 1], O[:]]
                for n in range(4):
                    act.wait_ge(proj_pe.sem, proj_pe.at(b, n + 1))
                    if n < 2:
                        nc.scalar.activation(qf[:, n], banks[n][:, 0:T], ACT.Identity, bias=bq4[:, n:n + 1],
                                             scale=AD ** -0.5).then_inc(proj_act.sem, 1)
                    else:
                        nc.scalar.activation(kf[:, n - 2], banks[n][:, 0:T], ACT.Identity,
                                             bias=bk1[:, n - 2:n - 1], scale=1.0).then_inc(proj_act.sem, 1)
                for i in range(TT):
                    act.wait_ge(proj_pe.sem, proj_pe.at(b, 8 + i))
                    nc.scalar.activation(rel_log[:, i], banks[(3 + i) % 4][:, 0:RJ], ACT.Copy
                                         ).then_inc(proj_act.sem, 1)

            def negate(b):
                act.wait_ge(neg_pe.sem, neg_pe.at(b, 1))
                nc.scalar.activation(neg_max[:, 0], O[0:AH, 0:T], ACT.Copy, scale=-1.0
                                     ).then_inc(neg_act.sem, 1)

            def attend(b, h):
                act.wait_ge(sc_add.sem, sc_add.at(b, 4 * (h + 1)))
                if h >= PTS:
                    act.wait_ge(pv_done.sem, pv_done.at(b, (h - PTS) // GRP + 1))
                    act.wait_ge(win_done.sem, win_done.at(b, WINS * (h - PTS + 1)))
                nc.scalar.activation(p_t[:, h % PTS], S[:, :, PAD:PAD + T], ACT.Exp
                                     ).then_inc(exp_done.sem, 1)

            def values(b, g):
                act.wait_ge(pv_done.sem, pv_done.at(b, g + 1))
                nc.scalar.activation(o_sb[:, g], O[:, 0:T], ACT.Copy).then_inc(o_copied.sem, 1)

            def output(b):
                act.wait_ge(rw_pe.sem, rw_pe.at(b, 1))
                nc.scalar.activation(rwt0, O[:, 0:T], ACT.Copy).then_inc(rw_act.sem, 1)
                act.wait_ge(rw_pe.sem, rw_pe.at(b, 2))
                nc.scalar.activation(rwt1, S[0:RJ - P, 0, 0:T], ACT.Copy).then_inc(rw_act.sem, 1)
                for k in range(KT):
                    act.wait_ge(at_pe.sem, at_pe.at(b, k + 1))
                    nc.scalar.activation(attn_t[:, k], S[:, k, 0:T], ACT.Copy).then_inc(at_act.sem, 1)
                root(b, ln3, 2 * TT, ln3_root, TT)
                if not isinstance(b, int):
                    act.wait_ge(down_pe.sem, down_pe.at(b - 1, NE))
                for k in range(KT):
                    act.wait_ge(x2_pe.sem, x2_pe.at(b, k + 1))
                    nc.scalar.activation(x2_hi[:, k], S[:, k, 0:T], ACT.Copy).then_inc(x2_hi_done.sem, 1)
                act.wait_ge(r_pe.sem, r_pe.at(b, 1))
                nc.scalar.activation(rt[0], S[:, 2, 0:TT * NE].rearrange("p (i e) -> p i e", i=TT),
                                     ACT.Exp, scale=neg_temp[:]).then_inc(r_act.sem, 1)
                act.wait_ge(r_dve.sem, r_dve.at(b, R_DIST))
                nc.scalar.activation(rt[4], rt[3], ACT.Exp, scale=-1.0 / 0.1).then_inc(r_act.sem, 1)
                nc.scalar.activation(rt[5], rt[3], ACT.Exp, scale=-1.0 / 0.3).then_inc(r_act.sem, 1)

            def gate(f, n):
                act.wait_ge(gate_pe.sem, gate_pe.at(f, n + 1))
                if n:
                    act.wait_ge(h_done.sem, h_done.at(f, n))
                nc.scalar.activation(silu[:], G[:, 0:T], ACT.Silu).then_inc(silu_done.sem, 1)

            def do(step, b, f):
                kind = step[0]
                if kind == "mix":
                    mix(b)
                elif kind == "project":
                    project(b)
                elif kind == "negate":
                    negate(b)
                elif kind == "attend":
                    attend(b, step[1])
                elif kind == "values":
                    values(b, step[1])
                elif kind == "output":
                    output(b)
                elif kind == "ffn" and step[1] == "u":
                    gate(f, step[2])

            rounds(act, do)

        @block.vector
        def _(dve):
            steps = [0]

            def mark(ins):
                steps[0] += 1
                ins.then_inc(set_dve, 1)

            mark(dve.memset(band_t[:], 0.0))
            mark(dve.memset(S[:], 0.0))
            mark(dve.memset(O[:], 0.0))
            mark(dve.memset(v_one[:], 1.0))
            mark(dve.memset(x_in[F:F + 1], 1.0))
            mark(dve.memset(k_st[KST:KST + 2], 1.0))
            mark(dve.memset(eps[:], EPS))
            mark(dve.memset(one[:], 1.0))
            mark(dve.memset(root_e[:], float(E) ** 0.5))
            dve.wait_ge(loaded, 16 * N_LOADS)
            mark(dve.tensor_copy(zone(1024, IT, L), Z[:, 512:640].bitcast(U8).rearrange("p (i s) -> p i s", i=IT)))
            dve.wait_ge(set_dve, steps[0])
            mark(dve.tensor_tensor(zone(0, IT, L), zone(0, IT, L), zone(1024, IT, L), ALU.mult))
            assert steps[0] == SET_DVE_WB
            for h in range(H):
                mark(dve.tensor_copy(resid[0:F, h], ident[0:F, 0:F]))
            for m in range(KT):
                mark(dve.tensor_tensor(rel_k[:, m], Z[:, 640:640 + NJ].unsqueeze(2).broadcast_to([P, NJ, AH]),
                                       head_of_row[:, m].unsqueeze(1).broadcast_to([P, NJ, AH]), ALU.mult))
            mark(dve.tensor_tensor(rel_v0[:], Z[:, 656:656 + AD].unsqueeze(1).broadcast_to([P, AH, AD]),
                                   head_of_rel[:].unsqueeze(2).broadcast_to([P, AH, AD]), ALU.mult))
            n1 = RJ - P
            mark(dve.tensor_tensor(rel_v1[:], Z[0:n1, 672:672 + AD].unsqueeze(1).broadcast_to([n1, AH, AD]),
                                   head_of_rel[0:n1].unsqueeze(2).broadcast_to([n1, AH, AD]), ALU.mult))
            assert steps[0] == SET_DVE_STAGED
            mark(dve.reciprocal(neg_temp[:], neg_temp[:]))
            dve.wait_ge(set_dve, steps[0])
            mark(dve.tensor_scalar(neg_temp[:], neg_temp[:], -1.0, None, ALU.mult))
            dve.wait_ge(set_act, 4)
            mark(dve.tensor_tensor(wr_lo[:], w_r[:], wr_hi[:].bitcast(F32), ALU.subtract))
            dve.wait_ge(set_act, 5)
            mark(dve.tensor_tensor(wg_lo[:], zone(0, NE, KT, FI), wg_hi[:].bitcast(F32), ALU.subtract))
            dve.wait_ge(set_act, 6)
            mark(dve.tensor_tensor(wu_lo[:], zone(4096, NE, KT, FI), wu_hi[:].bitcast(F32), ALU.subtract))
            assert steps[0] == SET_DVE_ALL
            dve.wait_ge(set_dve, SET_DVE_ALL)

            def carry_wait():
                dve.memset(spare[:, 0:1], 0.0)

            def norm(b, sg, rooted, first, src, dst, tiles):
                k = first
                for i in range(tiles):
                    dve.bn_stats(stat[:, i], src(i)).then_inc(sg.sem, 1)
                dve.wait_ge(sg.sem, sg.at(b, k + tiles))
                carry_wait()
                for i in range(tiles):
                    dve.bn_aggr(mv[:, i], stat[:, i]).then_inc(sg.sem, 1)
                dve.wait_ge(rooted.sem, rooted.at(b, 1))
                dve.reciprocal(rstd[:, 0:tiles], rstd[:, 0:tiles]).then_inc(sg.sem, 1)
                dve.wait_ge(sg.sem, sg.at(b, k + 2 * tiles + 1))
                for i in range(tiles):
                    dve.tensor_scalar(dst(i), src(i), mv[:, i, 0:1], rstd[:, i:i + 1], ALU.subtract,
                                      ALU.mult).then_inc(sg.sem, 1)

            def mix(b):
                for i in range(IT):
                    dve.wait_ge(mix_act.sem, mix_act.at(b, i + 1))
                    dve.tensor_tensor(ekv[:, i].rearrange("p (h d) -> p h d", h=H),
                                      ek[:, i].rearrange("p (h d) -> p h d", h=H),
                                      S[:, i].rearrange("p (h c) -> p h c", h=H)[:, :, F:2 * F],
                                      ALU.mult).then_inc(mix_dve.sem, 1)
                dve.wait_ge(mix_act.sem, mix_act.at(b, 3))
                dve.wait_ge(mix_pe.sem, mix_pe.at(b, 4))
                dve.scalar_tensor_tensor(dd.rearrange("p m t -> p (m t)"), eq.rearrange("p m t -> p (m t)"),
                                         1.0, O[:, 0:KT * L], ALU.add, ALU.mult).then_inc(mix_dve.sem, 1)
                dve.wait_ge(mix_dve.sem, mix_dve.at(b, 3))
                dve.reciprocal(dd, dd).then_inc(mix_dve.sem, 1)
                dve.wait_ge(mix_pe.sem, mix_pe.at(b, 5))
                dve.wait_ge(mix_dve.sem, mix_dve.at(b, 4))
                dve.tensor_tensor(y_t.rearrange("p m t -> p (m t)"), S[:, 0, 0:KT * L],
                                  dd.rearrange("p m t -> p (m t)"), ALU.mult).then_inc(mix_dve.sem, 1)
                dve.wait_ge(mix_pe.sem, mix_pe.at(b, 7))
                norm(b, mix_dve, mix_root, 5, lambda i: S[:, 1, i * E:(i + 1) * E], lambda i: hid[:, i], IT)
                dve.wait_ge(mix_dve.sem, mix_dve.at(b, 12))
                dve.wait_ge(hid_ready.sem, hid_ready.at(b, 5))
                norm(b, ln2, ln2_root, 0, lambda i: hid[:, i], lambda i: xn[:, i], TT)

            def project(b):
                banks = [S[:, 2], S[:, 0], S[:, 1]]
                for i in range(TT):
                    dve.wait_ge(proj_pe.sem, proj_pe.at(b, 5 + i))
                    dve.tensor_tensor(v_one[:, i, :, 0:AD], banks[i][:, 0:E].rearrange("p (h d) -> p h d", h=AH),
                                      bv_all[:].rearrange("p (h d) -> p h d", h=AH), ALU.add
                                      ).then_inc(v_done.sem, 1)
                for n, (src, rest, p3) in enumerate(((qf, qr, parts[0:3]), (kf, kr, parts[3:6]))):
                    k = 4 * n
                    dve.wait_ge(proj_act.sem, proj_act.at(b, 2 + 2 * n))
                    dve.tensor_copy(p3[0], src).then_inc(split.sem, 1)
                    dve.wait_ge(split.sem, split.at(b, k + 1))
                    dve.tensor_tensor(rest, src, p3[0], ALU.subtract).then_inc(split.sem, 1)
                    dve.wait_ge(split.sem, split.at(b, k + 2))
                    dve.tensor_copy(p3[1], rest).then_inc(split.sem, 1)
                    dve.wait_ge(split.sem, split.at(b, k + 3))
                    dve.tensor_tensor(p3[2], rest, p3[1], ALU.subtract).then_inc(split.sem, 1)

            def add_band(b, h, band, done):
                for c in range(P // BL):
                    rows = slice(c * BL, (c + 1) * BL)
                    pitch = S[rows].ap[0][0]
                    win = bass.AP(tensor=S, offset=S[rows].offset + PAD + c * BL - WIN,
                                  ap=[[pitch, BL], [512 + P, TT], [1, WD_]])
                    dve.tensor_tensor(win, win, band[rows, :, :, h], ALU.add).then_inc(done.sem, 1)

            def maxima_head(b, h):
                if h == 0:
                    dve.wait_ge(band_in.sem, band_in.at(b, 5))
                dve.wait_ge(max_pe.sem, max_pe.at(b, h + 1))
                add_band(b, h, band_t, max_add)
                dve.wait_ge(max_add.sem, max_add.at(b, 4 * (h + 1)))
                dve.tensor_reduce(maxima[:, :, h], S[:, :, PAD:PAD + T], AX, ALU.max).then_inc(max_done.sem, 1)

            def negate(b):
                dve.wait_ge(neg_act.sem, neg_act.at(b, 1))
                dve.scalar_tensor_tensor(neg_max[:, 1], O[0:AH, 0:T], -1.0, neg_max[:, 0], ALU.mult,
                                         ALU.subtract).then_inc(neg_dve.sem, 1)

            def attend(b, h):
                dve.wait_ge(sc_pe.sem, sc_pe.at(b, h + 1))
                add_band(b, h, band_s, sc_add)

            def output(b):
                for n, i in enumerate((1, 2, 0)):
                    dve.wait_ge(or_pe.sem, or_pe.at(b, n + 1))
                    dve.wait_ge(ot_pe.sem, ot_pe.at(b, n + 1))
                    heads = S[:, i].rearrange("p (h d) -> p h d", h=AH)
                    dve.tensor_copy(attn[:, i], O[:, 0:E]).then_inc(att_dve.sem, 1)
                    dve.reciprocal(rden[:, i], heads[:, :, AD]).then_inc(att_dve.sem, 1)
                    dve.wait_ge(att_dve.sem, att_dve.at(b, 3 * n + 2))
                    av = attn[:, i].rearrange("p (h d) -> p h d", h=AH)
                    dve.tensor_tensor(av, av, heads[:, :, 0:AD], ALU.add).then_inc(att_mid.sem, 1)
                    dve.wait_ge(att_mid.sem, att_mid.at(b, n + 1))
                    dve.tensor_tensor(av, av, rden[:, i].unsqueeze(2).broadcast_to([P, AH, AD]), ALU.mult
                                      ).then_inc(att_dve.sem, 1)
                if not isinstance(b, int):
                    dve.wait_ge(stored.sem, stored.at(b - 1, 1))
                dve.wait_ge(hid_bo.sem, hid_bo.at(b, 1))
                for i in range(TT):
                    dve.wait_ge(wo_pe.sem, wo_pe.at(b, max(i + 1, 2)))
                    src = S[:, 2, i * E:(i + 1) * E] if i < 2 else O[:, 0:E]
                    dve.tensor_tensor(res[:, i], src, hid[:, i], ALU.add).then_inc(res_ready.sem, 1)
                dve.wait_ge(res_ready.sem, res_ready.at(b, TT))
                norm(b, ln3, ln3_root, 0, lambda i: res[:, i], lambda i: xn2[:, i], TT)
                for k in range(KT):
                    dve.wait_ge(x2_hi_done.sem, x2_hi_done.at(b, k + 1))
                    dve.tensor_tensor(x2_lo[:, k], S[:, k, 0:T], x2_hi[:, k].bitcast(F32), ALU.subtract
                                      ).then_inc(x2_lo_done.sem, 1)
                route(b)

            def route(b):
                k = [0]

                def step(ins):
                    k[0] += 1
                    ins.then_inc(r_dve.sem, 1)
                    dve.wait_ge(r_dve.sem, r_dve.at(b, k[0]))

                def each(x):
                    return x.unsqueeze(2).broadcast_to([P, TT, NE])

                ex, inh, zone_, dist, w, fb, rank, fbw = rt[0:8]
                dve.wait_ge(r_act.sem, r_act.at(b, 1))
                step(dve.tensor_scalar(inh, ex, 1.0, None, ALU.add))
                step(dve.reciprocal(inh, inh))
                step(dve.tensor_scalar(dist, inh, CENTER, None, ALU.subtract))
                step(dve.scalar_tensor_tensor(dist, dist, -1.0, dist, ALU.mult, ALU.max))
                assert k[0] == R_DIST
                step(dve.tensor_scalar(zone_, inh, ZONE_HI, None, ALU.is_le))
                step(dve.scalar_tensor_tensor(zone_, inh, ZONE_LO, zone_, ALU.is_ge, ALU.mult))
                dve.wait_ge(r_act.sem, r_act.at(b, 3))
                step(dve.tensor_tensor(w, w, zone_, ALU.mult))
                step(dve.tensor_reduce(rsum, w, AX, ALU.add))
                step(dve.tensor_scalar(rsum, rsum, 1e-8, None, ALU.is_lt))
                other = fb.unsqueeze(2).broadcast_to([P, TT, NE, NE])
                own = fb.unsqueeze(3).broadcast_to([P, TT, NE, NE])
                low = earlier[:].unsqueeze(1).broadcast_to([P, TT, NE, NE])
                step(dve.tensor_tensor(rpair, other, own, ALU.is_equal))
                step(dve.tensor_tensor(rpair, rpair, low, ALU.mult))
                step(dve.tensor_tensor(rpair2, other, own, ALU.is_gt))
                step(dve.tensor_tensor(rpair, rpair, rpair2, ALU.add))
                step(dve.tensor_reduce(rank, rpair, AX, ALU.add))
                step(dve.scalar_tensor_tensor(fbw, rank, 2.0, fb, ALU.is_lt, ALU.mult))
                step(dve.tensor_reduce(rt[8][:, :, 0], fbw, AX, ALU.add))
                step(dve.tensor_scalar(rt[8][:, :, 0], rt[8][:, :, 0], 1e-8, None, ALU.max))
                step(dve.reciprocal(rt[8][:, :, 0], rt[8][:, :, 0]))
                step(dve.tensor_tensor(fbw, fbw, each(rt[8][:, :, 0]), ALU.mult))
                carry_wait()
                step(dve.copy_predicated(w, each(rsum.bitcast(I32)), fbw))
                step(dve.tensor_reduce(rt[8][:, :, 1], w, AX, ALU.add))
                step(dve.tensor_scalar(rt[8][:, :, 1], rt[8][:, :, 1], 1e-8, None, ALU.max))
                step(dve.reciprocal(rt[8][:, :, 1], rt[8][:, :, 1]))
                step(dve.tensor_tensor(wgt[:], w, each(rt[8][:, :, 1]), ALU.mult))
                assert k[0] == R_STEPS

            def hidden(f, n):
                dve.wait_ge(silu_done.sem, silu_done.at(f, n + 1))
                dve.wait_ge(up_pe.sem, up_pe.at(f, n + 1))
                if n >= 3:
                    dve.wait_ge(down_pe.sem, down_pe.at(f, (n - 3) // FT + 1))
                dve.tensor_tensor(hT[:, n % 3], silu[:], U[:, 0:T], ALU.mult).then_inc(h_done.sem, 1)

            def accumulate(f, e):
                dve.wait_ge(down_pe.sem, down_pe.at(f, e + 1))
                if e:
                    dve.wait_ge(acc_done.sem, acc_done.at(f, TT * e))
                for i in range(TT):
                    dve.scalar_tensor_tensor(res[:, i], D[:, i // 2, (i % 2) * E:(i % 2 + 1) * E],
                                             wgt[:, i, e:e + 1], res[:, i], ALU.mult, ALU.add
                                             ).then_inc(acc_done.sem, 1)

            def do(step, b, f):
                kind = step[0]
                if kind == "mix":
                    mix(b)
                elif kind == "project":
                    project(b)
                elif kind == "maxima":
                    maxima_head(b, step[1])
                elif kind == "negate":
                    negate(b)
                elif kind == "attend":
                    attend(b, step[1])
                elif kind == "output":
                    output(b)
                elif kind == "ffn":
                    if step[1] == "u":
                        hidden(f, step[2])
                    else:
                        accumulate(f, step[2])

            rounds(dve, do)

        @block.gpsimd
        def _(pool):
            pool.wait_ge(set_dve, SET_DVE_ALL)
            pool.wait_ge(loaded, 16 * N_LOADS)

            def mix(b):
                pool.wait_ge(idx_loaded.sem, idx_loaded.at(b, 1))
                if not isinstance(b, int):
                    pool.wait_ge(hid_ready.sem, hid_ready.at(b - 1, 5))
                nc.gpsimd.tensor_tensor(spare[:, 1:2], one[:], one[:], ALU.mult)
                pool.indirect_dma_start(txt_row[:], None, a["L0_txt_W_E"],
                                        bass.IndirectOffsetOnAxis(ap=txt_idx[:, 0:1], axis=0)
                                        ).then_inc(txt_loaded.sem, 16)
                for i in range(IT):
                    pool.wait_ge(mix_dve.sem, mix_dve.at(b, 11 + i))
                    nc.gpsimd.tensor_tensor(hid[:, i], hid[:, i], ln_g[:], ALU.mult).then_inc(hid_ready.sem, 1)
                for i in range(IT):
                    pool.wait_ge(hid_ready.sem, hid_ready.at(b, i + 1))
                    nc.gpsimd.tensor_tensor(hid[:, i], hid[:, i], ln_b[:], ALU.add).then_inc(hid_ready.sem, 1)
                pool.wait_ge(txt_loaded.sem, txt_loaded.at(b, 1))
                if not isinstance(b, int):
                    pool.wait_ge(res_ready.sem, res_ready.at(b - 1, TT))
                nc.gpsimd.tensor_tensor(hid[:, IT], txt_row[:], root_e[:].broadcast_to([P, E]), ALU.mult
                                        ).then_inc(hid_ready.sem, 1)

            def project(b):
                pool.wait_ge(ln2.sem, ln2.at(b, 3 * TT + 1))
                nc.gpsimd.tensor_tensor(hid[:], hid[:], bo_all[:].unsqueeze(1).broadcast_to([P, TT, E]),
                                        ALU.add).then_inc(hid_bo.sem, 1)

            def attend(b, h):
                if h == 0:
                    pool.wait_ge(max_done.sem, max_done.at(b, AH))
                pool.wait_ge(exp_done.sem, exp_done.at(b, h + 1))
                n = 0
                for c in range(P // BL):
                    rows = slice(c * BL, (c + 1) * BL)
                    pitch = Z[rows].ap[0][0]
                    base = Z[rows].offset + (h % PTS) * TT * T + c * BL - WIN
                    if c == 0:
                        runs = [(0, 1, WIN, WD_), (1, TT, 0, WD_)]
                    elif c == P // BL - 1:
                        runs = [(0, TT - 1, 0, WD_), (TT - 1, TT, 0, WD_ - WIN)]
                    else:
                        runs = [(0, TT, 0, WD_)]
                    for i0, i1, lo, hi in runs:
                        if n:
                            pool.wait_ge(win_done.sem, win_done.at(b, WINS * h + n))
                        elif h:
                            pool.wait_ge(win_done.sem, win_done.at(b, WINS * h))
                        else:
                            pool.wait_ge(hid_bo.sem, hid_bo.at(b, 1))
                        n += 1
                        win = bass.AP(tensor=Z, offset=base + i0 * (T + P) + lo,
                                      ap=[[pitch, BL], [T + P, i1 - i0], [1, hi - lo]])
                        nc.gpsimd.tensor_tensor(
                            band_t[rows, i0:i1, lo:hi, h], win,
                            one[rows].unsqueeze(2).broadcast_to([BL, i1 - i0, hi - lo]), ALU.mult
                        ).then_inc(win_done.sem, 1)

            def do(step, b, f):
                kind = step[0]
                if kind == "mix":
                    mix(b)
                elif kind == "project":
                    project(b)
                elif kind == "attend":
                    attend(b, step[1])

            rounds(pool, do)


_NAMES = ["x", "L0_tok_w_bias", "L0_tok_Wk_b", "L0_tok_Wv_b", "L0_tok_Wq_b", "L0_tok_out_w", "L0_tok_out_b",
          "L0_tok_ln_g", "L0_tok_ln_b", "L0_txt_W_E", "L0_attn_Wq", "L0_attn_bq", "L0_attn_Wk", "L0_attn_bk",
          "L0_attn_Wv", "L0_attn_bv", "L0_attn_Wo", "L0_attn_bo", "L0_attn_emb_rel_k", "L0_attn_emb_rel_v",
          "L0_ffn_Wg", "L0_ffn_Wu", "L0_ffn_Wd", "L0_ffn_Wr", "L0_ffn_temperature"]


def kernel(**inputs):
    import concourse.bacc as bacc
    from concourse.bass_utils import run_bass_kernel_spmd

    data = {n: np.ascontiguousarray(inputs[n]) for n in _NAMES}
    data["tok_wk_t"] = np.ascontiguousarray(np.asarray(inputs["L0_tok_Wk_w"]).T)
    data["tok_wv_t"] = np.ascontiguousarray(np.asarray(inputs["L0_tok_Wv_w"]).T)
    data["tok_wq_t"] = np.ascontiguousarray(np.asarray(inputs["L0_tok_Wq_w"]).T)
    data["txt_t"] = np.ascontiguousarray(inputs["x_txt"]).reshape(NB, TXT, 1)
    data["mask"] = np.ascontiguousarray(inputs["L0_tok_local_mask"])
    row = np.arange(P)
    data["ident"] = np.eye(P, dtype=np.float32)
    data["head_of_row"] = (row[:, None, None] // AD + (P // AD) * np.arange(KT)[None, :, None]
                           == np.arange(AH)[None, None, :]).astype(np.float32)
    data["head_of_rel"] = (row[:, None] % AH == np.arange(AH)[None, :]).astype(np.float32)
    data["earlier"] = np.broadcast_to((np.arange(NE)[None, :] < np.arange(NE)[:, None]).astype(np.float32),
                                      (P, NE, NE)).copy()

    nc = bacc.Bacc("TRN2", target_bir_lowering=False, num_devices=1)
    arrays, aps = {}, {}
    for name, array in data.items():
        arrays[f"in_{name}"] = array
        aps[name] = nc.dram_tensor(f"in_{name}", array.shape, mybir.dt.from_np(array.dtype),
                                   kind="ExternalInput").ap()
    out = nc.dram_tensor("out_0", (NB, T, E), F32, kind="ExternalOutput").ap()
    fusion_block(nc, aps, out)
    return run_bass_kernel_spmd(nc, [arrays], core_ids=[0]).results[0]["out_0"]
```

```python
from contextlib import ExitStack

import numpy as np

import concourse.bass as bass
from concourse import mybir

F32 = mybir.dt.float32
F32R = mybir.dt.float32r
BF16 = mybir.dt.bfloat16
I32 = mybir.dt.int32
U8 = mybir.dt.uint8
ALU = mybir.AluOpType
ACT = mybir.ActivationFunctionType
AX = mybir.AxisListType.X

P = 128
NB = 8
F, L, H = 64, 256, 4
E = H * F
KT = E // P
TXT = 128
T = L + TXT
TT = T // P
IT = L // P
AH, AD = 16, 16
WIN = 4
NJ = 2 * WIN + 1
NE = 8
FI = 256
FT = FI // P
SLOTS = 6
KST = SLOTS * AD
Q_PART = [0, 0, 1, 0, 2, 1]
K_PART = [0, 1, 0, 2, 0, 1]
BL = 32
WD_ = BL + 2 * WIN
ROW = WD_ * AH
RJ = NJ * AH
BPITCH = BL * ROW + BL * AH
LEAD = 4096
BAND = LEAD + (T // BL) * BPITCH + 8192
PAD = WIN
TP = T + 2 * PAD
GRP = 4
PTS = 6
VC = AD + 1
EPS = 1e-5
WINS = P // BL
N_LOADS = (9, 4, 13 + P // AD + NJ)
N_ZERO = 7
N_CONSTS = 7
FILL_MIX = [("mix_in", 2), ("mix_sums", 3), ("mix_out", 2), ("mix_norm", 2), ("norm_stats", 1),
            ("turn_norm", 1), ("project_qk", 1), ("project_rest", 5)]
FILL_NEGATE = 3
FILL_OUT = [("turn_outputs", 1), ("turn_weights", 1), ("rel_values", 1), ("turn_attn", 0),
            ("residual", 0), ("turn_x2", 0), ("router", 0)]
R_DIST = 4
ZONE_LO = float(np.float32(0.5 - np.log(4.0 / 3.0)))
ZONE_HI = 0.5
CENTER = float(np.float32(1.0 / np.e))


class Signal:

    def __init__(self, sem, n, unit=1):
        self.sem, self.n, self.unit = sem, n, unit

    def at(self, b, k):
        return b * (self.n * self.unit) + k * self.unit


def fusion_block(nc, a, out):
    ctx = ExitStack()

    def sb(name, shape, dt=F32):
        return ctx.enter_context(nc.sbuf_tensor(name, shape, dt))

    def ps(name, shape, dt=F32):
        return ctx.enter_context(nc.psum_tensor(name, shape, dt))

    def sem(name):
        return ctx.enter_context(nc.semaphore(name))

    def sig(name, n, unit=1):
        return Signal(sem(name), n, unit)

    with ctx:
        ident = sb("ident", [P, P])
        head_of_row = sb("head_of_row", [P, KT, AH])
        head_of_rel = sb("head_of_rel", [P, AH])
        earlier = sb("earlier", [P, NE, NE])
        wkv = sb("wkv", [F + 1, 2 * F])
        wq_t = sb("wq_t", [F + 1, F])
        resid = sb("resid", [F + 1, H, F])
        ew_t = sb("ew_t", [P, IT, L])
        out_w = sb("out_w", [P, KT, E])
        ln_g = sb("ln_g", [P, E])
        ln_b = sb("ln_b", [P, E])
        bv_all = sb("bv_all", [P, E])
        bo_all = sb("bo_all", [P, E])
        bq4 = sb("bq4", [P, KT])
        bk1 = sb("bk1", [P, KT])
        w_q = sb("w_q", [P, KT, E])
        w_k = sb("w_k", [P, KT, E])
        w_v = sb("w_v", [P, KT, E])
        w_o = sb("w_o", [P, KT, E])
        rel_k = sb("rel_k", [P, KT, NJ, AH])
        rel_v0 = sb("rel_v0", [P, AH, AD])
        rel_v1 = sb("rel_v1", [RJ - P, AH, AD])
        wg_hi = sb("wg_hi", [P, NE, KT, FI], F32R)
        wg_lo = sb("wg_lo", [P, NE, KT, FI], F32R)
        wu_hi = sb("wu_hi", [P, NE, KT, FI], F32R)
        wu_lo = sb("wu_lo", [P, NE, KT, FI], F32R)
        w_d = sb("w_d", [P, NE, FT, E])
        w_r = sb("w_r", [P, KT, NE])
        wr_hi = sb("wr_hi", [P, KT, NE], F32R)
        wr_lo = sb("wr_lo", [P, KT, NE], F32R)
        neg_temp = sb("neg_temp", [P, 1])

        x_in = sb("x_in", [F + 1, L, H])
        txt_idx = sb("txt_idx", [P, 1], I32)
        txt_row = sb("txt_row", [P, E])
        hid = sb("hid", [P, TT, E])
        q_st = sb("q_st", [KST + 2, AH, T], BF16)
        k_st = sb("k_st", [KST + 2, AH, T], BF16)
        v_one = sb("v_one", [P, TT, AH, VC])
        band_t = sb("band_t", [P, TT, WD_, AH])
        band_s = sb("band_s", [P, TT, WD_, AH])
        maxima = sb("maxima", [P, TT, AH])
        neg_max = sb("neg_max", [AH, 2, T], BF16)
        o_sb = sb("o_sb", [P, AH // GRP, T])
        res = sb("res", [P, TT, E])
        x2_hi = sb("x2_hi", [P, KT, T], F32R)
        x2_lo = sb("x2_lo", [P, KT, T], F32R)
        wgt = sb("wgt", [P, TT, NE])
        silu = sb("silu", [P, T])
        hT = sb("hT", [P, 3, T])
        stat = sb("stat", [P, TT, 6])
        mv = sb("mv", [P, TT, 2])
        rstd = sb("rstd", [P, TT])
        eps = sb("eps", [P, 1])
        neg_half = sb("neg_half", [P, 1])
        root_e = sb("root_e", [P, 1])
        one = sb("one", [P, 1])
        spare = sb("spare", [P, 2])

        Z = sb("scratch", [P, max(PTS * TT * T, 2 * NE * KT * FI)])

        def zone(start, *dims, rows=P):
            n = int(np.prod(dims))
            v = Z[0:rows, start:start + n]
            names = "abcd"[:len(dims)]
            if len(dims) > 1:
                v = v.rearrange(f"p ({' '.join(names)}) -> p {' '.join(names)}",
                                **{c: d for c, d in zip(names[1:], dims[1:])})
            return v

        p_t = zone(0, PTS, TT, TP)[:, :, :, PAD:PAD + T]
        ek, ekv = zone(0, IT, E), zone(512, IT, E)
        eq, dd, y_t = zone(1024, KT, L), zone(1536, KT, L), zone(2048, KT, L)
        xn = zone(2560, TT, E)
        xn_t = zone(3328, KT, T)
        qf, kf = zone(4096, KT, T), zone(4864, KT, T)
        qr, kr = zone(0, KT, T), zone(768, KT, T)
        rel_log = zone(5632, TT, RJ)
        parts = [Z[:, at:at + KT * T // 2].bitcast(BF16).rearrange("p (m t) -> p m t", m=KT)
                 for at in (1536, 1920, 6064, 6448, 6832, 7216)]
        rel_w = zone(0, TT, RJ)
        rwt0, rwt1 = zone(512, T), zone(896, T, rows=RJ - P)
        attn, attn_t = zone(1280, TT, E), zone(2048, KT, T)
        xn2 = zone(2816, TT, E)
        rden = zone(3584, TT, AH)
        rt = [zone(3700 + 32 * i, TT, NE) for i in range(14)]
        rsum = zone(4200, TT)
        rpair = zone(4300, TT, NE, NE)
        rpair2 = zone(4500, TT, NE, NE)

        emb_k_rows = zone(7640, NJ)
        emb_v_rows0, emb_v_rows1 = zone(7656, AD), zone(7672, AD)
        staged_w = [zone(0, NE, KT, FI), zone(NE * KT * FI, NE, KT, FI)]

        S = ps("S", [P, 8, 512])
        O, G, U = S[:, 3], S[:, 6], S[:, 7]
        D = S[:, 4:6]

        d_parts = nc.dram_tensor("d_parts", [6, E, T], BF16, kind="Internal").ap()
        d_neg = nc.dram_tensor("d_neg", [2, AH, T], BF16, kind="Internal").ap()
        d_band_t = nc.dram_tensor("d_band_t", [T * ROW], F32, kind="Internal").ap()
        d_band_s = nc.dram_tensor("d_band_s", [BAND], F32, kind="Internal").ap()
        d_band_w = nc.dram_tensor("d_band_w", [BAND], F32, kind="Internal").ap()

        def dram(t, offset, *dims):
            return bass.AP(tensor=t.tensor, offset=offset, ap=[list(d) for d in dims])

        loaded = [sem(f"loaded{g}") for g in range(3)]
        gu_loaded = [sem(f"gu_loaded{n}") for n in range(2)]
        wd_loaded, zeroed = sem("wd_loaded"), sem("zeroed")
        zero_ready, ones_ready, psum_clear = sem("zero_ready"), sem("ones_ready"), sem("psum_clear")
        mask_float, wb_masked, ew_exp = sem("mask_float"), sem("wb_masked"), sem("ew_exp")
        ew_turned, ew_ready, resid_ready = sem("ew_turned"), sem("ew_ready"), sem("resid_ready")
        temp_inverse, wr_high, consts = sem("temp_inverse"), sem("wr_high"), sem("consts")
        gu_high, gu_low, pool_consts = sem("gu_high"), sem("gu_low"), sem("pool_consts")
        x_loaded = sig("x_loaded", 1, 16)
        idx_loaded = sig("idx_loaded", 1, 16)
        txt_loaded = sig("txt_loaded", 1, 16)
        mix_pe = sig("mix_pe", 7)
        mix_act = sig("mix_act", 3)
        mix_dve = sig("mix_dve", 11)
        hid_ready = sig("hid_ready", 5)
        mix_root, ln2_root, ln3_root = sig("mix_root", 2), sig("ln2_root", 2), sig("ln3_root", 2)
        ln2 = sig("ln2", 3 * TT)
        xt_pe, xt_act = sig("xt_pe", 2), sig("xt_act", 2)
        proj_pe = sig("proj_pe", 10)
        proj_act = sig("proj_act", 7)
        v_done = sig("v_done", TT)
        split = sig("split", 8)
        parts_out = sig("parts_out", 6, 16)
        stacked = sig("stacked", 12, 16)
        rel_out = sig("rel_out", 7, 16)
        band_t_in, band_s_in = sig("band_t_in", 1, 16), sig("band_s_in", 4, 16)
        max_pe = sig("max_pe", AH)
        max_add = sig("max_add", 4 * AH)
        max_done = sig("max_done", AH)
        neg_pe, neg_act, neg_dve = sig("neg_pe", 1), sig("neg_act", 1), sig("neg_dve", 1)
        neg_out, neg_in = sig("neg_out", 1, 16), sig("neg_in", 1, 16)
        sc_pe = sig("sc_pe", AH)
        sc_add = sig("sc_add", 4 * AH)
        exp_done = sig("exp_done", AH)
        win_done = sig("win_done", WINS * AH // 2)
        pv_done = sig("pv_done", AH // GRP)
        o_copied = sig("o_copied", AH // GRP)
        win_out = sig("win_out", 4, 16)
        relw_in = sig("relw_in", 3, 16)
        rw_pe, rw_act = sig("rw_pe", 2), sig("rw_act", 2)
        ot_pe = sig("ot_pe", TT)
        or_pe = sig("or_pe", TT)
        att_dve = sig("att_dve", 3 * TT)
        att_mid = sig("att_mid", TT)
        at_pe, at_act = sig("at_pe", 2), sig("at_act", 2)
        wo_pe = sig("wo_pe", TT)
        hid_bo = sig("hid_bo", 1)
        res_ready = sig("res_ready", TT)
        ln3 = sig("ln3", 3 * TT)
        x2_pe, x2_hi_done, x2_lo_done = sig("x2_pe", 2), sig("x2_hi_done", 2), sig("x2_lo_done", 2)
        r_pe = sig("r_pe", 1)
        r_act = sig("r_act", 3)
        R_STEPS = 24
        r_dve = sig("r_dve", R_STEPS)
        gate_pe, up_pe = sig("gate_pe", NE * FT), sig("up_pe", NE * FT)
        silu_done = sig("silu_done", NE * FT)
        h_done = sig("h_done", NE * FT)
        down_pe = sig("down_pe", NE)
        acc_done = sig("acc_done", NE * TT)
        stored = sig("stored", 1, 16)

        units = [("u", 0), ("u", 1)]
        for e in range(NE):
            if e + 1 < NE:
                units += [("u", 2 * e + 2), ("d", e), ("u", 2 * e + 3)]
            else:
                units += [("d", e)]

        def schedule(attention, ffn):
            left = list(units) if ffn else []
            steps = []
            seen = {"u": 0, "d": 0}

            def fill(n):
                for _ in range(min(n, len(left))):
                    unit = left.pop(0)
                    seen[unit[0]] += 1
                    steps.append(("ffn",) + unit)

            if not attention:
                fill(len(left))
                return steps + [("store",)]
            for name, n in FILL_MIX:
                steps.append((name,))
                fill(n)
                if name == "mix_out" and not ffn:
                    steps.append(("prepare",))
            if not ffn:
                steps.append(("weights",))
            for h in range(AH):
                steps.append(("maxima", h, dict(seen)))
            if not ffn:
                steps.append(("weights_ready",))
            steps.append(("negate",))
            fill(FILL_NEGATE)
            for h in range(AH):
                steps.append(("attend", h, dict(seen)))
                if h % GRP == 0 and h:
                    steps.append(("values", h // GRP - 1, dict(seen)))
                if h % GRP == 1 and h > 1:
                    steps.append(("copy", h // GRP - 1))
            steps += [("values", AH // GRP - 1, dict(seen)), ("copy", AH // GRP - 1)]
            for name, n in FILL_OUT:
                if name == "residual":
                    fill(len(left))
                    if ffn:
                        steps.append(("store",))
                steps.append((name,))
                fill(n)
            return steps

        def rounds(engine, parts, setup=None):

            def do(step, b, f):
                part = parts.get(step[0])
                if part is not None:
                    part(f if step[0] in ("ffn", "store") else b, f, *step[1:])

            for s in schedule(True, False):
                do(s, 0, None)
            with engine.Fori(1, NB) as b:
                for s in schedule(True, True):
                    do(s, b, b - 1)
            for s in schedule(False, True):
                do(s, None, NB - 1)

        def later(b):
            return not isinstance(b, int)

        block = ctx.enter_context(nc.Block())

        @block.sync
        def _(sp):
            groups = [[
                (Z[:, 0:512].rearrange("p (i s) -> p i s", i=IT),
                 a["L0_tok_w_bias"].rearrange("(i p) s -> p i s", p=P)),
                (Z[:, 512:640].bitcast(U8).rearrange("p (i s) -> p i s", i=IT),
                 a["mask"].rearrange("(i p) s -> p i s", p=P)),
                (ident[:], a["ident"]),
                (wkv[0:F, 0:F], a["tok_wk_t"]), (wkv[0:F, F:2 * F], a["tok_wv_t"]),
                (wkv[F:F + 1, 0:F], a["L0_tok_Wk_b"].unsqueeze(0)),
                (wkv[F:F + 1, F:2 * F], a["L0_tok_Wv_b"].unsqueeze(0)),
                (wq_t[0:F, :], a["tok_wq_t"]), (wq_t[F:F + 1, :], a["L0_tok_Wq_b"].unsqueeze(0)),
            ], [
                (resid[F:F + 1, :, :], a["L0_tok_out_b"].rearrange("(o h c) -> o h c", o=1, h=H)),
                (out_w[:], a["L0_tok_out_w"].rearrange("(k p) n -> p k n", p=P)),
                (ln_g[:], a["L0_tok_ln_g"].partition_broadcast(P)),
                (ln_b[:], a["L0_tok_ln_b"].partition_broadcast(P)),
            ], [
                (head_of_row[:], a["head_of_row"]), (head_of_rel[:], a["head_of_rel"]),
                (earlier[:], a["earlier"]),
                (bq4[:], a["L0_attn_bq"].rearrange("(k p) -> p k", p=P)),
                (bk1[:], a["L0_attn_bk"].rearrange("(k p) -> p k", p=P)),
                (w_q[:], a["L0_attn_Wq"].rearrange("(k p) n -> p k n", p=P)),
                (w_k[:], a["L0_attn_Wk"].rearrange("(k p) n -> p k n", p=P)),
                (w_v[:], a["L0_attn_Wv"].rearrange("(k p) n -> p k n", p=P)),
                (w_o[:], a["L0_attn_Wo"].rearrange("(k p) n -> p k n", p=P)),
                (bv_all[:], a["L0_attn_bv"].partition_broadcast(P)),
                (bo_all[:], a["L0_attn_bo"].partition_broadcast(P)),
                (w_r[:], a["L0_ffn_Wr"].rearrange("(k p) n -> p k n", p=P)),
                (neg_temp[:], a["L0_ffn_temperature"].partition_broadcast(P)),
            ]]
            emb_v = a["L0_attn_emb_rel_v"]
            for r in range(P // AD):
                groups[2].append((emb_k_rows[AD * r:AD * (r + 1)],
                                  a["L0_attn_emb_rel_k"].rearrange("o j d -> d (o j)")))
            for j in range(NJ):
                rows = slice(AH * j, AH * (j + 1)) if j < P // AH else slice(0, AH)
                at = emb_v_rows0 if j < P // AH else emb_v_rows1
                groups[2].append((at[rows], dram(emb_v, j * AD, (0, AH), (1, AD))))

            def load(g):
                assert len(groups[g]) == N_LOADS[g]
                with nc.allow_non_contiguous_dma(reason="small bias and embedding columns, once"):
                    for dst, src in groups[g]:
                        sp.dma_start(dst, src).then_inc(loaded[g], 16)

            load(0)

            def mix_in(b, f):
                if later(b):
                    sp.wait_ge(mix_pe.sem, mix_pe.at(b - 1, 7))
                    sp.wait_ge(txt_loaded.sem, txt_loaded.at(b - 1, 1))
                sp.dma_start(x_in[0:F, :, :], a["x"][b]).then_inc(x_loaded.sem, 16)
                sp.dma_start(txt_idx[:], a["txt_t"][b]).then_inc(idx_loaded.sem, 16)
                if not later(b):
                    load(1)
                    load(2)
                    sp.wait_ge(zero_ready, 1)
                    zero = band_t[:].rearrange("p i w h -> p (i w h)")
                    n = TT * ROW
                    sp.dma_start(dram(d_band_t, 0, (n, P), (1, n)), zero).then_inc(zeroed, 16)
                    for d in (d_band_s, d_band_w):
                        for r0 in range(0, BAND, P * n):
                            rows = min(P, (BAND - r0) // n)
                            rest = min(BAND - r0 - rows * n, n) if rows < P else 0
                            sp.dma_start(dram(d, r0, (n, rows), (1, n)), zero[0:rows]).then_inc(zeroed, 16)
                            if rest:
                                sp.dma_start(dram(d, r0 + rows * n, (rest, 1), (1, rest)),
                                             zero[0:1, 0:rest]).then_inc(zeroed, 16)

            def prepare(b, f):
                sp.dma_start(w_d[:], a["L0_ffn_Wd"].rearrange("e (k p) n -> p e k n", p=P)
                             ).then_inc(wd_loaded, 16)

            def project_rest(b, f):
                if not later(b):
                    sp.wait_ge(zeroed, N_ZERO * 16)
                for n in range(6):
                    sp.wait_ge(split.sem, split.at(b, 4 * (n // 3) + (1, 3, 4)[n % 3]))
                    sp.dma_start(d_parts[n].rearrange("(m p) t -> p m t", p=P),
                                 parts[n]).then_inc(parts_out.sem, 16)
                sp.wait_ge(proj_act.sem, proj_act.at(b, 7))
                for c in range(P // BL):
                    sp.dma_start(
                        dram(d_band_t, c * BL * ROW, (ROW + AH, BL), (P * ROW, TT), (1, RJ)),
                        rel_log[c * BL:(c + 1) * BL]).then_inc(rel_out.sem, 16)
                for i in range(TT):
                    sp.dma_start(
                        dram(d_band_s, LEAD + (i * P) * (ROW + AH) - WIN * ROW + WIN * AH,
                             (ROW + AH, P), (ROW, NJ), (1, AH)),
                        rel_log[:, i].rearrange("p (j h) -> p j h", j=NJ)).then_inc(rel_out.sem, 16)
                sp.wait_ge(parts_out.sem, parts_out.at(b, 6))
                if later(b):
                    sp.wait_ge(sc_pe.sem, sc_pe.at(b - 1, AH))
                for st, base, order in ((q_st, 0, Q_PART), (k_st, 3, K_PART)):
                    for s in range(SLOTS):
                        sp.dma_start(
                            st[AD * s:AD * (s + 1)],
                            d_parts[base + order[s]].rearrange("(h d) t -> d h t", d=AD)
                        ).then_inc(stacked.sem, 16)
                sp.wait_ge(rel_out.sem, rel_out.at(b, 7))
                if later(b):
                    sp.wait_ge(win_out.sem, win_out.at(b - 1, 4))
                    sp.wait_ge(sc_add.sem, sc_add.at(b - 1, 4 * AH))
                sp.dma_start(band_t[:].rearrange("p i w h -> p i (w h)"),
                             dram(d_band_t, 0, (ROW, P), (P * ROW, TT), (1, ROW))
                             ).then_inc(band_t_in.sem, 16)
                for c in range(P // BL):
                    sp.dma_start(
                        band_s[c * BL:(c + 1) * BL].rearrange("p i w h -> p i (w h)"),
                        dram(d_band_s, LEAD + c * BPITCH, (ROW, BL), (P // BL * BPITCH, TT), (1, ROW))
                    ).then_inc(band_s_in.sem, 16)

            def weights(b, f):
                sp.wait_ge(proj_pe.sem, proj_pe.at(b, 10))
                sp.wait_ge(consts, N_CONSTS)
                for n, name in enumerate(("L0_ffn_Wg", "L0_ffn_Wu")):
                    sp.dma_start(staged_w[n], a[name].rearrange("e (k p) n -> p e k n", p=P)
                                 ).then_inc(gu_loaded[n], 16)

            def negate(b, f):
                sp.wait_ge(neg_act.sem, neg_act.at(b, 1))
                sp.wait_ge(neg_dve.sem, neg_dve.at(b, 1))
                sp.dma_start(d_neg.rearrange("i h t -> h i t"), neg_max[:]).then_inc(neg_out.sem, 16)
                sp.wait_ge(neg_out.sem, neg_out.at(b, 1))
                sp.dma_start(q_st[KST:KST + 2], d_neg).then_inc(neg_in.sem, 16)

            def windows_back(b, f):
                sp.wait_ge(win_done.sem, win_done.at(b, WINS * AH // 2))
                for c in range(P // BL):
                    sp.dma_start(
                        dram(d_band_w, LEAD + c * BPITCH, (ROW, BL), (P // BL * BPITCH, TT), (1, ROW)),
                        band_t[c * BL:(c + 1) * BL].rearrange("p i w h -> p i (w h)")
                    ).then_inc(win_out.sem, 16)
                sp.wait_ge(win_out.sem, win_out.at(b, 4))
                sp.wait_ge(pv_done.sem, pv_done.at(b, AH // GRP))
                for i in range(TT):
                    sp.dma_start(
                        rel_w[:, i].rearrange("p (j h) -> p j h", j=NJ),
                        dram(d_band_w, LEAD + (i * P) * (ROW + AH) - WIN * ROW + WIN * AH,
                             (ROW + AH, P), (ROW, NJ), (1, AH))).then_inc(relw_in.sem, 16)

            def store(f, _):
                sp.wait_ge(acc_done.sem, acc_done.at(f, NE * TT))
                sp.dma_start(out[f].rearrange("(i p) e -> p i e", p=P), res[:]).then_inc(stored.sem, 16)

            rounds(sp, {"mix_in": mix_in, "prepare": prepare, "project_rest": project_rest,
                        "weights": weights, "negate": negate, "turn_weights": windows_back,
                        "store": store})
            sp.wait_ge(stored.sem, stored.at(NB - 1, 1))

        @block.tensor
        def _(pe):
            def turn(dst, src, rows=P):
                return pe.transpose(dst, src, ident[0:rows, 0:rows])

            pe.wait_ge(loaded[0], 16 * N_LOADS[0])
            pe.wait_ge(ew_exp, 1)
            for si in range(IT):
                for ti in range(IT):
                    last = turn(S[:, si, ti * P:(ti + 1) * P],
                                Z[:, 1024 + ti * L + si * P:1024 + ti * L + (si + 1) * P])
                last.then_inc(ew_turned, 1)

            def mix_in(b, f):
                if later(b):
                    pe.wait_ge(r_act.sem, r_act.at(b - 1, 1))
                else:
                    pe.wait_ge(ones_ready, 1)
                    pe.wait_ge(ew_ready, 1)
                pe.wait_ge(x_loaded.sem, x_loaded.at(b, 1))
                for i in range(IT):
                    for h in range(H):
                        mm = pe.matmul(S[:, i, h * P:(h + 1) * P], x_in[:, i * P:(i + 1) * P, h],
                                       wkv[:], start=True, stop=True)
                    mm.then_inc(mix_pe.sem, 1)
                for h in range(H):
                    mm = pe.matmul(S[F * (h % 2):F * (h % 2) + F, 2, (h // 2) * L:(h // 2 + 1) * L],
                                   wq_t[:], x_in[:, :, h], start=True, stop=True)
                mm.then_inc(mix_pe.sem, 1)

            def mix_sums(b, f):
                if not later(b):
                    pe.wait_ge(psum_clear, 1)
                pe.wait_ge(mix_act.sem, mix_act.at(b, 2))
                for m in range(KT):
                    for i in range(IT):
                        mm = pe.matmul(O[:, m * L:(m + 1) * L], ek[:, i, m * P:(m + 1) * P],
                                       ew_t[:, i, :], start=(i == 0), stop=(i == IT - 1))
                mm.then_inc(mix_pe.sem, 1)
                pe.wait_ge(mix_dve.sem, mix_dve.at(b, 2))
                for m in range(KT):
                    for i in range(IT):
                        mm = pe.matmul(S[:, 0, m * L:(m + 1) * L], ekv[:, i, m * P:(m + 1) * P],
                                       ew_t[:, i, :], start=(i == 0), stop=(i == IT - 1))
                mm.then_inc(mix_pe.sem, 1)

            def mix_out(b, f):
                if not later(b):
                    pe.wait_ge(loaded[1], 16 * N_LOADS[1])
                    pe.wait_ge(resid_ready, H)
                pe.wait_ge(mix_dve.sem, mix_dve.at(b, 5))
                for i in range(IT):
                    for k in range(KT):
                        pe.matmul(S[:, 1, i * E:(i + 1) * E], y_t[:, k, i * P:(i + 1) * P], out_w[:, k, :],
                                  start=(k == 0), stop=False, skip_group_check=True)
                    for h in range(H):
                        mm = pe.matmul(S[:, 1, i * E + h * F:i * E + (h + 1) * F],
                                       x_in[:, i * P:(i + 1) * P, h], resid[:, h, :],
                                       start=False, stop=(h == H - 1), skip_group_check=True)
                    mm.then_inc(mix_pe.sem, 1)

            def turned(src, ready, steps, done, b):
                pe.wait_ge(ready.sem, ready.at(b, steps))
                for k in range(KT):
                    for i in range(TT):
                        last = turn(S[:, k, i * P:(i + 1) * P], src[:, i, k * P:(k + 1) * P])
                    last.then_inc(done.sem, 1)

            def turn_norm(b, f):
                turned(xn, ln2, 3 * TT, xt_pe, b)

            banks = [S[:, 2], S[:, 0], S[:, 1], O]

            def project_qk(b, f):
                if not later(b):
                    pe.wait_ge(loaded[2], 16 * N_LOADS[2])
                    pe.wait_ge(consts, N_CONSTS)
                pe.wait_ge(xt_act.sem, xt_act.at(b, 2))
                for n, (w, m) in enumerate([(w_q, 0), (w_q, 1), (w_k, 0), (w_k, 1)]):
                    for k in range(KT):
                        mm = pe.matmul(banks[n][:, 0:T], w[:, k, m * P:(m + 1) * P], xn_t[:, k, :],
                                       start=(k == 0), stop=(k == KT - 1))
                    mm.then_inc(proj_pe.sem, 1)

            def project_rest(b, f):
                for i in range(TT):
                    pe.wait_ge(proj_act.sem, proj_act.at(b, i + 1))
                    for k in range(KT):
                        mm = pe.matmul(banks[i][:, 0:E], xn_t[:, k, i * P:(i + 1) * P], w_v[:, k, :],
                                       start=(k == 0), stop=(k == KT - 1))
                    mm.then_inc(proj_pe.sem, 1)
                pe.wait_ge(proj_act.sem, proj_act.at(b, 4))
                for i in range(TT):
                    if i:
                        pe.wait_ge(v_done.sem, v_done.at(b, i))
                    for m in range(KT):
                        mm = pe.matmul(banks[(3 + i) % 4][:, 0:RJ], qf[:, m, i * P:(i + 1) * P],
                                       rel_k[:, m].rearrange("p j h -> p (j h)"),
                                       start=(m == 0), stop=(m == KT - 1))
                    mm.then_inc(proj_pe.sem, 1)

            def score_set(h):
                return S[:, 3 * (h % 2):3 * (h % 2) + 3]

            def maxima_head(b, f, h, seen):
                if h == 0:
                    pe.wait_ge(stacked.sem, stacked.at(b, 12))
                    pe.wait_ge(v_done.sem, v_done.at(b, TT))
                    pe.wait_ge(proj_act.sem, proj_act.at(b, 7))
                if h == 1 and seen["d"]:
                    pe.wait_ge(acc_done.sem, acc_done.at(f, TT * seen["d"]))
                if h >= 2:
                    pe.wait_ge(max_done.sem, max_done.at(b, h - 1))
                for i in range(TT):
                    mm = pe.matmul(score_set(h)[:, i, PAD:PAD + T], q_st[0:KST, h, i * P:(i + 1) * P],
                                   k_st[0:KST, h, :], start=True, stop=True)
                mm.then_inc(max_pe.sem, 1)

            def weights_ready(b, f):
                pe.wait_ge(wd_loaded, 16)
                pe.wait_ge(gu_high, 2)
                pe.wait_ge(gu_low, 2)

            def negate(b, f):
                pe.wait_ge(max_done.sem, max_done.at(b, AH))
                for i in range(TT):
                    last = turn(O[0:AH, i * P:(i + 1) * P], maxima[:, i, :])
                last.then_inc(neg_pe.sem, 1)

            def attend(b, f, h, seen):
                if h == 0:
                    pe.wait_ge(neg_in.sem, neg_in.at(b, 1))
                if h == 1 and seen["d"]:
                    pe.wait_ge(acc_done.sem, acc_done.at(f, TT * seen["d"]))
                if h >= 2:
                    pe.wait_ge(exp_done.sem, exp_done.at(b, h - 1))
                for i in range(TT):
                    mm = pe.matmul(score_set(h)[:, i, PAD:PAD + T], k_st[:, h, i * P:(i + 1) * P],
                                   q_st[:, h, :], start=True, stop=True)
                mm.then_inc(sc_pe.sem, 1)

            def values(b, f, g, seen):
                pe.wait_ge(exp_done.sem, exp_done.at(b, GRP * (g + 1)))
                if g >= 2:
                    pe.wait_ge(o_copied.sem, o_copied.at(b, g - 1))
                elif seen["u"]:
                    pe.wait_ge(h_done.sem, h_done.at(f, seen["u"]))
                for i in range(TT):
                    for l in range(GRP):
                        h = GRP * g + l
                        mm = pe.matmul(S[32 * l:32 * l + VC, 6 + g % 2, 0:T], v_one[:, i, h, :],
                                       p_t[:, h % PTS, i, :], start=(i == 0), stop=(i == TT - 1),
                                       skip_group_check=True)
                mm.then_inc(pv_done.sem, 1)

            def turn_weights(b, f):
                pe.wait_ge(relw_in.sem, relw_in.at(b, TT))
                for i in range(TT):
                    last = turn(O[:, i * P:(i + 1) * P], rel_w[:, i, 0:P])
                last.then_inc(rw_pe.sem, 1)
                for i in range(TT):
                    last = turn(S[0:RJ - P, 0, i * P:(i + 1) * P], rel_w[:, i, P:RJ])
                last.then_inc(rw_pe.sem, 1)

            def turn_outputs(b, f):
                pe.wait_ge(o_copied.sem, o_copied.at(b, AH // GRP))
                for i in (1, 2):
                    for g in range(AH // GRP):
                        last = turn(S[:, i, g * P:(g + 1) * P], o_sb[:, g, i * P:(i + 1) * P])
                    last.then_inc(ot_pe.sem, 1)

            def rel_values(b, f):
                pe.wait_ge(rw_act.sem, rw_act.at(b, 2))
                for g in range(AH // GRP):
                    last = turn(S[:, 0, g * P:(g + 1) * P], o_sb[:, g, 0:P])
                last.then_inc(ot_pe.sem, 1)
                for n, i in enumerate((1, 2, 0)):
                    if n:
                        pe.wait_ge(att_dve.sem, att_dve.at(b, 3 * (n - 1) + 1))
                    pe.matmul(O[:, 0:E], rwt0[:, i * P:(i + 1) * P],
                              rel_v0[:].rearrange("p h d -> p (h d)"), start=True, stop=False)
                    pe.matmul(O[:, 0:E], rwt1[:, i * P:(i + 1) * P],
                              rel_v1[:].rearrange("p h d -> p (h d)"), start=False, stop=True
                              ).then_inc(or_pe.sem, 1)

            def turn_attn(b, f):
                turned(attn, att_dve, 3 * TT, at_pe, b)

            def residual(b, f):
                pe.wait_ge(at_act.sem, at_act.at(b, 2))
                for i in range(TT):
                    dst = S[:, 2, i * E:(i + 1) * E] if i < 2 else O[:, 0:E]
                    for k in range(KT):
                        mm = pe.matmul(dst, attn_t[:, k, i * P:(i + 1) * P], w_o[:, k, :],
                                       start=(k == 0), stop=(k == KT - 1))
                    mm.then_inc(wo_pe.sem, 1)

            def turn_x2(b, f):
                turned(xn2, ln3, 3 * TT, x2_pe, b)

            def router(b, f):
                pe.wait_ge(x2_hi_done.sem, x2_hi_done.at(b, 2))
                pe.wait_ge(x2_lo_done.sem, x2_lo_done.at(b, 2))
                for i in range(TT):
                    n = 0
                    for xs, ws in ((x2_hi, wr_hi), (x2_hi, wr_lo), (x2_lo, wr_hi)):
                        for k in range(KT):
                            mm = pe.matmul(S[:, 2, i * NE:(i + 1) * NE], xs[:, k, i * P:(i + 1) * P],
                                           ws[:, k, :], start=(n == 0), stop=(n == 3 * KT - 1))
                            n += 1
                mm.then_inc(r_pe.sem, 1)

            def gate_up(f, n):
                e, m = n // FT, n % FT
                for dst, hi, lo, done, free in ((G, wg_hi, wg_lo, gate_pe, silu_done),
                                                (U, wu_hi, wu_lo, up_pe, h_done)):
                    if n:
                        pe.wait_ge(free.sem, free.at(f, n))
                    j = 0
                    for ws, xs in ((hi, x2_hi), (hi, x2_lo), (lo, x2_hi)):
                        for k in range(KT):
                            mm = pe.matmul(dst[:, 0:T], ws[:, e, k, m * P:(m + 1) * P], xs[:, k, :],
                                           start=(j == 0), stop=(j == 3 * KT - 1))
                            j += 1
                    mm.then_inc(done.sem, 1)

            def down(f, e):
                pe.wait_ge(h_done.sem, h_done.at(f, FT * (e + 1)))
                if e:
                    pe.wait_ge(acc_done.sem, acc_done.at(f, TT * e))
                for i in range(TT):
                    for m in range(FT):
                        mm = pe.matmul(D[:, i // 2, (i % 2) * E:(i % 2 + 1) * E],
                                       hT[:, (FT * e + m) % 3, i * P:(i + 1) * P], w_d[:, e, m, :],
                                       start=(m == 0), stop=(m == FT - 1))
                mm.then_inc(down_pe.sem, 1)

            def ffn(f, _, kind, n):
                if kind == "u":
                    gate_up(f, n)
                else:
                    down(f, n)

            rounds(pe, {"mix_in": mix_in, "mix_sums": mix_sums, "mix_out": mix_out,
                        "turn_norm": turn_norm, "project_qk": project_qk, "project_rest": project_rest,
                        "maxima": maxima_head, "weights_ready": weights_ready, "negate": negate,
                        "attend": attend, "values": values, "turn_weights": turn_weights,
                        "turn_outputs": turn_outputs, "rel_values": rel_values, "turn_attn": turn_attn,
                        "residual": residual, "turn_x2": turn_x2, "router": router, "ffn": ffn})

        @block.scalar
        def _(act):
            act.wait_ge(wb_masked, 1)
            nc.scalar.activation(zone(1024, IT, L), zone(0, IT, L), ACT.Exp).then_inc(ew_exp, 1)
            act.wait_ge(ew_turned, IT)
            nc.scalar.activation(ew_t[:], S[:, 0:IT, 0:L], ACT.Copy).then_inc(ew_ready, 1)

            def mix_in(b, f):
                for i in range(IT):
                    act.wait_ge(mix_pe.sem, mix_pe.at(b, i + 1))
                    nc.scalar.activation(ek[:, i].rearrange("p (h d) -> p h d", h=H),
                                         S[:, i].rearrange("p (h c) -> p h c", h=H)[:, :, 0:F],
                                         ACT.Exp).then_inc(mix_act.sem, 1)
                act.wait_ge(mix_pe.sem, mix_pe.at(b, 3))
                nc.scalar.activation(eq, S[:, 2].rearrange("p (m t) -> p m t", m=KT), ACT.Exp,
                                     scale=-1.0).then_inc(mix_act.sem, 1)

            def prepare(b, f):
                act.wait_ge(loaded[2], 16 * N_LOADS[2])
                nc.scalar.activation(bq4[:], bq4[:], ACT.Copy, scale=AD ** -0.5).then_inc(consts, 1)
                nc.scalar.activation(wr_hi[:], w_r[:], ACT.Copy).then_inc(wr_high, 1)

            def turn_norm(b, f):
                if not later(b):
                    act.wait_ge(consts, N_CONSTS)
                for k in range(KT):
                    act.wait_ge(xt_pe.sem, xt_pe.at(b, k + 1))
                    nc.scalar.activation(xn_t[:, k], S[:, k, 0:T], ACT.Copy).then_inc(xt_act.sem, 1)

            banks = [S[:, 2], S[:, 0], S[:, 1], O]

            def project_qk(b, f):
                for n in range(4):
                    act.wait_ge(proj_pe.sem, proj_pe.at(b, n + 1))
                    dst, bias, scale = (qf, bq4, AD ** -0.5) if n < 2 else (kf, bk1, 1.0)
                    nc.scalar.activation(dst[:, n % 2], banks[n][:, 0:T], ACT.Identity,
                                         bias=bias[:, n % 2:n % 2 + 1], scale=scale
                                         ).then_inc(proj_act.sem, 1)

            def project_rest(b, f):
                for i in range(TT):
                    act.wait_ge(proj_pe.sem, proj_pe.at(b, 8 + i))
                    nc.scalar.activation(rel_log[:, i], banks[(3 + i) % 4][:, 0:RJ], ACT.Copy
                                         ).then_inc(proj_act.sem, 1)

            def weights(b, f):
                for n, hi in enumerate((wg_hi, wu_hi)):
                    act.wait_ge(gu_loaded[n], 16)
                    nc.scalar.activation(hi[:], staged_w[n], ACT.Copy).then_inc(gu_high, 1)

            def negate(b, f):
                act.wait_ge(neg_pe.sem, neg_pe.at(b, 1))
                nc.scalar.activation(neg_max[:, 0], O[0:AH, 0:T], ACT.Copy, scale=-1.0
                                     ).then_inc(neg_act.sem, 1)

            def attend(b, f, h, seen):
                if h == 0 and not later(b):
                    act.wait_ge(gu_low, 2)
                act.wait_ge(sc_add.sem, sc_add.at(b, 4 * (h + 1)))
                if h >= PTS:
                    act.wait_ge(pv_done.sem, pv_done.at(b, (h - PTS) // GRP + 1))
                    act.wait_ge(win_done.sem, win_done.at(b, WINS * ((h - PTS) // 2 + 1)))
                c0 = 3 * (h % 2)
                nc.scalar.activation(p_t[:, h % PTS], S[:, c0:c0 + 3, PAD:PAD + T], ACT.Exp
                                     ).then_inc(exp_done.sem, 1)

            def copy(b, f, g):
                act.wait_ge(pv_done.sem, pv_done.at(b, g + 1))
                nc.scalar.activation(o_sb[:, g], S[:, 6 + g % 2, 0:T], ACT.Copy).then_inc(o_copied.sem, 1)

            def turn_weights(b, f):
                act.wait_ge(rw_pe.sem, rw_pe.at(b, 1))
                nc.scalar.activation(rwt0, O[:, 0:T], ACT.Copy).then_inc(rw_act.sem, 1)
                act.wait_ge(rw_pe.sem, rw_pe.at(b, 2))
                nc.scalar.activation(rwt1, S[0:RJ - P, 0, 0:T], ACT.Copy).then_inc(rw_act.sem, 1)

            def turn_attn(b, f):
                for k in range(KT):
                    act.wait_ge(at_pe.sem, at_pe.at(b, k + 1))
                    nc.scalar.activation(attn_t[:, k], S[:, k, 0:T], ACT.Copy).then_inc(at_act.sem, 1)

            def turn_x2(b, f):
                if later(b):
                    act.wait_ge(down_pe.sem, down_pe.at(b - 1, NE))
                for k in range(KT):
                    act.wait_ge(x2_pe.sem, x2_pe.at(b, k + 1))
                    nc.scalar.activation(x2_hi[:, k], S[:, k, 0:T], ACT.Copy).then_inc(x2_hi_done.sem, 1)

            def router(b, f):
                act.wait_ge(r_pe.sem, r_pe.at(b, 1))
                nc.scalar.activation(rt[0], S[:, 2, 0:TT * NE].rearrange("p (i e) -> p i e", i=TT),
                                     ACT.Exp, scale=neg_temp[:]).then_inc(r_act.sem, 1)
                act.wait_ge(r_dve.sem, r_dve.at(b, R_DIST))
                nc.scalar.activation(rt[4], rt[3], ACT.Exp, scale=-1.0 / 0.1).then_inc(r_act.sem, 1)
                nc.scalar.activation(rt[5], rt[3], ACT.Exp, scale=-1.0 / 0.3).then_inc(r_act.sem, 1)

            def ffn(f, _, kind, n):
                if kind == "u":
                    act.wait_ge(gate_pe.sem, gate_pe.at(f, n + 1))
                    if n:
                        act.wait_ge(h_done.sem, h_done.at(f, n))
                    nc.scalar.activation(silu[:], G[:, 0:T], ACT.Silu).then_inc(silu_done.sem, 1)

            rounds(act, {"mix_in": mix_in, "prepare": prepare, "turn_norm": turn_norm,
                         "project_qk": project_qk, "project_rest": project_rest, "weights": weights,
                         "negate": negate, "attend": attend, "copy": copy, "turn_weights": turn_weights,
                         "turn_attn": turn_attn, "turn_x2": turn_x2, "router": router, "ffn": ffn})

        @block.vector
        def _(dve):
            dve.memset(band_t[:], 0.0).then_inc(zero_ready, 1)
            dve.memset(x_in[F:F + 1], 1.0).then_inc(ones_ready, 1)
            dve.wait_ge(loaded[0], 16 * N_LOADS[0])
            dve.tensor_copy(zone(1024, IT, L), Z[:, 512:640].bitcast(U8).rearrange("p (i s) -> p i s", i=IT)
                            ).then_inc(mask_float, 1)
            dve.wait_ge(mask_float, 1)
            dve.tensor_tensor(zone(0, IT, L), zone(0, IT, L), zone(1024, IT, L), ALU.mult
                              ).then_inc(wb_masked, 1)
            for h in range(H):
                dve.tensor_copy(resid[0:F, h], ident[0:F, 0:F]).then_inc(resid_ready, 1)
            dve.memset(S[:, 3:8], 0.0).then_inc(psum_clear, 1)
            dve.wait_ge(psum_clear, 1)

            def stats(b, sg, k, src, tiles):
                for i in range(tiles):
                    dve.bn_stats(stat[:, i], src(i)).then_inc(sg.sem, 1)
                dve.wait_ge(sg.sem, sg.at(b, k + tiles))
                dve.memset(spare[:, 0:1], 0.0)
                for i in range(tiles):
                    dve.bn_aggr(mv[:, i], stat[:, i]).then_inc(sg.sem, 1)

            def norm(b, sg, rooted, src, dst, tiles):
                dve.wait_ge(rooted.sem, rooted.at(b, 2))
                for i in range(tiles):
                    dve.tensor_scalar(dst(i), src(i), mv[:, i, 0:1], rstd[:, i:i + 1], ALU.subtract,
                                      ALU.mult).then_inc(sg.sem, 1)

            def mix_in(b, f):
                for i in range(IT):
                    dve.wait_ge(mix_act.sem, mix_act.at(b, i + 1))
                    dve.tensor_tensor(ekv[:, i].rearrange("p (h d) -> p h d", h=H),
                                      ek[:, i].rearrange("p (h d) -> p h d", h=H),
                                      S[:, i].rearrange("p (h c) -> p h c", h=H)[:, :, F:2 * F],
                                      ALU.mult).then_inc(mix_dve.sem, 1)

            def mix_sums(b, f):
                dve.wait_ge(mix_act.sem, mix_act.at(b, 3))
                dve.wait_ge(mix_pe.sem, mix_pe.at(b, 4))
                dve.scalar_tensor_tensor(dd.rearrange("p m t -> p (m t)"), eq.rearrange("p m t -> p (m t)"),
                                         1.0, O[:, 0:KT * L], ALU.add, ALU.mult).then_inc(mix_dve.sem, 1)
                dve.wait_ge(mix_dve.sem, mix_dve.at(b, 3))
                dve.reciprocal(dd, dd).then_inc(mix_dve.sem, 1)
                dve.wait_ge(mix_pe.sem, mix_pe.at(b, 5))
                dve.wait_ge(mix_dve.sem, mix_dve.at(b, 4))
                dve.tensor_tensor(y_t.rearrange("p m t -> p (m t)"), S[:, 0, 0:KT * L],
                                  dd.rearrange("p m t -> p (m t)"), ALU.mult).then_inc(mix_dve.sem, 1)

            def mixed(i):
                return S[:, 1, i * E:(i + 1) * E]

            def mix_out(b, f):
                dve.wait_ge(mix_pe.sem, mix_pe.at(b, 7))
                stats(b, mix_dve, 5, mixed, IT)

            def mix_norm(b, f):
                norm(b, mix_dve, mix_root, mixed, lambda i: hid[:, i], IT)

            def prepare(b, f):
                dve.wait_ge(loaded[2], 16 * N_LOADS[2])
                for m in range(KT):
                    dve.tensor_tensor(rel_k[:, m], emb_k_rows.unsqueeze(2).broadcast_to([P, NJ, AH]),
                                      head_of_row[:, m].unsqueeze(1).broadcast_to([P, NJ, AH]), ALU.mult
                                      ).then_inc(consts, 1)
                for dst, rows, n in ((rel_v0, emb_v_rows0, P), (rel_v1, emb_v_rows1, RJ - P)):
                    dve.tensor_tensor(dst[:], rows[0:n].unsqueeze(1).broadcast_to([n, AH, AD]),
                                      head_of_rel[0:n].unsqueeze(2).broadcast_to([n, AH, AD]), ALU.mult
                                      ).then_inc(consts, 1)
                dve.reciprocal(neg_temp[:], neg_temp[:]).then_inc(temp_inverse, 1)
                dve.wait_ge(temp_inverse, 1)
                dve.tensor_scalar(neg_temp[:], neg_temp[:], -1.0, None, ALU.mult).then_inc(consts, 1)
                dve.wait_ge(wr_high, 1)
                dve.tensor_tensor(wr_lo[:], w_r[:], wr_hi[:].bitcast(F32), ALU.subtract
                                  ).then_inc(consts, 1)

            def norm_stats(b, f):
                dve.wait_ge(hid_ready.sem, hid_ready.at(b, 5))
                stats(b, ln2, 0, lambda i: hid[:, i], TT)

            def turn_norm(b, f):
                norm(b, ln2, ln2_root, lambda i: hid[:, i], lambda i: xn[:, i], TT)

            banks = [S[:, 2], S[:, 0], S[:, 1]]

            def project_rest(b, f):
                for n, (src, rest, p3) in enumerate(((qf, qr, parts[0:3]), (kf, kr, parts[3:6]))):
                    k = 4 * n
                    dve.wait_ge(proj_act.sem, proj_act.at(b, 2 + 2 * n))
                    dve.tensor_copy(p3[0], src).then_inc(split.sem, 1)
                    dve.wait_ge(split.sem, split.at(b, k + 1))
                    dve.tensor_tensor(rest, src, p3[0], ALU.subtract).then_inc(split.sem, 1)
                    dve.wait_ge(split.sem, split.at(b, k + 2))
                    dve.tensor_copy(p3[1], rest).then_inc(split.sem, 1)
                    dve.wait_ge(split.sem, split.at(b, k + 3))
                    dve.tensor_tensor(p3[2], rest, p3[1], ALU.subtract).then_inc(split.sem, 1)
                    if n == 0:
                        for i in range(TT):
                            dve.wait_ge(proj_pe.sem, proj_pe.at(b, 5 + i))
                            dve.tensor_tensor(v_one[:, i, :, 0:AD],
                                              banks[i][:, 0:E].rearrange("p (h d) -> p h d", h=AH),
                                              bv_all[:].rearrange("p (h d) -> p h d", h=AH), ALU.add
                                              ).then_inc(v_done.sem, 1)

            def add_band(h, band, done):
                for c in range(P // BL):
                    rows = slice(c * BL, (c + 1) * BL)
                    win = bass.AP(tensor=S, offset=S[rows].offset + 3 * (h % 2) * 512 + PAD + c * BL - WIN,
                                  ap=[[S[rows].ap[0][0], BL], [512 + P, TT], [1, WD_]])
                    dve.tensor_tensor(win, win, band[rows, :, :, h], ALU.add).then_inc(done.sem, 1)

            def maxima_head(b, f, h, seen):
                if h == 0:
                    dve.wait_ge(band_t_in.sem, band_t_in.at(b, 1))
                dve.wait_ge(max_pe.sem, max_pe.at(b, h + 1))
                add_band(h, band_t, max_add)
                dve.wait_ge(max_add.sem, max_add.at(b, 4 * (h + 1)))
                c0 = 3 * (h % 2)
                dve.tensor_reduce(maxima[:, :, h], S[:, c0:c0 + 3, PAD:PAD + T], AX, ALU.max
                                  ).then_inc(max_done.sem, 1)

            def negate(b, f):
                dve.wait_ge(neg_act.sem, neg_act.at(b, 1))
                dve.scalar_tensor_tensor(neg_max[:, 1], O[0:AH, 0:T], -1.0, neg_max[:, 0], ALU.mult,
                                         ALU.subtract).then_inc(neg_dve.sem, 1)

            def attend(b, f, h, seen):
                if h == 0:
                    dve.wait_ge(band_s_in.sem, band_s_in.at(b, 4))
                dve.wait_ge(sc_pe.sem, sc_pe.at(b, h + 1))
                add_band(h, band_s, sc_add)

            def rel_values(b, f):
                for n, i in enumerate((1, 2, 0)):
                    dve.wait_ge(or_pe.sem, or_pe.at(b, n + 1))
                    dve.wait_ge(ot_pe.sem, ot_pe.at(b, n + 1))
                    heads = S[:, i].rearrange("p (h d) -> p h d", h=AH)
                    dve.tensor_copy(attn[:, i], O[:, 0:E]).then_inc(att_dve.sem, 1)
                    dve.reciprocal(rden[:, i], heads[:, :, AD]).then_inc(att_dve.sem, 1)
                    dve.wait_ge(att_dve.sem, att_dve.at(b, 3 * n + 2))
                    av = attn[:, i].rearrange("p (h d) -> p h d", h=AH)
                    dve.tensor_tensor(av, av, heads[:, :, 0:AD], ALU.add).then_inc(att_mid.sem, 1)
                    dve.wait_ge(att_mid.sem, att_mid.at(b, n + 1))
                    dve.tensor_tensor(av, av, rden[:, i].unsqueeze(2).broadcast_to([P, AH, AD]), ALU.mult
                                      ).then_inc(att_dve.sem, 1)

            def residual(b, f):
                if later(b):
                    dve.wait_ge(stored.sem, stored.at(b - 1, 1))
                dve.wait_ge(hid_bo.sem, hid_bo.at(b, 1))
                for i in range(TT):
                    dve.wait_ge(wo_pe.sem, wo_pe.at(b, max(i + 1, 2)))
                    src = S[:, 2, i * E:(i + 1) * E] if i < 2 else O[:, 0:E]
                    dve.tensor_tensor(res[:, i], src, hid[:, i], ALU.add).then_inc(res_ready.sem, 1)
                dve.wait_ge(res_ready.sem, res_ready.at(b, TT))
                stats(b, ln3, 0, lambda i: res[:, i], TT)

            def turn_x2(b, f):
                norm(b, ln3, ln3_root, lambda i: res[:, i], lambda i: xn2[:, i], TT)
                for k in range(KT):
                    dve.wait_ge(x2_hi_done.sem, x2_hi_done.at(b, k + 1))
                    dve.tensor_tensor(x2_lo[:, k], S[:, k, 0:T], x2_hi[:, k].bitcast(F32), ALU.subtract
                                      ).then_inc(x2_lo_done.sem, 1)

            def router(b, f):
                k = [0]

                def step(ins):
                    k[0] += 1
                    ins.then_inc(r_dve.sem, 1)
                    dve.wait_ge(r_dve.sem, r_dve.at(b, k[0]))

                def each(x):
                    return x.unsqueeze(2).broadcast_to([P, TT, NE])

                ex, inh, zone_, dist, w, fb, rank, fbw = rt[0:8]
                dve.wait_ge(r_act.sem, r_act.at(b, 1))
                step(dve.tensor_scalar(inh, ex, 1.0, None, ALU.add))
                step(dve.reciprocal(inh, inh))
                step(dve.tensor_scalar(dist, inh, CENTER, None, ALU.subtract))
                step(dve.scalar_tensor_tensor(dist, dist, -1.0, dist, ALU.mult, ALU.max))
                assert k[0] == R_DIST
                step(dve.tensor_scalar(zone_, inh, ZONE_HI, None, ALU.is_le))
                step(dve.scalar_tensor_tensor(zone_, inh, ZONE_LO, zone_, ALU.is_ge, ALU.mult))
                dve.wait_ge(r_act.sem, r_act.at(b, 3))
                step(dve.tensor_tensor(w, w, zone_, ALU.mult))
                step(dve.tensor_reduce(rsum, w, AX, ALU.add))
                step(dve.tensor_scalar(rsum, rsum, 1e-8, None, ALU.is_lt))
                other = fb.unsqueeze(2).broadcast_to([P, TT, NE, NE])
                own = fb.unsqueeze(3).broadcast_to([P, TT, NE, NE])
                low = earlier[:].unsqueeze(1).broadcast_to([P, TT, NE, NE])
                step(dve.tensor_tensor(rpair, other, own, ALU.is_equal))
                step(dve.tensor_tensor(rpair, rpair, low, ALU.mult))
                step(dve.tensor_tensor(rpair2, other, own, ALU.is_gt))
                step(dve.tensor_tensor(rpair, rpair, rpair2, ALU.add))
                step(dve.tensor_reduce(rank, rpair, AX, ALU.add))
                step(dve.scalar_tensor_tensor(fbw, rank, 2.0, fb, ALU.is_lt, ALU.mult))
                step(dve.tensor_reduce(rt[8][:, :, 0], fbw, AX, ALU.add))
                step(dve.tensor_scalar(rt[8][:, :, 0], rt[8][:, :, 0], 1e-8, None, ALU.max))
                step(dve.reciprocal(rt[8][:, :, 0], rt[8][:, :, 0]))
                step(dve.tensor_tensor(fbw, fbw, each(rt[8][:, :, 0]), ALU.mult))
                dve.memset(spare[:, 0:1], 0.0)
                step(dve.copy_predicated(w, each(rsum.bitcast(I32)), fbw))
                step(dve.tensor_reduce(rt[8][:, :, 1], w, AX, ALU.add))
                step(dve.tensor_scalar(rt[8][:, :, 1], rt[8][:, :, 1], 1e-8, None, ALU.max))
                step(dve.reciprocal(rt[8][:, :, 1], rt[8][:, :, 1]))
                step(dve.tensor_tensor(wgt[:], w, each(rt[8][:, :, 1]), ALU.mult))
                assert k[0] == R_STEPS

            def hidden(f, n):
                dve.wait_ge(silu_done.sem, silu_done.at(f, n + 1))
                dve.wait_ge(up_pe.sem, up_pe.at(f, n + 1))
                if n >= 3:
                    dve.wait_ge(down_pe.sem, down_pe.at(f, (n - 3) // FT + 1))
                dve.tensor_tensor(hT[:, n % 3], silu[:], U[:, 0:T], ALU.mult).then_inc(h_done.sem, 1)

            def accumulate(f, e):
                dve.wait_ge(down_pe.sem, down_pe.at(f, e + 1))
                if e:
                    dve.wait_ge(acc_done.sem, acc_done.at(f, TT * e))
                for i in range(TT):
                    dve.scalar_tensor_tensor(res[:, i], D[:, i // 2, (i % 2) * E:(i % 2 + 1) * E],
                                             wgt[:, i, e:e + 1], res[:, i], ALU.mult, ALU.add
                                             ).then_inc(acc_done.sem, 1)

            def ffn(f, _, kind, n):
                if kind == "u":
                    hidden(f, n)
                else:
                    accumulate(f, n)

            rounds(dve, {"mix_in": mix_in, "mix_sums": mix_sums, "mix_out": mix_out, "mix_norm": mix_norm,
                         "prepare": prepare, "norm_stats": norm_stats, "turn_norm": turn_norm,
                         "project_rest": project_rest, "maxima": maxima_head, "negate": negate,
                         "attend": attend, "rel_values": rel_values, "residual": residual,
                         "turn_x2": turn_x2, "router": router, "ffn": ffn})

        @block.gpsimd
        def _(pool):
            for n, (dst, value) in enumerate(((one, 1.0), (eps, EPS), (neg_half, -0.5),
                                              (root_e, float(E) ** 0.5))):
                nc.gpsimd.memset(dst[:], value).then_inc(pool_consts, 1)
            nc.gpsimd.memset(v_one[:], 1.0).then_inc(pool_consts, 1)
            pool.wait_ge(pool_consts, 5)
            nc.gpsimd.memset(k_st[KST:KST + 2], 1.0).then_inc(pool_consts, 1)
            pool.wait_ge(pool_consts, 6)

            def root(b, stats, steps, done, tiles):
                pool.wait_ge(stats.sem, stats.at(b, steps))
                nc.gpsimd.tensor_tensor(rstd[:, 0:tiles], mv[:, 0:tiles, 1], eps[:].broadcast_to([P, tiles]),
                                        ALU.add).then_inc(done.sem, 1)
                pool.wait_ge(done.sem, done.at(b, 1))
                nc.gpsimd.tensor_tensor(rstd[:, 0:tiles], rstd[:, 0:tiles],
                                        neg_half[:].broadcast_to([P, tiles]), ALU.pow
                                        ).then_inc(done.sem, 1)

            def mix_in(b, f):
                pool.wait_ge(idx_loaded.sem, idx_loaded.at(b, 1))
                if later(b):
                    pool.wait_ge(hid_ready.sem, hid_ready.at(b - 1, 5))
                nc.gpsimd.tensor_tensor(spare[:, 1:2], one[:], one[:], ALU.mult)
                pool.indirect_dma_start(txt_row[:], None, a["L0_txt_W_E"],
                                        bass.IndirectOffsetOnAxis(ap=txt_idx[:, 0:1], axis=0)
                                        ).then_inc(txt_loaded.sem, 16)

            def mix_sums(b, f):
                pool.wait_ge(txt_loaded.sem, txt_loaded.at(b, 1))
                if later(b):
                    pool.wait_ge(res_ready.sem, res_ready.at(b - 1, TT))
                nc.gpsimd.tensor_tensor(hid[:, IT], txt_row[:], root_e[:].broadcast_to([P, E]), ALU.mult
                                        ).then_inc(hid_ready.sem, 1)

            def mix_out(b, f):
                root(b, mix_dve, 5 + 2 * IT, mix_root, IT)

            def mix_norm(b, f):
                if not later(b):
                    pool.wait_ge(loaded[1], 16 * N_LOADS[1])
                for i in range(IT):
                    pool.wait_ge(mix_dve.sem, mix_dve.at(b, 5 + 2 * IT + 1 + i))
                    nc.gpsimd.tensor_tensor(hid[:, i], hid[:, i], ln_g[:], ALU.mult).then_inc(hid_ready.sem, 1)
                    pool.wait_ge(hid_ready.sem, hid_ready.at(b, 2 + 2 * i))
                    nc.gpsimd.tensor_tensor(hid[:, i], hid[:, i], ln_b[:], ALU.add).then_inc(hid_ready.sem, 1)

            def norm_stats(b, f):
                root(b, ln2, 2 * TT, ln2_root, TT)

            def project_rest(b, f):
                if not later(b):
                    pool.wait_ge(loaded[2], 16 * N_LOADS[2])
                pool.wait_ge(ln2.sem, ln2.at(b, 3 * TT))
                nc.gpsimd.tensor_tensor(hid[:], hid[:], bo_all[:].unsqueeze(1).broadcast_to([P, TT, E]),
                                        ALU.add).then_inc(hid_bo.sem, 1)

            def weights(b, f):
                for n, (hi, lo) in enumerate(((wg_hi, wg_lo), (wu_hi, wu_lo))):
                    pool.wait_ge(gu_high, n + 1)
                    nc.gpsimd.tensor_tensor(lo[:], staged_w[n], hi[:].bitcast(F32), ALU.subtract
                                            ).then_inc(gu_low, 1)
                pool.wait_ge(gu_low, 2)

            def attend(b, f, h, seen):
                if h % 2 == 0:
                    return
                if h == 1:
                    pool.wait_ge(max_done.sem, max_done.at(b, AH))
                pool.wait_ge(exp_done.sem, exp_done.at(b, h + 1))
                for c in range(P // BL):
                    rows = slice(c * BL, (c + 1) * BL)
                    if c or h > 1:
                        pool.wait_ge(win_done.sem, win_done.at(b, WINS * (h // 2) + c))
                    else:
                        pool.wait_ge(hid_bo.sem, hid_bo.at(b, 1))
                    slot = (h - 1) % PTS
                    win = bass.AP(tensor=Z, offset=Z[rows].offset + slot * TT * TP + PAD + c * BL - WIN,
                                  ap=[[Z[rows].ap[0][0], BL], [TT * TP, 2], [TP + P, TT], [1, WD_]])
                    nc.gpsimd.tensor_tensor(
                        band_t[rows, :, :, h - 1:h + 1].rearrange("p i w h -> p h i w"), win,
                        one[rows].unsqueeze(2).unsqueeze(3).broadcast_to([BL, 2, TT, WD_]), ALU.mult
                    ).then_inc(win_done.sem, 1)

            def residual(b, f):
                root(b, ln3, 2 * TT, ln3_root, TT)

            rounds(pool, {"mix_in": mix_in, "mix_sums": mix_sums, "mix_out": mix_out,
                          "mix_norm": mix_norm, "norm_stats": norm_stats, "project_rest": project_rest,
                          "weights": weights, "attend": attend, "residual": residual})


_NAMES = ["x", "L0_tok_w_bias", "L0_tok_Wk_b", "L0_tok_Wv_b", "L0_tok_Wq_b", "L0_tok_out_w", "L0_tok_out_b",
          "L0_tok_ln_g", "L0_tok_ln_b", "L0_txt_W_E", "L0_attn_Wq", "L0_attn_bq", "L0_attn_Wk", "L0_attn_bk",
          "L0_attn_Wv", "L0_attn_bv", "L0_attn_Wo", "L0_attn_bo", "L0_attn_emb_rel_k", "L0_attn_emb_rel_v",
          "L0_ffn_Wg", "L0_ffn_Wu", "L0_ffn_Wd", "L0_ffn_Wr", "L0_ffn_temperature"]


def kernel(**inputs):
    import concourse.bacc as bacc
    from concourse.bass_utils import run_bass_kernel_spmd

    data = {n: np.ascontiguousarray(inputs[n]) for n in _NAMES}
    data["tok_wk_t"] = np.ascontiguousarray(np.asarray(inputs["L0_tok_Wk_w"]).T)
    data["tok_wv_t"] = np.ascontiguousarray(np.asarray(inputs["L0_tok_Wv_w"]).T)
    data["tok_wq_t"] = np.ascontiguousarray(np.asarray(inputs["L0_tok_Wq_w"]).T)
    data["txt_t"] = np.ascontiguousarray(inputs["x_txt"]).reshape(NB, TXT, 1)
    data["mask"] = np.ascontiguousarray(inputs["L0_tok_local_mask"])
    row = np.arange(P)
    data["ident"] = np.eye(P, dtype=np.float32)
    data["head_of_row"] = (row[:, None, None] // AD + (P // AD) * np.arange(KT)[None, :, None]
                           == np.arange(AH)[None, None, :]).astype(np.float32)
    data["head_of_rel"] = (row[:, None] % AH == np.arange(AH)[None, :]).astype(np.float32)
    data["earlier"] = np.broadcast_to((np.arange(NE)[None, :] < np.arange(NE)[:, None]).astype(np.float32),
                                      (P, NE, NE)).copy()

    nc = bacc.Bacc("TRN2", target_bir_lowering=False, num_devices=1)
    arrays, aps = {}, {}
    for name, array in data.items():
        arrays[f"in_{name}"] = array
        aps[name] = nc.dram_tensor(f"in_{name}", array.shape, mybir.dt.from_np(array.dtype),
                                   kind="ExternalInput").ap()
    out = nc.dram_tensor("out_0", (NB, T, E), F32, kind="ExternalOutput").ap()
    fusion_block(nc, aps, out)
    return run_bass_kernel_spmd(nc, [arrays], core_ids=[0]).results[0]["out_0"]
```

```python
from contextlib import ExitStack

import numpy as np

import concourse.bass as bass
from concourse import mybir

F32 = mybir.dt.float32
F32R = mybir.dt.float32r
BF16 = mybir.dt.bfloat16
I32 = mybir.dt.int32
U8 = mybir.dt.uint8
ALU = mybir.AluOpType
ACT = mybir.ActivationFunctionType
AX = mybir.AxisListType.X

P = 128
NB = 8
F, L, H = 64, 256, 4
E = H * F
KT = E // P
TXT = 128
T = L + TXT
TT = T // P
IT = L // P
AH, AD = 16, 16
WIN = 4
NJ = 2 * WIN + 1
NE = 8
FI = 256
FT = FI // P
SLOTS = 6
KST = SLOTS * AD
Q_PART = [0, 0, 1, 0, 2, 1]
K_PART = [0, 1, 0, 2, 0, 1]
BL = 32
WD_ = BL + 2 * WIN
ROW = WD_ * AH
BT = 64
WB = BT + 2 * WIN
ROWB = WB * AH
RJ = NJ * AH
BPITCH = BL * ROW + BL * AH
LEAD = 4096
BAND = LEAD + (T // BL) * BPITCH + 8192
PAD = WIN
TP = T + 2 * PAD
GRP = 4
PTS = 6
VC = AD + 1
EPS = 1e-5
ITEMS = AH * TT // 2
WINS = P // BL
N_LOADS = (9, 4, 13 + P // AD + NJ)
N_ZERO = 7
N_CONSTS = 8
FILL_MIX = [("residual", 0), ("mix_in", 0), ("turn_x2", 0), ("mix_sums", 0), ("router", 1),
            ("mix_out", 0), ("router_zone", 1), ("mix_norm", 1), ("router_rank", 2),
            ("norm_stats", 2), ("router_pick", 1), ("turn_norm", 2), ("project_qk", 0),
            ("project_rel", 1), ("project_v", 12)]
FILL_MAXIMA = [1, 1, 0, 0, 2, 0, 1, 1, 0, 2, 0, 0, 2, 0, 0, 2, 1, 0, 1, 1, 0, 2, 1, 0]
FILL_NEGATE = 3
FILL_OUT = [("turn_outputs", 3), ("turn_weights", 2), ("rel_values", 2), ("turn_attn", 3)]
R_DIST = 4
ZONE_LO = float(np.float32(0.5 - np.log(4.0 / 3.0)))
ZONE_HI = 0.5
CENTER = float(np.float32(1.0 / np.e))


class Signal:

    def __init__(self, sem, n, unit=1, first=0):
        self.sem, self.n, self.unit, self.first = sem, n, unit, first

    def at(self, b, k):
        return b * (self.n * self.unit) + k * self.unit + self.first


def fusion_block(nc, a, out):
    ctx = ExitStack()

    def sb(name, shape, dt=F32):
        return ctx.enter_context(nc.sbuf_tensor(name, shape, dt))

    def ps(name, shape, dt=F32):
        return ctx.enter_context(nc.psum_tensor(name, shape, dt))

    def sem(name):
        return ctx.enter_context(nc.semaphore(name))

    def sig(name, n, unit=1, first=0):
        return Signal(sem(name), n, unit, first)

    with ctx:
        ident = sb("ident", [P, P])
        ident_b = sb("ident_b", [P, P], BF16)
        head_of_row = sb("head_of_row", [P, KT, AH])
        head_of_rel = sb("head_of_rel", [P, AH])
        earlier = sb("earlier", [P, NE, NE])
        wkv = sb("wkv", [F + 1, 2 * F])
        wq_t = sb("wq_t", [F + 1, F])
        resid = sb("resid", [F + 1, H, F])
        ew_t = sb("ew_t", [P, IT, L])
        out_w = sb("out_w", [P, KT, E])
        ln_g = sb("ln_g", [P, E])
        ln_b = sb("ln_b", [P, E])
        bv_all = sb("bv_all", [P, E])
        bo_all = sb("bo_all", [P, E])
        bq4 = sb("bq4", [P, KT])
        bk1 = sb("bk1", [P, KT])
        w_q = sb("w_q", [P, KT, E])
        w_k = sb("w_k", [P, KT, E])
        w_v = sb("w_v", [P, KT, E])
        w_o = sb("w_o", [P, KT, E])
        rel_k = sb("rel_k", [P, KT, NJ, AH])
        rel_v0 = sb("rel_v0", [P, AH, AD])
        rel_v1 = sb("rel_v1", [RJ - P, AH, AD])
        wg_hi = sb("wg_hi", [P, NE, KT, FI], F32R)
        wg_lo = sb("wg_lo", [P, NE, KT, FI], F32R)
        wu_hi = sb("wu_hi", [P, NE, KT, FI], F32R)
        wu_lo = sb("wu_lo", [P, NE, KT, FI], F32R)
        w_d = sb("w_d", [P, NE, FT, E])
        w_r = sb("w_r", [P, KT, NE])
        wr_hi = sb("wr_hi", [P, KT, NE], F32R)
        wr_lo = sb("wr_lo", [P, KT, NE], F32R)
        neg_temp = sb("neg_temp", [P, 1])

        x_in = sb("x_in", [F + 1, L, H])
        txt_idx = sb("txt_idx", [P, 1], I32)
        txt_row = sb("txt_row", [P, E])
        hid = sb("hid", [P, TT, E])
        q_st = sb("q_st", [KST + 2, AH, T], BF16)
        k_st = sb("k_st", [KST + 2, AH, T], BF16)
        v_one = sb("v_one", [P, TT, AH, VC])
        band_w = sb("band_w", [P, TT, WD_, AH])
        band_s = sb("band_s", [P, TT, WD_, AH])
        maxima_sb = sb("maxima", [P, TT, AH])
        neg_max = sb("neg_max", [AH // 2, 2, T], BF16)
        o_sb = sb("o_sb", [P, AH // GRP, T])
        res = sb("res", [P, TT, E])
        x2_hi = sb("x2_hi", [P, KT, T], F32R)
        x2_lo = sb("x2_lo", [P, KT, T], F32R)
        wgt = sb("wgt", [P, TT, NE])
        silu = sb("silu", [P, T])
        hT = sb("hT", [P, 3, T])
        stat = sb("stat", [P, TT, 6])
        mv = sb("mv", [P, TT, 2])
        rstd = sb("rstd", [P, TT])
        eps = sb("eps", [P, 1])
        neg_half = sb("neg_half", [P, 1])
        root_e = sb("root_e", [P, 1])
        one = sb("one", [P, 1])
        spare = sb("spare", [P, 4])

        ZF = 8192
        Z = sb("scratch", [P, ZF])

        def zone(start, *dims, rows=P):
            n = int(np.prod(dims))
            v = Z[0:rows, start:start + n]
            names = "abcd"[:len(dims)]
            if len(dims) > 1:
                v = v.rearrange(f"p ({' '.join(names)}) -> p {' '.join(names)}",
                                **{c: d for c, d in zip(names[1:], dims[1:])})
            return v

        p_t = zone(0, PTS, TT, TP)[:, :, :, PAD:PAD + T]
        ek, ekv = zone(0, IT, E), zone(512, IT, E)
        eq, dd, y_t = zone(1024, KT, L), zone(1536, KT, L), zone(2048, KT, L)
        xn = zone(4928, TT, E)
        xn_t = zone(5696, KT, T)
        qf, kf = zone(2304, KT, T), zone(3072, KT, T)
        rest = zone(4928, KT, T)
        rel_log = zone(3840, TT, RJ)
        parts = [Z[:, at:at + KT * T // 2].bitcast(BF16).rearrange("p (m t) -> p m t", m=KT)
                 for at in range(0, 6 * KT * T // 2, KT * T // 2)]
        rel_w = zone(0, TT, RJ)
        rwt0, rwt1 = zone(512, T), zone(896, T, rows=RJ - P)
        out_st = zone(6400, TT, E)
        attn, rden = zone(5568, TT, E), zone(6336, TT, AH)
        attn_t = zone(4800, KT, T)
        xn2 = zone(5600, TT, E)
        rt = [zone(6400 + 32 * i, TT, NE) for i in range(9)]
        rsum = zone(6700, TT)
        rpair = zone(6720, TT, NE, NE)
        rpair2 = zone(6920, TT, NE, NE)

        emb_k_rows = zone(7640, NJ)
        emb_v_rows0, emb_v_rows1 = zone(7656, AD), zone(7672, AD)
        rel_log_b = Z[:, 4272:4272 + TT * RJ // 2].bitcast(BF16).rearrange("p (i r) -> p i r", i=TT)
        BAND_AT = ZF - TT * ROWB // 2
        band_t = Z[:, BAND_AT:ZF].bitcast(BF16).rearrange("p (i w h) -> p i w h", i=TT, h=AH)

        S = ps("S", [P, 8, 512])
        O, G, U = S[:, 3], S[:, 6], S[:, 7]
        D = S[:, 4:6]

        REL_TILES = ((0, S[:, 0, 0:E]), (1, S[:, 2, 0:E]), (2, O[:, 0:E]))

        d_parts = nc.dram_tensor("d_parts", [6, E, T], BF16, kind="Internal").ap()
        d_neg = nc.dram_tensor("d_neg", [2, 2, AH // 2, T], BF16, kind="Internal").ap()
        d_band_t = nc.dram_tensor("d_band_t", [T * ROWB], BF16, kind="Internal").ap()
        d_band_s = nc.dram_tensor("d_band_s", [BAND], F32, kind="Internal").ap()
        d_band_w = nc.dram_tensor("d_band_w", [BAND], F32, kind="Internal").ap()

        def dram(t, offset, *dims):
            return bass.AP(tensor=t.tensor, offset=offset, ap=[list(d) for d in dims])

        loaded = [sem(f"loaded{g}") for g in range(3)]
        gu_loaded = [sem(f"gu_loaded{n}") for n in range(4)]
        wd_loaded, zeroed = sem("wd_loaded"), sem("zeroed")
        zero_ready, ones_ready, psum_clear = sem("zero_ready"), sem("ones_ready"), sem("psum_clear")
        mask_float, wb_masked, ew_exp = sem("mask_float"), sem("wb_masked"), sem("ew_exp")
        ew_turned, ew_ready, resid_ready = sem("ew_turned"), sem("ew_ready"), sem("resid_ready")
        temp_inverse, wr_high, consts = sem("temp_inverse"), sem("wr_high"), sem("consts")
        gu_high, gu_low, pool_consts = sem("gu_high"), sem("gu_low"), sem("pool_consts")
        x_loaded = sig("x_loaded", 1, 16)
        idx_loaded = sig("idx_loaded", 1, 16)
        txt_loaded = sig("txt_loaded", 1, 16)
        mix_pe = sig("mix_pe", 7)
        mix_act = sig("mix_act", 3)
        mix_dve = sig("mix_dve", 11)
        hid_ready = sig("hid_ready", 5)
        mix_root, ln2_root, ln3_root = sig("mix_root", 2), sig("ln2_root", 2), sig("ln3_root", 2)
        ln2 = sig("ln2", 3 * TT)
        xt_pe, xt_act = sig("xt_pe", 2), sig("xt_act", 2)
        proj_pe = sig("proj_pe", 10)
        proj_act = sig("proj_act", 10)
        v_done = sig("v_done", TT)
        split = sig("split", 6)
        q_out, k_out = sig("q_out", 3, 16), sig("k_out", 3, 16)
        stacked = sig("stacked", 2 * SLOTS, 16)
        rel_t_out, rel_s_out = sig("rel_t_out", P // BT, 16), sig("rel_s_out", TT, 16)
        band_t_in, band_s_in = sig("band_t_in", 1, 16), sig("band_s_in", 4, 16)
        max_pe = sig("max_pe", ITEMS)
        max_done = sig("max_done", ITEMS)
        neg_pe, neg_act, neg_dve = sig("neg_pe", 2), sig("neg_act", 2), sig("neg_dve", 2)
        neg_out, neg_in = sig("neg_out", 2, 16), [sig(f"neg_in{half}", 1, 16) for half in range(2)]
        sc_pe = sig("sc_pe", ITEMS)
        sc_add = sig("sc_add", 4 * ITEMS)
        exp_done = sig("exp_done", ITEMS)
        win_done = sig("win_done", WINS * AH // 2)
        pv_done = sig("pv_done", AH // GRP)
        o_copied = sig("o_copied", AH // GRP)
        win_out = sig("win_out", 4, 16)
        relw_in = sig("relw_in", 3, 16)
        rw_pe, rw_act = sig("rw_pe", 2), sig("rw_act", 2)
        ot_pe = sig("ot_pe", TT)
        or_pe = sig("or_pe", TT)
        att_dve = sig("att_dve", 3 * TT + 1)
        at_pe, at_act = sig("at_pe", 2), sig("at_act", 2)
        wo_pe = sig("wo_pe", TT)
        hid_bo = sig("hid_bo", 1)
        res_ready = sig("res_ready", TT)
        ln3 = sig("ln3", 3 * TT)
        x2_pe, x2_hi_done, x2_lo_done = sig("x2_pe", 2), sig("x2_hi_done", 2), sig("x2_lo_done", 2)
        r_pe = sig("r_pe", 1)
        r_act = sig("r_act", 3)
        R_STEPS = 24
        r_dve = sig("r_dve", R_STEPS)
        gate_pe, up_pe = sig("gate_pe", NE * FT), sig("up_pe", NE * FT)
        silu_done = sig("silu_done", NE * FT)
        h_done = sig("h_done", NE * FT)
        down_pe = sig("down_pe", 2 * NE)
        acc_done = sig("acc_done", NE * TT, first=1)
        stored = sig("stored", 1, 16, first=16)

        units = [("gate", 0), ("up", 0), ("gate", 1), ("up", 1)]
        for e in range(NE):
            if e + 1 < NE:
                units += [("gate", 2 * e + 2), ("up", 2 * e + 2)]
            units += [("down", e, 0), ("down", e, 1)]
            if e + 1 < NE:
                units += [("gate", 2 * e + 3), ("up", 2 * e + 3)]
        after = {"up": "hidden", "down": "accumulate"}

        def tiles_of(n):
            h = 2 * (n // 3)
            return (((h, 0), (h, 1)), ((h, 2), (h + 1, 2)), ((h + 1, 0), (h + 1, 1)))[n % 3]

        def schedule(attention, ffn):
            left = list(units) if ffn else []
            steps = []
            late, owed = [], []
            seen = {"up": 0, "down": 0}

            def flush():
                while late:
                    steps.append(late.pop(0))

            def fill(n):
                for _ in range(min(n, len(left))):
                    unit = left.pop(0)
                    flush()
                    if owed and unit[0] == "down" and unit[2]:
                        steps.append(owed.pop())
                    steps.append(unit)
                    if unit[0] in after:
                        late.append((after[unit[0]],) + unit[1:])
                        seen[unit[0]] += 1

            if not attention:
                steps += [("residual",), ("turn_x2",), ("router",)]
                fill(3)
                steps += [("router_zone",), ("router_rank",), ("router_pick",)]
                fill(len(left))
                flush()
                return steps + [("store",)]
            for name, n in FILL_MIX:
                if name not in LATE_STEPS or ffn:
                    steps.append((name,))
                fill(n)
                if name == "mix_out" and not ffn:
                    steps.append(("prepare",))
            if not ffn:
                steps.append(("weights",))
            for n in range(ITEMS):
                steps.append(("maxima", n))
                fill(FILL_MAXIMA[n])
                if n == ITEMS // 2 + 1:
                    flush()
                    steps.append(("negate", 0, dict(seen)))
                    owed.append(("negated", 0))
            if not ffn:
                steps.append(("weights_ready",))
            flush()
            steps.append(("negate", 1, dict(seen)))
            owed[:] = [("negated", 1)]
            fill(FILL_NEGATE)
            flush()
            for n in range(ITEMS):
                steps.append(("attend", n, dict(seen)))
                g, at = divmod(n - 7, 6)
                if g >= 0 and at < TT:
                    steps.append(("values", g, at, dict(seen)))
                if n >= 9 and (n - 9) % 6 == 0:
                    steps.append(("copy", (n - 9) // 6))
            last = AH // GRP - 1
            steps += [("values", last, i, dict(seen)) for i in range(TT)] + [("copy", last)]
            for name, n in FILL_OUT:
                steps.append((name,))
                fill(n)
            fill(len(left))
            flush()
            if ffn:
                steps.append(("store",))
                order = [s[0] for s in steps]
                assert order.index("router_pick") < order.index("accumulate")
                assert order.index("turn_x2") < order.index("gate")
            return steps

        LATE_STEPS = ("residual", "turn_x2", "router", "router_zone", "router_rank", "router_pick",
                      "gate", "up", "down", "hidden", "accumulate", "store")

        def rounds(engine, parts):

            def do(step, b, f):
                part = parts.get(step[0])
                if part is not None:
                    part(f if step[0] in LATE_STEPS else b, *step[1:])

            for s in schedule(True, False):
                do(s, 0, None)
            with engine.Fori(1, NB) as b:
                for s in schedule(True, True):
                    do(s, b, b - 1)
            for s in schedule(False, True):
                do(s, None, NB - 1)

        def acc_of(parts):
            return TT * (parts // 2) + 2 * (parts % 2)

        def expert_half(n):
            return slice(n % 2 * NE // 2, (n % 2 + 1) * NE // 2)

        def later(b):
            return not isinstance(b, int)

        block = ctx.enter_context(nc.Block())

        @block.sync
        def _(sp):
            groups = [[
                (Z[:, 0:512].rearrange("p (i s) -> p i s", i=IT),
                 a["L0_tok_w_bias"].rearrange("(i p) s -> p i s", p=P)),
                (Z[:, 512:640].bitcast(U8).rearrange("p (i s) -> p i s", i=IT),
                 a["mask"].rearrange("(i p) s -> p i s", p=P)),
                (ident[:], a["ident"]),
                (wkv[0:F, 0:F], a["tok_wk_t"]), (wkv[0:F, F:2 * F], a["tok_wv_t"]),
                (wkv[F:F + 1, 0:F], a["L0_tok_Wk_b"].unsqueeze(0)),
                (wkv[F:F + 1, F:2 * F], a["L0_tok_Wv_b"].unsqueeze(0)),
                (wq_t[0:F, :], a["tok_wq_t"]), (wq_t[F:F + 1, :], a["L0_tok_Wq_b"].unsqueeze(0)),
            ], [
                (resid[F:F + 1, :, :], a["L0_tok_out_b"].rearrange("(o h c) -> o h c", o=1, h=H)),
                (out_w[:], a["L0_tok_out_w"].rearrange("(k p) n -> p k n", p=P)),
                (ln_g[:], a["L0_tok_ln_g"].partition_broadcast(P)),
                (ln_b[:], a["L0_tok_ln_b"].partition_broadcast(P)),
            ], [
                (head_of_row[:], a["head_of_row"]), (head_of_rel[:], a["head_of_rel"]),
                (earlier[:], a["earlier"]),
                (bq4[:], a["L0_attn_bq"].rearrange("(k p) -> p k", p=P)),
                (bk1[:], a["L0_attn_bk"].rearrange("(k p) -> p k", p=P)),
                (w_q[:], a["L0_attn_Wq"].rearrange("(k p) n -> p k n", p=P)),
                (w_k[:], a["L0_attn_Wk"].rearrange("(k p) n -> p k n", p=P)),
                (w_v[:], a["L0_attn_Wv"].rearrange("(k p) n -> p k n", p=P)),
                (w_o[:], a["L0_attn_Wo"].rearrange("(k p) n -> p k n", p=P)),
                (bv_all[:], a["L0_attn_bv"].partition_broadcast(P)),
                (bo_all[:], a["L0_attn_bo"].partition_broadcast(P)),
                (w_r[:], a["L0_ffn_Wr"].rearrange("(k p) n -> p k n", p=P)),
                (neg_temp[:], a["L0_ffn_temperature"].partition_broadcast(P)),
            ]]
            emb_v = a["L0_attn_emb_rel_v"]
            for r in range(P // AD):
                groups[2].append((emb_k_rows[AD * r:AD * (r + 1)],
                                  a["L0_attn_emb_rel_k"].rearrange("o j d -> d (o j)")))
            for j in range(NJ):
                rows = slice(AH * j, AH * (j + 1)) if j < P // AH else slice(0, AH)
                at = emb_v_rows0 if j < P // AH else emb_v_rows1
                groups[2].append((at[rows], dram(emb_v, j * AD, (0, AH), (1, AD))))

            def load(g):
                assert len(groups[g]) == N_LOADS[g]
                with nc.allow_non_contiguous_dma(reason="small bias and embedding columns, once"):
                    for dst, src in groups[g]:
                        sp.dma_start(dst, src).then_inc(loaded[g], 16)

            load(0)

            def mix_in(b):
                if later(b):
                    sp.wait_ge(mix_pe.sem, mix_pe.at(b - 1, 7))
                    sp.wait_ge(txt_loaded.sem, txt_loaded.at(b - 1, 1))
                sp.dma_start(x_in[0:F, :, :], a["x"][b]).then_inc(x_loaded.sem, 16)
                sp.dma_start(txt_idx[:], a["txt_t"][b]).then_inc(idx_loaded.sem, 16)
                if not later(b):
                    load(1)
                    load(2)
                    sp.wait_ge(zero_ready, 1)
                    zero = band_w[:].rearrange("p i w h -> p (i w h)")
                    n = T * ROWB // P
                    sp.dma_start(dram(d_band_t, 0, (n, P), (1, n)), zero.bitcast(BF16)[:, 0:n]
                                 ).then_inc(zeroed, 16)
                    n = TT * ROW
                    for d in (d_band_s, d_band_w):
                        for r0 in range(0, BAND, P * n):
                            rows = min(P, (BAND - r0) // n)
                            rest = min(BAND - r0 - rows * n, n) if rows < P else 0
                            sp.dma_start(dram(d, r0, (n, rows), (1, n)), zero[0:rows]).then_inc(zeroed, 16)
                            if rest:
                                sp.dma_start(dram(d, r0 + rows * n, (rest, 1), (1, rest)),
                                             zero[0:1, 0:rest]).then_inc(zeroed, 16)

            def load_experts(n, name, done):
                sp.dma_start(w_d[:, expert_half(n)], a[name][expert_half(n)].rearrange(
                    "e (k p) n -> p e k n", p=P)).then_inc(done, 16)

            def prepare(b):
                for n in range(2):
                    load_experts(n, "L0_ffn_Wg", gu_loaded[n])

            def weights(b):
                for n in range(4):
                    sp.wait_ge(gu_low, n + 1)
                    if n < 2:
                        load_experts(n, "L0_ffn_Wu", gu_loaded[2 + n])
                    else:
                        load_experts(n, "L0_ffn_Wd", wd_loaded)


            def project_rel(b):
                if not later(b):
                    sp.wait_ge(zeroed, N_ZERO * 16)
                def part_out(n, done, k, out):
                    sp.wait_ge(done.sem, done.at(b, k))
                    sp.dma_start(d_parts[n].rearrange("(m p) t -> p m t", p=P), parts[n]
                                 ).then_inc(out.sem, 16)

                def stack(st, base, order):
                    for n in range(SLOTS):
                        sp.dma_start(
                            st[AD * n:AD * (n + 1)],
                            d_parts[base + order[n]].rearrange("(h d) t -> d h t", d=AD)
                        ).then_inc(stacked.sem, 16)

                part_out(0, proj_act, 3, q_out)
                part_out(1, split, 2, q_out)
                part_out(2, split, 3, q_out)
                part_out(3, proj_act, 6, k_out)
                sp.wait_ge(proj_act.sem, proj_act.at(b, 10))
                for c in range(P // BT):
                    sp.dma_start(
                        dram(d_band_t, c * BT * ROWB, (ROWB + AH, BT), (P * ROWB, TT), (1, RJ)),
                        rel_log_b[c * BT:(c + 1) * BT]).then_inc(rel_t_out.sem, 16)
                part_out(4, split, 5, k_out)
                part_out(5, split, 6, k_out)
                if later(b):
                    sp.wait_ge(sc_pe.sem, sc_pe.at(b - 1, ITEMS))
                sp.wait_ge(q_out.sem, q_out.at(b, 3))
                stack(q_st, 0, Q_PART)
                sp.wait_ge(rel_t_out.sem, rel_t_out.at(b, P // BT))
                sp.dma_start(band_t.rearrange("p i w h -> p i (w h)"),
                             dram(d_band_t, 0, (ROWB, P), (P * ROWB, TT), (1, ROWB))
                             ).then_inc(band_t_in.sem, 16)
                sp.wait_ge(k_out.sem, k_out.at(b, 3))
                stack(k_st, 3, K_PART)
                for i in range(TT):
                    sp.dma_start(
                        dram(d_band_s, LEAD + (i * P) * (ROW + AH) - WIN * ROW + WIN * AH,
                             (ROW + AH, P), (ROW, NJ), (1, AH)),
                        rel_log[:, i].rearrange("p (j h) -> p j h", j=NJ)).then_inc(rel_s_out.sem, 16)
                sp.wait_ge(rel_s_out.sem, rel_s_out.at(b, TT))
                if later(b):
                    sp.wait_ge(sc_add.sem, sc_add.at(b - 1, 4 * ITEMS))
                for c in range(P // BL):
                    sp.dma_start(
                        band_s[c * BL:(c + 1) * BL].rearrange("p i w h -> p i (w h)"),
                        dram(d_band_s, LEAD + c * BPITCH, (ROW, BL), (P // BL * BPITCH, TT), (1, ROW))
                    ).then_inc(band_s_in.sem, 16)

            def negate(b, half, seen):
                sp.wait_ge(neg_act.sem, neg_act.at(b, half + 1))
                sp.wait_ge(neg_dve.sem, neg_dve.at(b, half + 1))
                sp.dma_start(d_neg[half].rearrange("i h t -> h i t"), neg_max[:]
                             ).then_inc(neg_out.sem, 16)
                sp.wait_ge(neg_out.sem, neg_out.at(b, half + 1))
                sp.dma_start(q_st[KST:KST + 2, half * AH // 2:(half + 1) * AH // 2], d_neg[half]
                             ).then_inc(neg_in[half].sem, 16)

            def windows_back(b):
                sp.wait_ge(win_done.sem, win_done.at(b, WINS * AH // 2))
                for c in range(P // BL):
                    sp.dma_start(
                        dram(d_band_w, LEAD + c * BPITCH, (ROW, BL), (P // BL * BPITCH, TT), (1, ROW)),
                        band_w[c * BL:(c + 1) * BL].rearrange("p i w h -> p i (w h)")
                    ).then_inc(win_out.sem, 16)
                sp.wait_ge(win_out.sem, win_out.at(b, 4))
                sp.wait_ge(pv_done.sem, pv_done.at(b, AH // GRP))
                for i in range(TT):
                    sp.dma_start(
                        rel_w[:, i].rearrange("p (j h) -> p j h", j=NJ),
                        dram(d_band_w, LEAD + (i * P) * (ROW + AH) - WIN * ROW + WIN * AH,
                             (ROW + AH, P), (ROW, NJ), (1, AH))).then_inc(relw_in.sem, 16)

            def store(f):
                sp.wait_ge(acc_done.sem, acc_done.at(f, NE * TT))
                sp.dma_start(out[f].rearrange("(i p) e -> p i e", p=P), out_st).then_inc(stored.sem, 16)

            rounds(sp, {"mix_in": mix_in, "prepare": prepare, "project_rel": project_rel,
                        "weights": weights, "negate": negate, "turn_weights": windows_back,
                        "store": store})
            sp.wait_ge(stored.sem, stored.at(NB - 1, 1))

        @block.tensor
        def _(pe):
            def turn(dst, src, rows=P):
                return pe.transpose(dst, src, ident[0:rows, 0:rows])

            pe.wait_ge(loaded[0], 16 * N_LOADS[0])
            pe.wait_ge(ew_exp, 1)
            for si in range(IT):
                for ti in range(IT):
                    last = turn(S[:, si, ti * P:(ti + 1) * P],
                                Z[:, 1024 + ti * L + si * P:1024 + ti * L + (si + 1) * P])
                last.then_inc(ew_turned, 1)

            def mix_in(b):
                if not later(b):
                    pe.wait_ge(ones_ready, 1)
                    pe.wait_ge(ew_ready, 1)
                pe.wait_ge(x_loaded.sem, x_loaded.at(b, 1))
                for i in range(IT):
                    for h in range(H):
                        mm = pe.matmul(S[:, i, h * P:(h + 1) * P], x_in[:, i * P:(i + 1) * P, h],
                                       wkv[:], start=True, stop=True)
                    mm.then_inc(mix_pe.sem, 1)
                for h in range(H):
                    mm = pe.matmul(S[F * (h % 2):F * (h % 2) + F, 2, (h // 2) * L:(h // 2 + 1) * L],
                                   wq_t[:], x_in[:, :, h], start=True, stop=True)
                mm.then_inc(mix_pe.sem, 1)

            def mix_sums(b):
                if not later(b):
                    pe.wait_ge(psum_clear, 1)
                pe.wait_ge(mix_act.sem, mix_act.at(b, 2))
                for m in range(KT):
                    for i in range(IT):
                        mm = pe.matmul(O[:, m * L:(m + 1) * L], ek[:, i, m * P:(m + 1) * P],
                                       ew_t[:, i, :], start=(i == 0), stop=(i == IT - 1))
                mm.then_inc(mix_pe.sem, 1)
                pe.wait_ge(mix_dve.sem, mix_dve.at(b, 2))
                for m in range(KT):
                    for i in range(IT):
                        mm = pe.matmul(S[:, 0, m * L:(m + 1) * L], ekv[:, i, m * P:(m + 1) * P],
                                       ew_t[:, i, :], start=(i == 0), stop=(i == IT - 1))
                mm.then_inc(mix_pe.sem, 1)

            def mix_out(b):
                if not later(b):
                    pe.wait_ge(loaded[1], 16 * N_LOADS[1])
                    pe.wait_ge(resid_ready, H)
                pe.wait_ge(mix_dve.sem, mix_dve.at(b, 5))
                for i in range(IT):
                    for k in range(KT):
                        pe.matmul(S[:, 1, i * E:(i + 1) * E], y_t[:, k, i * P:(i + 1) * P], out_w[:, k, :],
                                  start=(k == 0), stop=False, skip_group_check=True)
                    for h in range(H):
                        mm = pe.matmul(S[:, 1, i * E + h * F:i * E + (h + 1) * F],
                                       x_in[:, i * P:(i + 1) * P, h], resid[:, h, :],
                                       start=False, stop=(h == H - 1), skip_group_check=True)
                    mm.then_inc(mix_pe.sem, 1)

            def turned(src, ready, steps, done, b, bank=0):
                pe.wait_ge(ready.sem, ready.at(b, steps))
                for k in range(KT):
                    for i in range(TT):
                        last = turn(S[:, bank + k, i * P:(i + 1) * P], src[:, i, k * P:(k + 1) * P])
                    last.then_inc(done.sem, 1)

            def turn_norm(b):
                turned(xn, ln2, 3 * TT, xt_pe, b)

            banks = [S[:, 2], S[:, 0], S[:, 1], O]

            def project_qk(b):
                if not later(b):
                    pe.wait_ge(loaded[2], 16 * N_LOADS[2])
                    pe.wait_ge(consts, N_CONSTS)
                pe.wait_ge(xt_act.sem, xt_act.at(b, 2))
                for n, (w, m) in enumerate([(w_q, 0), (w_q, 1), (w_k, 0), (w_k, 1)]):
                    for k in range(KT):
                        mm = pe.matmul(banks[n][:, 0:T], w[:, k, m * P:(m + 1) * P], xn_t[:, k, :],
                                       start=(k == 0), stop=(k == KT - 1))
                    mm.then_inc(proj_pe.sem, 1)

            def project_rel(b):
                for i, copied in enumerate((2, 2, 4)):
                    pe.wait_ge(proj_act.sem, proj_act.at(b, copied))
                    for m in range(KT):
                        mm = pe.matmul(banks[i][:, 0:RJ], qf[:, m, i * P:(i + 1) * P],
                                       rel_k[:, m].rearrange("p j h -> p (j h)"),
                                       start=(m == 0), stop=(m == KT - 1))
                    mm.then_inc(proj_pe.sem, 1)

            def project_v(b):
                for i in range(TT):
                    pe.wait_ge(proj_act.sem, proj_act.at(b, (5, 7, 8)[i]))
                    for k in range(KT):
                        mm = pe.matmul(banks[(3 + i) % 4][:, 0:E], xn_t[:, k, i * P:(i + 1) * P],
                                       w_v[:, k, :], start=(k == 0), stop=(k == KT - 1))
                    mm.then_inc(proj_pe.sem, 1)

            def maxima(b, n):
                if n == 0:
                    pe.wait_ge(stacked.sem, stacked.at(b, 2 * SLOTS))
                    pe.wait_ge(band_t_in.sem, band_t_in.at(b, 1))
                    pe.wait_ge(v_done.sem, v_done.at(b, TT))
                    pe.wait_ge(proj_act.sem, proj_act.at(b, 9))
                if n >= 2:
                    pe.wait_ge(max_done.sem, max_done.at(b, n - 1))
                for l, (h, i) in enumerate(tiles_of(n)):
                    bank = 2 * (n % 2) + l
                    pe.matmul(S[:, bank, PAD:PAD + T], q_st[0:KST, h, i * P:(i + 1) * P],
                              k_st[0:KST, h, :], start=True, stop=False, skip_group_check=True)
                    for c in range(P // BT):
                        rows = slice(c * BT, (c + 1) * BT)
                        first, last = i * P + c * BT == 0, i * P + (c + 1) * BT == T
                        w0, w1 = (WIN if first else 0), (WB - WIN if last else WB)
                        at = PAD + i * P + c * BT - WIN
                        mm = pe.matmul(S[rows, bank, at + w0:at + w1], ident_b[rows, rows],
                                       band_t[rows, i, w0:w1, h],
                                       start=False, stop=True, skip_group_check=True)
                mm.then_inc(max_pe.sem, 1)

            def weights_ready(b):
                pe.wait_ge(wd_loaded, 2 * 16)
                pe.wait_ge(gu_high, 4)
                pe.wait_ge(gu_low, 4)

            def negate(b, half, seen):
                pe.wait_ge(max_done.sem, max_done.at(b, (half + 1) * ITEMS // 2))
                if seen["down"]:
                    pe.wait_ge(acc_done.sem, acc_done.at(b - 1, acc_of(seen["down"])))
                if half:
                    pe.wait_ge(neg_dve.sem, neg_dve.at(b, half))
                for i in range(TT):
                    last = turn(S[0:AH // 2, 5, i * P:(i + 1) * P],
                                maxima_sb[:, i, half * AH // 2:(half + 1) * AH // 2])
                last.then_inc(neg_pe.sem, 1)

            def negated(b, half):
                pe.wait_ge(neg_dve.sem, neg_dve.at(b, half + 1))

            def attend(b, n, seen):
                if n % (ITEMS // 2) == 0:
                    half = n // (ITEMS // 2)
                    pe.wait_ge(neg_in[half].sem, neg_in[half].at(b, 1))
                if n == 0:
                    pe.wait_ge(max_done.sem, max_done.at(b, ITEMS))
                if n == 2:
                    pe.wait_ge(neg_dve.sem, neg_dve.at(b, 2))
                    if seen["down"]:
                        pe.wait_ge(acc_done.sem, acc_done.at(b - 1, acc_of(seen["down"])))
                if n >= 3:
                    pe.wait_ge(exp_done.sem, exp_done.at(b, n - 2))
                for l, (h, i) in enumerate(tiles_of(n)):
                    mm = pe.matmul(S[:, 2 * (n % 3) + l, PAD:PAD + T], k_st[:, h, i * P:(i + 1) * P],
                                   q_st[:, h, :], start=True, stop=True)
                mm.then_inc(sc_pe.sem, 1)

            def values(b, g, i, seen):
                if i == 0:
                    pe.wait_ge(exp_done.sem, exp_done.at(b, 6 * (g + 1)))
                    if g >= 2:
                        pe.wait_ge(o_copied.sem, o_copied.at(b, g - 1))
                    elif seen["up"]:
                        pe.wait_ge(h_done.sem, h_done.at(b - 1, seen["up"]))
                for l in range(GRP):
                    h = GRP * g + l
                    mm = pe.matmul(S[32 * l:32 * l + VC, 6 + g % 2, 0:T], v_one[:, i, h, :],
                                   p_t[:, h % PTS, i, :], start=(i == 0), stop=(i == TT - 1),
                                   skip_group_check=True)
                if i == TT - 1:
                    mm.then_inc(pv_done.sem, 1)

            def turn_outputs(b):
                pe.wait_ge(o_copied.sem, o_copied.at(b, AH // GRP))
                for i in range(TT):
                    for g in range(AH // GRP):
                        last = turn(S[:, i, g * P:(g + 1) * P], o_sb[:, g, i * P:(i + 1) * P])
                    last.then_inc(ot_pe.sem, 1)

            def turn_weights(b):
                pe.wait_ge(att_dve.sem, att_dve.at(b, 2 * TT + 1))
                for i in range(TT):
                    last = turn(O[:, i * P:(i + 1) * P], rel_w[:, i, 0:P])
                last.then_inc(rw_pe.sem, 1)
                for i in range(TT):
                    last = turn(S[0:RJ - P, 1, i * P:(i + 1) * P], rel_w[:, i, P:RJ])
                last.then_inc(rw_pe.sem, 1)

            def rel_values(b):
                pe.wait_ge(rw_act.sem, rw_act.at(b, 2))
                for i, dst in REL_TILES:
                    pe.matmul(dst, rwt0[:, i * P:(i + 1) * P], rel_v0[:].rearrange("p h d -> p (h d)"),
                              start=True, stop=False)
                    pe.matmul(dst, rwt1[:, i * P:(i + 1) * P], rel_v1[:].rearrange("p h d -> p (h d)"),
                              start=False, stop=True).then_inc(or_pe.sem, 1)

            def turn_attn(b):
                turned(attn, att_dve, 3 * TT + 1, at_pe, b)

            def residual(b):
                pe.wait_ge(at_act.sem, at_act.at(b, 2))
                pe.wait_ge(acc_done.sem, acc_done.at(b - 1, NE * TT))
                for i in range(TT):
                    dst = D[:, i // 2, (i % 2) * E:(i % 2 + 1) * E]
                    for k in range(KT):
                        mm = pe.matmul(dst, attn_t[:, k, i * P:(i + 1) * P], w_o[:, k, :],
                                       start=(k == 0), stop=(k == KT - 1))
                    mm.then_inc(wo_pe.sem, 1)

            def turn_x2(b):
                turned(xn2, ln3, 3 * TT, x2_pe, b, 6)

            def router(b):
                pe.wait_ge(x2_hi_done.sem, x2_hi_done.at(b, 2))
                pe.wait_ge(x2_lo_done.sem, x2_lo_done.at(b, 2))
                pe.wait_ge(res_ready.sem, res_ready.at(b, TT))
                for i in range(TT):
                    n = 0
                    for xs, ws in ((x2_hi, wr_hi), (x2_hi, wr_lo), (x2_lo, wr_hi)):
                        for k in range(KT):
                            mm = pe.matmul(S[:, 5, i * NE:(i + 1) * NE], xs[:, k, i * P:(i + 1) * P],
                                           ws[:, k, :], start=(n == 0), stop=(n == 3 * KT - 1))
                            n += 1
                mm.then_inc(r_pe.sem, 1)

            def hidden_tile(f, n, dst, hi, lo, done, free):
                e, m = n // FT, n % FT
                if n:
                    pe.wait_ge(free.sem, free.at(f, n))
                j = 0
                for ws, xs in ((hi, x2_hi), (hi, x2_lo), (lo, x2_hi)):
                    for k in range(KT):
                        mm = pe.matmul(dst[:, 0:T], ws[:, e, k, m * P:(m + 1) * P], xs[:, k, :],
                                       start=(j == 0), stop=(j == 3 * KT - 1))
                        j += 1
                mm.then_inc(done.sem, 1)

            def gate(f, n):
                hidden_tile(f, n, G, wg_hi, wg_lo, gate_pe, silu_done)

            def up(f, n):
                hidden_tile(f, n, U, wu_hi, wu_lo, up_pe, h_done)

            def down(f, e, part):
                if part == 0:
                    pe.wait_ge(h_done.sem, h_done.at(f, FT * (e + 1)))
                    if e == 0:
                        pe.wait_ge(r_act.sem, r_act.at(f, 1))
                if e:
                    pe.wait_ge(acc_done.sem, acc_done.at(f, acc_of(2 * e - 1 + part)))
                for i in ((0, 1), (2,))[part]:
                    for m in range(FT):
                        mm = pe.matmul(D[:, i // 2, (i % 2) * E:(i % 2 + 1) * E],
                                       hT[:, (FT * e + m) % 3, i * P:(i + 1) * P], w_d[:, e, m, :],
                                       start=(m == 0), stop=(m == FT - 1))
                mm.then_inc(down_pe.sem, 1)

            rounds(pe, {"mix_in": mix_in, "mix_sums": mix_sums, "mix_out": mix_out,
                        "turn_norm": turn_norm, "project_qk": project_qk, "project_rel": project_rel,
                        "project_v": project_v, "maxima": maxima, "weights_ready": weights_ready, "negate": negate,
                        "negated": negated, "attend": attend, "values": values, "turn_weights": turn_weights,
                        "turn_outputs": turn_outputs, "rel_values": rel_values, "turn_attn": turn_attn,
                        "residual": residual, "turn_x2": turn_x2, "router": router, "gate": gate,
                        "up": up, "down": down})

        @block.scalar
        def _(act):
            act.wait_ge(wb_masked, 1)
            nc.scalar.activation(zone(1024, IT, L), zone(0, IT, L), ACT.Exp).then_inc(ew_exp, 1)
            act.wait_ge(ew_turned, IT)
            nc.scalar.activation(ew_t[:], S[:, 0:IT, 0:L], ACT.Copy).then_inc(ew_ready, 1)

            def mix_in(b):
                for i in range(IT):
                    act.wait_ge(mix_pe.sem, mix_pe.at(b, i + 1))
                    nc.scalar.activation(ek[:, i].rearrange("p (h d) -> p h d", h=H),
                                         S[:, i].rearrange("p (h c) -> p h c", h=H)[:, :, 0:F],
                                         ACT.Exp).then_inc(mix_act.sem, 1)
                act.wait_ge(mix_pe.sem, mix_pe.at(b, 3))
                nc.scalar.activation(eq, S[:, 2].rearrange("p (m t) -> p m t", m=KT), ACT.Exp,
                                     scale=-1.0).then_inc(mix_act.sem, 1)

            def prepare(b):
                act.wait_ge(loaded[2], 16 * N_LOADS[2])
                nc.scalar.activation(bq4[:], bq4[:], ACT.Copy, scale=AD ** -0.5).then_inc(consts, 1)
                nc.scalar.activation(wr_hi[:], w_r[:], ACT.Copy).then_inc(wr_high, 1)

            def turn_norm(b):
                if not later(b):
                    act.wait_ge(consts, N_CONSTS)
                for k in range(KT):
                    act.wait_ge(xt_pe.sem, xt_pe.at(b, k + 1))
                    nc.scalar.activation(xn_t[:, k], S[:, k, 0:T], ACT.Copy).then_inc(xt_act.sem, 1)

            banks = [S[:, 2], S[:, 0], S[:, 1], O]

            def project_qk(b):
                for n in range(4):
                    act.wait_ge(proj_pe.sem, proj_pe.at(b, n + 1))
                    dst, bias, scale = (qf, bq4, AD ** -0.5) if n < 2 else (kf, bk1, 1.0)
                    nc.scalar.activation(dst[:, n % 2], banks[n][:, 0:T], ACT.Identity,
                                         bias=bias[:, n % 2:n % 2 + 1], scale=scale
                                         ).then_inc(proj_act.sem, 1)
                    if n % 2:
                        act.wait_ge(proj_act.sem, proj_act.at(b, (2, 5)[n // 2]))
                        nc.scalar.activation(parts[n // 2 * 3], (qf, kf)[n // 2], ACT.Copy
                                             ).then_inc(proj_act.sem, 1)

            def project_rel(b):
                for i in range(TT):
                    act.wait_ge(proj_pe.sem, proj_pe.at(b, 5 + i))
                    nc.scalar.activation(rel_log[:, i], banks[i][:, 0:RJ], ACT.Copy
                                         ).then_inc(proj_act.sem, 1)
                act.wait_ge(proj_act.sem, proj_act.at(b, 9))
                nc.scalar.activation(rel_log_b, rel_log, ACT.Copy).then_inc(proj_act.sem, 1)

            def weights(b):
                for n in range(4):
                    hi = (wg_hi, wu_hi)[n // 2]
                    act.wait_ge(gu_loaded[n], 16)
                    nc.scalar.activation(hi[:, expert_half(n)], w_d[:, expert_half(n)],
                                         ACT.Copy).then_inc(gu_high, 1)

            def negate(b, half, seen):
                act.wait_ge(neg_pe.sem, neg_pe.at(b, half + 1))
                if half:
                    act.wait_ge(neg_out.sem, neg_out.at(b, 1))
                elif later(b):
                    act.wait_ge(neg_out.sem, neg_out.at(b - 1, 2))
                nc.scalar.activation(neg_max[:, 0], S[0:AH // 2, 5, 0:T], ACT.Copy, scale=-1.0
                                     ).then_inc(neg_act.sem, 1)

            def attend(b, n, seen):
                act.wait_ge(sc_add.sem, sc_add.at(b, 4 * (n + 1)))
                (h, i), (h2, _) = tiles_of(n)
                if h >= PTS and n % 3 == 0:
                    act.wait_ge(pv_done.sem, pv_done.at(b, (h - PTS) // GRP + 1))
                    act.wait_ge(win_done.sem, win_done.at(b, WINS * ((h - PTS) // 2 + 1)))
                s0 = h % PTS
                dst = p_t[:, s0:s0 + 2, i, :] if h2 > h else p_t[:, s0, 0:2, :]
                c0 = 2 * (n % 3)
                nc.scalar.activation(dst, S[:, c0:c0 + 2, PAD:PAD + T], ACT.Exp).then_inc(exp_done.sem, 1)

            def copy(b, g):
                act.wait_ge(pv_done.sem, pv_done.at(b, g + 1))
                nc.scalar.activation(o_sb[:, g], S[:, 6 + g % 2, 0:T], ACT.Copy).then_inc(o_copied.sem, 1)

            def turn_weights(b):
                act.wait_ge(rw_pe.sem, rw_pe.at(b, 1))
                nc.scalar.activation(rwt0, O[:, 0:T], ACT.Copy).then_inc(rw_act.sem, 1)
                act.wait_ge(rw_pe.sem, rw_pe.at(b, 2))
                nc.scalar.activation(rwt1, S[0:RJ - P, 1, 0:T], ACT.Copy).then_inc(rw_act.sem, 1)

            def turn_attn(b):
                for k in range(KT):
                    act.wait_ge(at_pe.sem, at_pe.at(b, k + 1))
                    nc.scalar.activation(attn_t[:, k], S[:, k, 0:T], ACT.Copy).then_inc(at_act.sem, 1)

            def turn_x2(b):
                for k in range(KT):
                    act.wait_ge(x2_pe.sem, x2_pe.at(b, k + 1))
                    nc.scalar.activation(x2_hi[:, k], S[:, 6 + k, 0:T], ACT.Copy).then_inc(x2_hi_done.sem, 1)

            def router(b):
                act.wait_ge(r_pe.sem, r_pe.at(b, 1))
                act.wait_ge(stored.sem, stored.at(b - 1, 1))
                nc.scalar.activation(rt[0], S[:, 5, 0:TT * NE].rearrange("p (i e) -> p i e", i=TT),
                                     ACT.Exp, scale=neg_temp[:]).then_inc(r_act.sem, 1)
                act.wait_ge(r_dve.sem, r_dve.at(b, R_DIST))
                nc.scalar.activation(rt[4], rt[3], ACT.Exp, scale=-1.0 / 0.1).then_inc(r_act.sem, 1)
                nc.scalar.activation(rt[5], rt[3], ACT.Exp, scale=-1.0 / 0.3).then_inc(r_act.sem, 1)

            def gate(f, n):
                act.wait_ge(gate_pe.sem, gate_pe.at(f, n + 1))
                if n:
                    act.wait_ge(h_done.sem, h_done.at(f, n))
                nc.scalar.activation(silu[:], G[:, 0:T], ACT.Silu).then_inc(silu_done.sem, 1)

            rounds(act, {"mix_in": mix_in, "prepare": prepare, "turn_norm": turn_norm,
                         "project_qk": project_qk, "project_rel": project_rel, "weights": weights,
                         "negate": negate, "attend": attend, "copy": copy, "turn_weights": turn_weights,
                         "turn_attn": turn_attn, "turn_x2": turn_x2, "router": router, "gate": gate})

        @block.vector
        def _(dve):
            dve.memset(band_w[:], 0.0).then_inc(zero_ready, 1)
            dve.memset(x_in[F:F + 1], 1.0).then_inc(ones_ready, 1)
            dve.memset(spare[:, 2:3], 0.0).then_inc(stored.sem, 16)
            dve.memset(spare[:, 3:4], 0.0).then_inc(acc_done.sem, 1)
            dve.wait_ge(loaded[0], 16 * N_LOADS[0])
            dve.tensor_copy(zone(1024, IT, L), Z[:, 512:640].bitcast(U8).rearrange("p (i s) -> p i s", i=IT)
                            ).then_inc(mask_float, 1)
            dve.wait_ge(mask_float, 1)
            dve.tensor_tensor(zone(0, IT, L), zone(0, IT, L), zone(1024, IT, L), ALU.mult
                              ).then_inc(wb_masked, 1)
            for h in range(H):
                dve.tensor_copy(resid[0:F, h], ident[0:F, 0:F]).then_inc(resid_ready, 1)
            dve.memset(S[:, 3:8], 0.0).then_inc(psum_clear, 1)
            dve.wait_ge(psum_clear, 1)

            def stats(b, sg, k, src, tiles):
                for i in range(tiles):
                    dve.bn_stats(stat[:, i], src(i)).then_inc(sg.sem, 1)
                dve.wait_ge(sg.sem, sg.at(b, k + tiles))
                dve.memset(spare[:, 0:1], 0.0)
                for i in range(tiles):
                    dve.bn_aggr(mv[:, i], stat[:, i]).then_inc(sg.sem, 1)

            def norm(b, sg, rooted, src, dst, tiles):
                dve.wait_ge(rooted.sem, rooted.at(b, 2))
                for i in range(tiles):
                    dve.tensor_scalar(dst(i), src(i), mv[:, i, 0:1], rstd[:, i:i + 1], ALU.subtract,
                                      ALU.mult).then_inc(sg.sem, 1)

            def mix_in(b):
                for i in range(IT):
                    dve.wait_ge(mix_act.sem, mix_act.at(b, i + 1))
                    dve.tensor_tensor(ekv[:, i].rearrange("p (h d) -> p h d", h=H),
                                      ek[:, i].rearrange("p (h d) -> p h d", h=H),
                                      S[:, i].rearrange("p (h c) -> p h c", h=H)[:, :, F:2 * F],
                                      ALU.mult).then_inc(mix_dve.sem, 1)

            def mix_sums(b):
                dve.wait_ge(mix_act.sem, mix_act.at(b, 3))
                dve.wait_ge(mix_pe.sem, mix_pe.at(b, 4))
                dve.scalar_tensor_tensor(dd.rearrange("p m t -> p (m t)"), eq.rearrange("p m t -> p (m t)"),
                                         1.0, O[:, 0:KT * L], ALU.add, ALU.mult).then_inc(mix_dve.sem, 1)
                dve.wait_ge(mix_dve.sem, mix_dve.at(b, 3))
                dve.reciprocal(dd, dd).then_inc(mix_dve.sem, 1)
                dve.wait_ge(mix_pe.sem, mix_pe.at(b, 5))
                dve.wait_ge(mix_dve.sem, mix_dve.at(b, 4))
                dve.tensor_tensor(y_t.rearrange("p m t -> p (m t)"), S[:, 0, 0:KT * L],
                                  dd.rearrange("p m t -> p (m t)"), ALU.mult).then_inc(mix_dve.sem, 1)

            def mixed(i):
                return S[:, 1, i * E:(i + 1) * E]

            def mix_out(b):
                dve.wait_ge(mix_pe.sem, mix_pe.at(b, 7))
                stats(b, mix_dve, 5, mixed, IT)

            def mix_norm(b):
                norm(b, mix_dve, mix_root, mixed, lambda i: hid[:, i], IT)

            def prepare(b):
                dve.wait_ge(loaded[2], 16 * N_LOADS[2])
                for m in range(KT):
                    dve.tensor_tensor(rel_k[:, m], emb_k_rows.unsqueeze(2).broadcast_to([P, NJ, AH]),
                                      head_of_row[:, m].unsqueeze(1).broadcast_to([P, NJ, AH]), ALU.mult
                                      ).then_inc(consts, 1)
                for dst, rows, n in ((rel_v0, emb_v_rows0, P), (rel_v1, emb_v_rows1, RJ - P)):
                    dve.tensor_tensor(dst[:], rows[0:n].unsqueeze(1).broadcast_to([n, AH, AD]),
                                      head_of_rel[0:n].unsqueeze(2).broadcast_to([n, AH, AD]), ALU.mult
                                      ).then_inc(consts, 1)
                dve.reciprocal(neg_temp[:], neg_temp[:]).then_inc(temp_inverse, 1)
                dve.wait_ge(temp_inverse, 1)
                dve.tensor_scalar(neg_temp[:], neg_temp[:], -1.0, None, ALU.mult).then_inc(consts, 1)
                dve.wait_ge(wr_high, 1)
                dve.tensor_tensor(wr_lo[:], w_r[:], wr_hi[:].bitcast(F32), ALU.subtract
                                  ).then_inc(consts, 1)
                dve.tensor_copy(ident_b[:], ident[:]).then_inc(consts, 1)

            def norm_stats(b):
                dve.wait_ge(hid_ready.sem, hid_ready.at(b, 5))
                stats(b, ln2, 0, lambda i: hid[:, i], TT)

            def turn_norm(b):
                norm(b, ln2, ln2_root, lambda i: hid[:, i], lambda i: xn[:, i], TT)

            banks = [O, S[:, 2], S[:, 0]]

            def project_qk(b):
                for n, (src, p3) in enumerate(((qf, parts[0:3]), (kf, parts[3:6]))):
                    k = 3 * n
                    dve.wait_ge(proj_act.sem, proj_act.at(b, (3, 6)[n]))
                    if n:
                        dve.wait_ge(split.sem, split.at(b, k))
                    dve.tensor_tensor(rest, src, p3[0], ALU.subtract).then_inc(split.sem, 1)
                    dve.wait_ge(split.sem, split.at(b, k + 1))
                    dve.tensor_copy(p3[1], rest).then_inc(split.sem, 1)
                    dve.wait_ge(split.sem, split.at(b, k + 2))
                    dve.tensor_tensor(p3[2], rest, p3[1], ALU.subtract).then_inc(split.sem, 1)

            def project_v(b):
                for i in range(TT):
                    dve.wait_ge(proj_pe.sem, proj_pe.at(b, 8 + i))
                    dve.tensor_tensor(v_one[:, i, :, 0:AD],
                                      banks[i][:, 0:E].rearrange("p (h d) -> p h d", h=AH),
                                      bv_all[:].rearrange("p (h d) -> p h d", h=AH), ALU.add
                                      ).then_inc(v_done.sem, 1)

            def maxima(b, n):
                dve.wait_ge(max_pe.sem, max_pe.at(b, n + 1))
                (h, i), (h2, _) = tiles_of(n)
                dst = maxima_sb[:, i, h:h + 2] if h2 > h else maxima_sb[:, 0:2, h]
                c0 = 2 * (n % 2)
                dve.tensor_reduce(dst, S[:, c0:c0 + 2, PAD:PAD + T], AX, ALU.max).then_inc(max_done.sem, 1)

            def negate(b, half, seen):
                dve.wait_ge(neg_act.sem, neg_act.at(b, half + 1))
                dve.scalar_tensor_tensor(neg_max[:, 1], S[0:AH // 2, 5, 0:T], -1.0, neg_max[:, 0],
                                         ALU.mult, ALU.subtract).then_inc(neg_dve.sem, 1)

            def attend(b, n, seen):
                if n == 0:
                    dve.wait_ge(band_s_in.sem, band_s_in.at(b, 4))
                dve.wait_ge(sc_pe.sem, sc_pe.at(b, n + 1))
                (h, i), (h2, _) = tiles_of(n)
                for c in range(P // BL):
                    rows = slice(c * BL, (c + 1) * BL)
                    at = 2 * (n % 3) * 512 + PAD + i * P + c * BL - WIN
                    win = bass.AP(tensor=S, offset=S[rows].offset + at,
                                  ap=[[S[rows].ap[0][0], BL], [512 if h2 > h else 512 + P, 2], [1, WD_]])
                    band = (band_s[rows, i, :, h:h + 2].rearrange("p w h -> p h w") if h2 > h
                            else band_s[rows, 0:2, :, h])
                    dve.tensor_tensor(win, win, band, ALU.add).then_inc(sc_add.sem, 1)

            def turn_outputs(b):
                dve.wait_ge(win_done.sem, win_done.at(b, WINS * 6))
                for i in range(TT):
                    dve.wait_ge(ot_pe.sem, ot_pe.at(b, i + 1))
                    heads = S[:, i].rearrange("p (h d) -> p h d", h=AH)
                    dve.reciprocal(rden[:, i], heads[:, :, AD]).then_inc(att_dve.sem, 1)
                    dve.wait_ge(att_dve.sem, att_dve.at(b, 2 * i + 1))
                    dve.tensor_tensor(attn[:, i].rearrange("p (h d) -> p h d", h=AH), heads[:, :, 0:AD],
                                      rden[:, i].unsqueeze(2).broadcast_to([P, AH, AD]), ALU.mult
                                      ).then_inc(att_dve.sem, 1)

            def turn_weights(b):
                dve.wait_ge(relw_in.sem, relw_in.at(b, TT))
                by_j = rel_w.rearrange("p i (j h) -> p i j h", j=NJ)
                dve.tensor_tensor(by_j, by_j, rden.unsqueeze(2).broadcast_to([P, TT, NJ, AH]), ALU.mult
                                  ).then_inc(att_dve.sem, 1)

            def rel_values(b):
                for n, (i, rel) in enumerate(REL_TILES):
                    dve.wait_ge(or_pe.sem, or_pe.at(b, n + 1))
                    dve.tensor_tensor(attn[:, i], attn[:, i], rel, ALU.add).then_inc(att_dve.sem, 1)

            def residual(b):
                dve.wait_ge(hid_bo.sem, hid_bo.at(b, 1))
                for i in range(TT):
                    dve.wait_ge(wo_pe.sem, wo_pe.at(b, max(i + 1, 2)))
                    src = D[:, i // 2, (i % 2) * E:(i % 2 + 1) * E]
                    dve.tensor_tensor(res[:, i], src, hid[:, i], ALU.add).then_inc(res_ready.sem, 1)
                dve.wait_ge(res_ready.sem, res_ready.at(b, TT))
                stats(b, ln3, 0, lambda i: res[:, i], TT)

            def turn_x2(b):
                norm(b, ln3, ln3_root, lambda i: res[:, i], lambda i: xn2[:, i], TT)
                for k in range(KT):
                    dve.wait_ge(x2_hi_done.sem, x2_hi_done.at(b, k + 1))
                    dve.tensor_tensor(x2_lo[:, k], S[:, 6 + k, 0:T], x2_hi[:, k].bitcast(F32), ALU.subtract
                                      ).then_inc(x2_lo_done.sem, 1)

            def stepper(b, k):
                def step(ins):
                    k[0] += 1
                    ins.then_inc(r_dve.sem, 1)
                    dve.wait_ge(r_dve.sem, r_dve.at(b, k[0]))

                return step

            ex, inh, zone_, dist, w, fb, rank, fbw = rt[0:8]

            def router(b):
                k = [0]
                step = stepper(b, k)
                dve.wait_ge(r_act.sem, r_act.at(b, 1))
                step(dve.tensor_scalar(inh, ex, 1.0, None, ALU.add))
                step(dve.reciprocal(inh, inh))
                step(dve.tensor_scalar(dist, inh, CENTER, None, ALU.subtract))
                step(dve.scalar_tensor_tensor(dist, dist, -1.0, dist, ALU.mult, ALU.max))
                assert k[0] == R_DIST
                step(dve.tensor_scalar(zone_, inh, ZONE_HI, None, ALU.is_le))
                step(dve.scalar_tensor_tensor(zone_, inh, ZONE_LO, zone_, ALU.is_ge, ALU.mult))

            def each(x):
                return x.unsqueeze(2).broadcast_to([P, TT, NE])

            def router_zone(b):
                step = stepper(b, [R_DIST + 2])
                dve.wait_ge(r_act.sem, r_act.at(b, 3))
                step(dve.tensor_tensor(w, w, zone_, ALU.mult))
                step(dve.tensor_reduce(rsum, w, AX, ALU.add))
                step(dve.tensor_scalar(rsum, rsum, 1e-8, None, ALU.is_lt))

            def router_rank(b):
                step = stepper(b, [R_DIST + 5])
                other = fb.unsqueeze(2).broadcast_to([P, TT, NE, NE])
                own = fb.unsqueeze(3).broadcast_to([P, TT, NE, NE])
                low = earlier[:].unsqueeze(1).broadcast_to([P, TT, NE, NE])
                step(dve.tensor_tensor(rpair, other, own, ALU.is_equal))
                step(dve.tensor_tensor(rpair, rpair, low, ALU.mult))
                step(dve.tensor_tensor(rpair2, other, own, ALU.is_gt))
                step(dve.tensor_tensor(rpair, rpair, rpair2, ALU.add))
                step(dve.tensor_reduce(rank, rpair, AX, ALU.add))

            def router_pick(b):
                k = [R_DIST + 10]
                step = stepper(b, k)
                step(dve.scalar_tensor_tensor(fbw, rank, 2.0, fb, ALU.is_lt, ALU.mult))
                step(dve.tensor_reduce(rt[8][:, :, 0], fbw, AX, ALU.add))
                step(dve.tensor_scalar(rt[8][:, :, 0], rt[8][:, :, 0], 1e-8, None, ALU.max))
                step(dve.reciprocal(rt[8][:, :, 0], rt[8][:, :, 0]))
                step(dve.tensor_tensor(fbw, fbw, each(rt[8][:, :, 0]), ALU.mult))
                dve.memset(spare[:, 0:1], 0.0)
                step(dve.copy_predicated(w, each(rsum.bitcast(I32)), fbw))
                step(dve.tensor_reduce(rt[8][:, :, 1], w, AX, ALU.add))
                step(dve.tensor_scalar(rt[8][:, :, 1], rt[8][:, :, 1], 1e-8, None, ALU.max))
                step(dve.reciprocal(rt[8][:, :, 1], rt[8][:, :, 1]))
                step(dve.tensor_tensor(wgt[:], w, each(rt[8][:, :, 1]), ALU.mult))
                assert k[0] == R_STEPS

            def hidden(f, n):
                dve.wait_ge(silu_done.sem, silu_done.at(f, n + 1))
                dve.wait_ge(up_pe.sem, up_pe.at(f, n + 1))
                if n >= 3:
                    dve.wait_ge(down_pe.sem, down_pe.at(f, 2 * ((n - 3) // FT + 1)))
                dve.tensor_tensor(hT[:, n % 3], silu[:], U[:, 0:T], ALU.mult).then_inc(h_done.sem, 1)

            def accumulate(f, e, part):
                dve.wait_ge(down_pe.sem, down_pe.at(f, 2 * e + part + 1))
                if e and part == 0:
                    dve.wait_ge(acc_done.sem, acc_done.at(f, TT * e))
                last = e == NE - 1
                if last and part == 0 and not isinstance(f, int):
                    dve.wait_ge(win_done.sem, win_done.at(f + 1, WINS * 6))
                    dve.wait_ge(pv_done.sem, pv_done.at(f + 1, AH // GRP))
                for i in ((0, 1), (2,))[part]:
                    dve.scalar_tensor_tensor((out_st if last else res)[:, i], D[:, i // 2, (i % 2) * E:(i % 2 + 1) * E],
                                             wgt[:, i, e:e + 1], res[:, i], ALU.mult, ALU.add
                                             ).then_inc(acc_done.sem, 1)

            rounds(dve, {"mix_in": mix_in, "mix_sums": mix_sums, "mix_out": mix_out, "mix_norm": mix_norm,
                         "prepare": prepare, "norm_stats": norm_stats, "turn_norm": turn_norm,
                         "project_qk": project_qk, "project_v": project_v, "maxima": maxima,
                         "negate": negate, "attend": attend, "turn_outputs": turn_outputs,
                         "turn_weights": turn_weights, "rel_values": rel_values, "residual": residual,
                         "turn_x2": turn_x2, "router": router, "router_zone": router_zone,
                         "router_rank": router_rank, "router_pick": router_pick,
                         "hidden": hidden, "accumulate": accumulate})

        @block.gpsimd
        def _(pool):
            for n, (dst, value) in enumerate(((one, 1.0), (eps, EPS), (neg_half, -0.5),
                                              (root_e, float(E) ** 0.5))):
                nc.gpsimd.memset(dst[:], value).then_inc(pool_consts, 1)
            nc.gpsimd.memset(v_one[:], 1.0).then_inc(pool_consts, 1)
            pool.wait_ge(pool_consts, 5)
            nc.gpsimd.memset(k_st[KST:KST + 2], 1.0).then_inc(pool_consts, 1)
            pool.wait_ge(pool_consts, 6)

            def root(b, stats, steps, done, tiles):
                pool.wait_ge(stats.sem, stats.at(b, steps))
                nc.gpsimd.tensor_tensor(rstd[:, 0:tiles], mv[:, 0:tiles, 1], eps[:].broadcast_to([P, tiles]),
                                        ALU.add).then_inc(done.sem, 1)
                pool.wait_ge(done.sem, done.at(b, 1))
                nc.gpsimd.tensor_tensor(rstd[:, 0:tiles], rstd[:, 0:tiles],
                                        neg_half[:].broadcast_to([P, tiles]), ALU.pow
                                        ).then_inc(done.sem, 1)

            def mix_in(b):
                pool.wait_ge(idx_loaded.sem, idx_loaded.at(b, 1))
                if later(b):
                    pool.wait_ge(hid_ready.sem, hid_ready.at(b - 1, 5))
                nc.gpsimd.tensor_tensor(spare[:, 1:2], one[:], one[:], ALU.mult)
                pool.indirect_dma_start(txt_row[:], None, a["L0_txt_W_E"],
                                        bass.IndirectOffsetOnAxis(ap=txt_idx[:, 0:1], axis=0)
                                        ).then_inc(txt_loaded.sem, 16)

            def mix_sums(b):
                pool.wait_ge(txt_loaded.sem, txt_loaded.at(b, 1))
                if later(b):
                    pool.wait_ge(res_ready.sem, res_ready.at(b - 1, TT))
                nc.gpsimd.tensor_tensor(hid[:, IT], txt_row[:], root_e[:].broadcast_to([P, E]), ALU.mult
                                        ).then_inc(hid_ready.sem, 1)

            def mix_out(b):
                root(b, mix_dve, 5 + 2 * IT, mix_root, IT)

            def mix_norm(b):
                if not later(b):
                    pool.wait_ge(loaded[1], 16 * N_LOADS[1])
                for i in range(IT):
                    pool.wait_ge(mix_dve.sem, mix_dve.at(b, 5 + 2 * IT + 1 + i))
                    nc.gpsimd.tensor_tensor(hid[:, i], hid[:, i], ln_g[:], ALU.mult).then_inc(hid_ready.sem, 1)
                    pool.wait_ge(hid_ready.sem, hid_ready.at(b, 2 + 2 * i))
                    nc.gpsimd.tensor_tensor(hid[:, i], hid[:, i], ln_b[:], ALU.add).then_inc(hid_ready.sem, 1)

            def norm_stats(b):
                root(b, ln2, 2 * TT, ln2_root, TT)

            def project_rel(b):
                if not later(b):
                    pool.wait_ge(loaded[2], 16 * N_LOADS[2])
                pool.wait_ge(ln2.sem, ln2.at(b, 3 * TT))
                nc.gpsimd.tensor_tensor(hid[:], hid[:], bo_all[:].unsqueeze(1).broadcast_to([P, TT, E]),
                                        ALU.add).then_inc(hid_bo.sem, 1)

            def weights(b):
                for n in range(4):
                    hi, lo = ((wg_hi, wg_lo), (wu_hi, wu_lo))[n // 2]
                    half = expert_half(n)
                    pool.wait_ge(gu_high, n + 1)
                    nc.gpsimd.tensor_tensor(lo[:, half], w_d[:, half],
                                            hi[:, half].bitcast(F32), ALU.subtract).then_inc(gu_low, 1)
                pool.wait_ge(gu_low, 4)

            def attend(b, n, seen):
                if n % 3 < 2:
                    return
                pair = n // 3
                if n == 2:
                    if later(b):
                        pool.wait_ge(win_out.sem, win_out.at(b - 1, 4))
                    else:
                        pool.wait_ge(zeroed, 16 * N_ZERO)
                pool.wait_ge(exp_done.sem, exp_done.at(b, n + 1))
                if n == 2 and not later(b):
                    for m, at in enumerate((0, PAD + T)):
                        pads = bass.AP(tensor=Z, offset=at, ap=[[ZF, P], [TP, PTS * TT], [1, PAD]])
                        nc.gpsimd.memset(pads, 0.0).then_inc(pool_consts, 1)
                    pool.wait_ge(pool_consts, 8)
                for c in range(P // BL):
                    rows = slice(c * BL, (c + 1) * BL)
                    if c or pair:
                        pool.wait_ge(win_done.sem, win_done.at(b, WINS * pair + c))
                    else:
                        pool.wait_ge(hid_bo.sem, hid_bo.at(b, 1))
                    slot = 2 * pair % PTS
                    win = bass.AP(tensor=Z, offset=Z[rows].offset + slot * TT * TP + PAD + c * BL - WIN,
                                  ap=[[Z[rows].ap[0][0], BL], [TT * TP, 2], [TP + P, TT], [1, WD_]])
                    nc.gpsimd.tensor_tensor(
                        band_w[rows, :, :, 2 * pair:2 * pair + 2].rearrange("p i w h -> p h i w"), win,
                        one[rows].unsqueeze(2).unsqueeze(3).broadcast_to([BL, 2, TT, WD_]), ALU.mult
                    ).then_inc(win_done.sem, 1)

            def residual(b):
                root(b, ln3, 2 * TT, ln3_root, TT)

            rounds(pool, {"mix_in": mix_in, "mix_sums": mix_sums, "mix_out": mix_out,
                          "mix_norm": mix_norm, "norm_stats": norm_stats, "project_rel": project_rel,
                          "weights": weights, "attend": attend, "residual": residual})


_NAMES = ["x", "L0_tok_w_bias", "L0_tok_Wk_b", "L0_tok_Wv_b", "L0_tok_Wq_b", "L0_tok_out_w", "L0_tok_out_b",
          "L0_tok_ln_g", "L0_tok_ln_b", "L0_txt_W_E", "L0_attn_Wq", "L0_attn_bq", "L0_attn_Wk", "L0_attn_bk",
          "L0_attn_Wv", "L0_attn_bv", "L0_attn_Wo", "L0_attn_bo", "L0_attn_emb_rel_k", "L0_attn_emb_rel_v",
          "L0_ffn_Wg", "L0_ffn_Wu", "L0_ffn_Wd", "L0_ffn_Wr", "L0_ffn_temperature"]


def kernel(**inputs):
    import concourse.bacc as bacc
    from concourse.bass_utils import run_bass_kernel_spmd

    data = {n: np.ascontiguousarray(inputs[n]) for n in _NAMES}
    data["tok_wk_t"] = np.ascontiguousarray(np.asarray(inputs["L0_tok_Wk_w"]).T)
    data["tok_wv_t"] = np.ascontiguousarray(np.asarray(inputs["L0_tok_Wv_w"]).T)
    data["tok_wq_t"] = np.ascontiguousarray(np.asarray(inputs["L0_tok_Wq_w"]).T)
    data["txt_t"] = np.ascontiguousarray(inputs["x_txt"]).reshape(NB, TXT, 1)
    data["mask"] = np.ascontiguousarray(inputs["L0_tok_local_mask"])
    row = np.arange(P)
    data["ident"] = np.eye(P, dtype=np.float32)
    data["head_of_row"] = (row[:, None, None] // AD + (P // AD) * np.arange(KT)[None, :, None]
                           == np.arange(AH)[None, None, :]).astype(np.float32)
    data["head_of_rel"] = (row[:, None] % AH == np.arange(AH)[None, :]).astype(np.float32)
    data["earlier"] = np.broadcast_to((np.arange(NE)[None, :] < np.arange(NE)[:, None]).astype(np.float32),
                                      (P, NE, NE)).copy()

    nc = bacc.Bacc("TRN2", target_bir_lowering=False, num_devices=1)
    arrays, aps = {}, {}
    for name, array in data.items():
        arrays[f"in_{name}"] = array
        aps[name] = nc.dram_tensor(f"in_{name}", array.shape, mybir.dt.from_np(array.dtype),
                                   kind="ExternalInput").ap()
    out = nc.dram_tensor("out_0", (NB, T, E), F32, kind="ExternalOutput").ap()
    fusion_block(nc, aps, out)
    return run_bass_kernel_spmd(nc, [arrays], core_ids=[0]).results[0]["out_0"]
```
